# Optimizing a Trainium2 kernel written in Bass

```python
import numpy as np
import jax
import jax.numpy as jnp

def _softmax(x, axis=-1):
    return jax.nn.softmax(x, axis=axis)

def _gelu(x):
    return jax.nn.gelu(x, approximate=True)

def _silu(x):
    return jax.nn.silu(x)

def _sigmoid(x):
    return jax.nn.sigmoid(x)

def _layernorm(x, axis=-1, eps=1e-05):
    m = jnp.mean(x, axis=axis, keepdims=True)
    v = jnp.var(x, axis=axis, keepdims=True)
    return (x - m) / jnp.sqrt(v + eps)

def _scatter_add(tgt, idx, src, axis=0):
    return tgt.at[idx].add(src)

def _segment_sum(src, seg, n):
    return jax.ops.segment_sum(src, seg, n)
kernel_name = 'mk_xattn_ffn_d2_seqx_r4_19a775'

def setup_inputs(seed: int=0):
    np.random.seed(seed)
    _w = jnp.asarray

    def _rec_inputs():
        import jax
        import jax.numpy as jnp
        _rk = jax.random.key(seed)
        x = -0.0002928 + 1 * jax.random.normal(jax.random.fold_in(_rk, 1), (32, 256, 256), jnp.float32)
        _lenS = 256 - jax.random.randint(jax.random.fold_in(_rk, 7), (32,), 0, max(1, 256 // 4) + 1, jnp.int32)
        _lenS2 = 77 - jax.random.randint(jax.random.fold_in(_rk, 8), (32,), 0, max(1, 77 // 4) + 1, jnp.int32)
        _ctx_1024P = jax.random.normal(jax.random.fold_in(_rk, 11), (32, 16, 256), jnp.float32)
        _ctx_1024c = jax.random.dirichlet(jax.random.fold_in(_rk, 511), 0.3 * jnp.ones((16,), jnp.float32), (32, 77))
        _ctx_1024t = jnp.einsum('bsk,bkd->bsd', _ctx_1024c, _ctx_1024P)
        _ctx_1024t = _ctx_1024t * jax.lax.rsqrt(jnp.mean(jnp.square(_ctx_1024t)) + 1e-12) * 0.953939
        ctx_1024 = -1.39393e-06 + 0.999914 * (_ctx_1024t + 0.3 * jax.random.normal(jax.random.fold_in(_rk, 611), (32, 77, 256), jnp.float32))
        _validS = jnp.arange(256)[None, :] < _lenS[:, None]
        _validS2 = jnp.arange(77)[None, :] < _lenS2[:, None]
        _causal = jnp.tril(jnp.ones((256, 256), dtype=bool))
        mask_1x1xSxS2_ik0 = jnp.where(jnp.broadcast_to(_validS2[0:1, None, None, :], (1, 1, 256, 77)), 0, 1).astype(jnp.int32)
        mask_SxS_bc0 = jnp.logical_not(jnp.broadcast_to(_causal[:, :], (256, 256)))
        return (x, ctx_1024, mask_1x1xSxS2_ik0, mask_SxS_bc0)
    x, ctx_1024, mask_1x1xSxS2_ik0, mask_SxS_bc0 = _rec_inputs()

    def _L0_xattn_setup():
        import jax, jax.numpy as jnp
        import numpy as np
        B, S, D, H = (2, 512, 256, 16)
        HD = D // H

        def _split_heads(x):
            b, s, _ = x.shape
            return x.reshape(b, s, H, HD).transpose(0, 2, 1, 3)
        key = jax.random.key(seed)
        ks = jax.random.split(key, 12)
        s = 1.0 / np.sqrt(D)
        inp = {'Q': jax.random.normal(ks[0], (B, S, D), jnp.float32), 'K': jax.random.normal(ks[1], (B, S, D), jnp.float32), 'V': jax.random.normal(ks[2], (B, S, D), jnp.float32), 'mask': jnp.tril(jnp.ones((S, S), jnp.int32))[None, None], 'Wq': jax.random.normal(ks[3], (D, D), jnp.float32) * s, 'bq': jnp.zeros((D,), jnp.float32), 'Wk': jax.random.normal(ks[4], (D, D), jnp.float32) * s, 'bk': jnp.zeros((D,), jnp.float32), 'Wv': jax.random.normal(ks[5], (D, D), jnp.float32) * s, 'bv': jnp.zeros((D,), jnp.float32), 'Wo': jax.random.normal(ks[6], (D, D), jnp.float32) * s, 'bo': jnp.zeros((D,), jnp.float32)}
        return inp
    _L0_xattn_all = _L0_xattn_setup()
    _L0_xattn_in = {k: v for k, v in _L0_xattn_all.items() if k in ('Wq', 'bq', 'Wk', 'bk', 'Wv', 'bv', 'Wo', 'bo')}
    del _L0_xattn_all

    def _L0_ffn_setup():
        import jax, jax.numpy as jnp
        import numpy as np
        DIM = 256
        DEPTH = 2
        HEADS = 8
        DIM_HEAD = 64
        WINDOW = 128
        INNER = HEADS * DIM_HEAD
        HID = int(DIM * 4 * 2 / 3)
        B, N = (2, 2048)
        QK_SCALE = 8.0

        def shift_token(t):
            t1, t2 = jnp.split(t, 2, axis=-1)
            t2 = jnp.pad(t2, ((0, 0), (1, 0), (0, 0)))[:, :-1]
            return jnp.concatenate([t1, t2], axis=-1)

        def l2norm(t):
            return t / jnp.clip(jnp.linalg.norm(t, axis=-1, keepdims=True), 1e-12)

        def rotate_half(x):
            x1, x2 = jnp.split(x, 2, axis=-1)
            return jnp.concatenate([-x2, x1], axis=-1)

        def rotary_xpos(q, k):
            n = q.shape[-2]
            half_idx = jnp.arange(0, DIM_HEAD, 2, dtype=jnp.float32)
            inv_freq = 1.0 / 10000.0 ** (half_idx / DIM_HEAD)
            t = jnp.arange(n, dtype=jnp.float32)
            freqs = t[:, None] * inv_freq[None, :]
            freqs = jnp.concatenate([freqs, freqs], axis=-1)
            base = (half_idx + 0.4 * DIM_HEAD) / (1.4 * DIM_HEAD)
            power = (t - n // 2) / float(WINDOW // 2)
            scale = base[None, :] ** power[:, None]
            scale = jnp.concatenate([scale, scale], axis=-1)
            cos, sin = (jnp.cos(freqs), jnp.sin(freqs))
            q = q * cos * scale + rotate_half(q) * sin * scale
            k = k * cos / scale + rotate_half(k) * sin / scale
            return (q, k)

        def local_attention(q, k, v):
            b, h, n, d = q.shape
            w = n // WINDOW
            bq = q.reshape(b, h, w, WINDOW, d) * QK_SCALE
            bk = k.reshape(b, h, w, WINDOW, d)
            bv = v.reshape(b, h, w, WINDOW, d)

            def look_around(t):
                p = jnp.pad(t, ((0, 0), (0, 0), (1, 0), (0, 0), (0, 0)))
                return jnp.concatenate([p[:, :, :w], p[:, :, 1:]], axis=3)
            bk, bv = (look_around(bk), look_around(bv))
            bt = jnp.arange(n).reshape(w, WINDOW)
            btp = jnp.pad(bt, ((1, 0), (0, 0)), constant_values=-1)
            btk = jnp.concatenate([btp[:w], btp[1:]], axis=1)
            sim = jnp.einsum('bhwid,bhwjd->bhwij', bq, bk)
            i = bt[:, :, None]
            j = btk[:, None, :]
            mask = (i < j) | (i > j + WINDOW) | (j == -1)
            sim = jnp.where(mask, -jnp.finfo(sim.dtype).max, sim)
            attn = jax.nn.softmax(sim, axis=-1)
            out = jnp.einsum('bhwij,bhwjd->bhwid', attn, bv)
            return out.reshape(b, h, n, d)

        def _layer(x, wqkv, qs, ksc, wo, lg, lb, w1, b1, w2, b2):
            b, n, _ = x.shape
            h = shift_token(x)
            qkv = h @ wqkv
            q, k, v = jnp.split(qkv, 3, axis=-1)
            to_heads = lambda t: t.reshape(b, n, HEADS, DIM_HEAD).transpose(0, 2, 1, 3)
            q, k, v = (to_heads(q), to_heads(k), to_heads(v))
            q = l2norm(q) * qs
            k = l2norm(k) * ksc
            q, k = rotary_xpos(q, k)
            o = local_attention(q, k, v)
            o = o.transpose(0, 2, 1, 3).reshape(b, n, INNER)
            x = x + o @ wo
            h = shift_token(x)
            mu = h.mean(-1, keepdims=True)
            var = h.var(-1, keepdims=True)
            h = (h - mu) / jnp.sqrt(var + 1e-05) * lg + lb
            h = h @ w1 + b1
            a, g = jnp.split(h, 2, axis=-1)
            h = a * jax.nn.gelu(g, approximate=False)
            x = x + h @ w2 + b2
            return x
        key = jax.random.key(seed)
        ks = jax.random.split(key, 6)
        return {'x': jax.random.normal(ks[0], (B, N, DIM), jnp.float32), 'wqkv': jax.random.normal(ks[1], (DEPTH, DIM, 3 * INNER), jnp.float32) * 0.02, 'q_scale': jnp.ones((DEPTH, DIM_HEAD), jnp.float32), 'k_scale': jnp.ones((DEPTH, DIM_HEAD), jnp.float32), 'wo': jax.random.normal(ks[2], (DEPTH, INNER, DIM), jnp.float32) * 0.02, 'ln_g': jnp.ones((DEPTH, DIM), jnp.float32), 'ln_b': jnp.zeros((DEPTH, DIM), jnp.float32), 'w1': jax.random.normal(ks[3], (DEPTH, DIM, 2 * HID), jnp.float32) * 0.02, 'b1': jnp.zeros((DEPTH, 2 * HID), jnp.float32), 'w2': jax.random.normal(ks[4], (DEPTH, HID, DIM), jnp.float32) * 0.02, 'b2': jnp.zeros((DEPTH, DIM), jnp.float32)}
    _L0_ffn_all = _L0_ffn_setup()
    _L0_ffn_in = {k: v for k, v in _L0_ffn_all.items() if k in ('wqkv', 'q_scale', 'k_scale', 'wo', 'ln_g', 'ln_b', 'w1', 'b1', 'w2', 'b2')}
    del _L0_ffn_all

    def _L1_xattn_setup():
        import jax, jax.numpy as jnp
        import numpy as np
        from jax import lax
        H = 16
        K1, K2 = (3, 3)
        LN_EPS = 1e-05

        def _ln(x, g, b):
            m = jnp.mean(x, axis=-1, keepdims=True)
            v = jnp.mean(jnp.square(x - m), axis=-1, keepdims=True)
            return (x - m) * lax.rsqrt(v + LN_EPS) * g + b

        def _gelu(x):
            return jax.nn.gelu(x, approximate=False)
        key = jax.random.key(seed)
        B, T, D, Th = (4, 256, 256, 64)
        C = 2 * D
        ks = jax.random.split(key, 16)

        def w(k, shape):
            fan_in = shape[0]
            return (jax.random.normal(k, shape, jnp.float32) / np.sqrt(fan_in)).astype(jnp.float32)
        inp = {'x': jax.random.normal(ks[0], (B, T, D), jnp.float32), 'historical_data': jax.random.normal(ks[1], (B, Th, D), jnp.float32), 'Wq': w(ks[2], (D, D)), 'Wk': w(ks[3], (D, D)), 'Wv': w(ks[4], (D, D)), 'hist_W': w(ks[5], (D, C)), 'hist_b': jnp.zeros((C,), jnp.float32), 'hist_ln_g': jnp.ones((C,), jnp.float32), 'hist_ln_b': jnp.zeros((C,), jnp.float32), 'ctx_W1': w(ks[6], (C, C // 4)), 'ctx_b1': jnp.zeros((C // 4,), jnp.float32), 'ctx_W2': w(ks[7], (C // 4, 1)), 'ctx_b2': jnp.zeros((1,), jnp.float32), 'kg_W1': w(ks[8], (C, D)), 'kg_b1': jnp.zeros((D,), jnp.float32), 'kg_ln_g': jnp.ones((D,), jnp.float32), 'kg_ln_b': jnp.zeros((D,), jnp.float32), 'kg_W2': w(ks[9], (D, H * K1 * K2)), 'kg_b2': jnp.zeros((H * K1 * K2,), jnp.float32), 'proj_W': w(ks[10], (D, D)), 'proj_b': jnp.zeros((D,), jnp.float32), 'causal_mask': jnp.triu(jnp.ones((T, T), bool), k=1)}
        return inp
    _L1_xattn_all = _L1_xattn_setup()
    _L1_xattn_in = {k: v for k, v in _L1_xattn_all.items() if k in ('Wq', 'Wk', 'Wv', 'hist_W', 'hist_b', 'hist_ln_g', 'hist_ln_b', 'ctx_W1', 'ctx_b1', 'ctx_W2', 'ctx_b2', 'kg_W1', 'kg_b1', 'kg_ln_g', 'kg_ln_b', 'kg_W2', 'kg_b2', 'proj_W', 'proj_b')}
    del _L1_xattn_all

    def _L1_ffn_setup():
        import jax, jax.numpy as jnp
        import numpy as np
        DIM = 256

        def _reference_tuple_inner(x, W_r, W_k, W_v, mu_r, mu_k):
            B, T, C = x.shape
            x_prev = jnp.concatenate([jnp.zeros((B, 1, C), x.dtype), x[:, :-1, :]], axis=1)
            xr = mu_r * x + (1.0 - mu_r) * x_prev
            xk = mu_k * x + (1.0 - mu_k) * x_prev
            r = jax.nn.sigmoid(jnp.einsum('btc,dc->btd', xr, W_r))
            k = jnp.einsum('btc,dc->btd', xk, W_k)
            k_act = jnp.square(jax.nn.relu(k))
            out = r * jnp.einsum('btc,dc->btd', k_act, W_v)
            new_state = x[:, -1, :]
            return (out, new_state)
        key = jax.random.key(seed)
        ks = jax.random.split(key, 6)
        B, T, C = (8, 512, DIM)
        x = jax.random.normal(ks[0], (B, T, C), dtype=jnp.float32)
        s = 1.0 / np.sqrt(C)
        W_r = jax.random.uniform(ks[1], (C, C), jnp.float32, -s, s)
        W_k = jax.random.uniform(ks[2], (C, C), jnp.float32, -s, s)
        W_v = jax.random.uniform(ks[3], (C, C), jnp.float32, -s, s)
        mu_r = jax.random.uniform(ks[4], (C,), jnp.float32)
        mu_k = jax.random.uniform(ks[5], (C,), jnp.float32)
        return {'x': x, 'W_r': W_r, 'W_k': W_k, 'W_v': W_v, 'mu_r': mu_r, 'mu_k': mu_k}
    _L1_ffn_all = _L1_ffn_setup()
    _L1_ffn_in = {k: v for k, v in _L1_ffn_all.items() if k in ('W_r', 'W_k', 'W_v', 'mu_r', 'mu_k')}
    del _L1_ffn_all
    return {'x': x, 'ctx_1024': ctx_1024, 'mask_1x1xSxS2_ik0': mask_1x1xSxS2_ik0, 'mask_SxS_bc0': mask_SxS_bc0, 'L0_xattn_Wq': _L0_xattn_in['Wq'], 'L0_xattn_bq': _L0_xattn_in['bq'], 'L0_xattn_Wk': _L0_xattn_in['Wk'], 'L0_xattn_bk': _L0_xattn_in['bk'], 'L0_xattn_Wv': _L0_xattn_in['Wv'], 'L0_xattn_bv': _L0_xattn_in['bv'], 'L0_xattn_Wo': _L0_xattn_in['Wo'], 'L0_xattn_bo': _L0_xattn_in['bo'], 'L0_ffn_wqkv': _L0_ffn_in['wqkv'], 'L0_ffn_q_scale': _L0_ffn_in['q_scale'], 'L0_ffn_k_scale': _L0_ffn_in['k_scale'], 'L0_ffn_wo': _L0_ffn_in['wo'], 'L0_ffn_ln_g': _L0_ffn_in['ln_g'], 'L0_ffn_ln_b': _L0_ffn_in['ln_b'], 'L0_ffn_w1': _L0_ffn_in['w1'], 'L0_ffn_b1': _L0_ffn_in['b1'], 'L0_ffn_w2': _L0_ffn_in['w2'], 'L0_ffn_b2': _L0_ffn_in['b2'], 'L1_xattn_Wq': _L1_xattn_in['Wq'], 'L1_xattn_Wk': _L1_xattn_in['Wk'], 'L1_xattn_Wv': _L1_xattn_in['Wv'], 'L1_xattn_hist_W': _L1_xattn_in['hist_W'], 'L1_xattn_hist_b': _L1_xattn_in['hist_b'], 'L1_xattn_hist_ln_g': _L1_xattn_in['hist_ln_g'], 'L1_xattn_hist_ln_b': _L1_xattn_in['hist_ln_b'], 'L1_xattn_ctx_W1': _L1_xattn_in['ctx_W1'], 'L1_xattn_ctx_b1': _L1_xattn_in['ctx_b1'], 'L1_xattn_ctx_W2': _L1_xattn_in['ctx_W2'], 'L1_xattn_ctx_b2': _L1_xattn_in['ctx_b2'], 'L1_xattn_kg_W1': _L1_xattn_in['kg_W1'], 'L1_xattn_kg_b1': _L1_xattn_in['kg_b1'], 'L1_xattn_kg_ln_g': _L1_xattn_in['kg_ln_g'], 'L1_xattn_kg_ln_b': _L1_xattn_in['kg_ln_b'], 'L1_xattn_kg_W2': _L1_xattn_in['kg_W2'], 'L1_xattn_kg_b2': _L1_xattn_in['kg_b2'], 'L1_xattn_proj_W': _L1_xattn_in['proj_W'], 'L1_xattn_proj_b': _L1_xattn_in['proj_b'], 'L1_ffn_W_r': _L1_ffn_in['W_r'], 'L1_ffn_W_k': _L1_ffn_in['W_k'], 'L1_ffn_W_v': _L1_ffn_in['W_v'], 'L1_ffn_mu_r': _L1_ffn_in['mu_r'], 'L1_ffn_mu_k': _L1_ffn_in['mu_k']}

def reference(x, ctx_1024, mask_1x1xSxS2_ik0, mask_SxS_bc0, L0_xattn_Wq, L0_xattn_bq, L0_xattn_Wk, L0_xattn_bk, L0_xattn_Wv, L0_xattn_bv, L0_xattn_Wo, L0_xattn_bo, L0_ffn_wqkv, L0_ffn_q_scale, L0_ffn_k_scale, L0_ffn_wo, L0_ffn_ln_g, L0_ffn_ln_b, L0_ffn_w1, L0_ffn_b1, L0_ffn_w2, L0_ffn_b2, L1_xattn_Wq, L1_xattn_Wk, L1_xattn_Wv, L1_xattn_hist_W, L1_xattn_hist_b, L1_xattn_hist_ln_g, L1_xattn_hist_ln_b, L1_xattn_ctx_W1, L1_xattn_ctx_b1, L1_xattn_ctx_W2, L1_xattn_ctx_b2, L1_xattn_kg_W1, L1_xattn_kg_b1, L1_xattn_kg_ln_g, L1_xattn_kg_ln_b, L1_xattn_kg_W2, L1_xattn_kg_b2, L1_xattn_proj_W, L1_xattn_proj_b, L1_ffn_W_r, L1_ffn_W_k, L1_ffn_W_v, L1_ffn_mu_r, L1_ffn_mu_k):
    import jax
    import jax.numpy as jnp

    def _L0_xattn_ref(Q, K, V, mask, Wq, bq, Wk, bk, Wv, bv, Wo, bo):
        import jax, jax.numpy as jnp
        import numpy as np
        B, S, D, H = (2, 512, 256, 16)
        HD = D // H

        def _split_heads(x):
            b, s, _ = x.shape
            return x.reshape(b, s, H, HD).transpose(0, 2, 1, 3)
        q = _split_heads(Q @ Wq.T + bq)
        k = _split_heads(K @ Wk.T + bk)
        v = _split_heads(V @ Wv.T + bv)
        scale = 1.0 / jnp.sqrt(jnp.asarray(D / H, q.dtype))
        scores = jnp.einsum('bhqd,bhkd->bhqk', q, k) * scale
        scores = jnp.where(mask == 0, jnp.asarray(-1000000000.0, scores.dtype), scores)
        probs = jax.nn.softmax(scores, axis=-1)
        z = jnp.einsum('bhqk,bhkd->bhqd', probs, v)
        z = z.transpose(0, 2, 1, 3).reshape(Q.shape[0], Q.shape[1], D)
        return z @ Wo.T + bo

    def _L0_ffn_ref(x, wqkv, q_scale, k_scale, wo, ln_g, ln_b, w1, b1, w2, b2):
        import jax, jax.numpy as jnp
        import numpy as np
        DIM = 256
        DEPTH = 2
        HEADS = 8
        DIM_HEAD = 64
        WINDOW = 128
        INNER = HEADS * DIM_HEAD
        HID = int(DIM * 4 * 2 / 3)
        B, N = (2, 2048)
        QK_SCALE = 8.0

        def shift_token(t):
            t1, t2 = jnp.split(t, 2, axis=-1)
            t2 = jnp.pad(t2, ((0, 0), (1, 0), (0, 0)))[:, :-1]
            return jnp.concatenate([t1, t2], axis=-1)

        def l2norm(t):
            return t / jnp.clip(jnp.linalg.norm(t, axis=-1, keepdims=True), 1e-12)

        def rotate_half(x):
            x1, x2 = jnp.split(x, 2, axis=-1)
            return jnp.concatenate([-x2, x1], axis=-1)

        def rotary_xpos(q, k):
            n = q.shape[-2]
            half_idx = jnp.arange(0, DIM_HEAD, 2, dtype=jnp.float32)
            inv_freq = 1.0 / 10000.0 ** (half_idx / DIM_HEAD)
            t = jnp.arange(n, dtype=jnp.float32)
            freqs = t[:, None] * inv_freq[None, :]
            freqs = jnp.concatenate([freqs, freqs], axis=-1)
            base = (half_idx + 0.4 * DIM_HEAD) / (1.4 * DIM_HEAD)
            power = (t - n // 2) / float(WINDOW // 2)
            scale = base[None, :] ** power[:, None]
            scale = jnp.concatenate([scale, scale], axis=-1)
            cos, sin = (jnp.cos(freqs), jnp.sin(freqs))
            q = q * cos * scale + rotate_half(q) * sin * scale
            k = k * cos / scale + rotate_half(k) * sin / scale
            return (q, k)

        def local_attention(q, k, v):
            b, h, n, d = q.shape
            w = n // WINDOW
            bq = q.reshape(b, h, w, WINDOW, d) * QK_SCALE
            bk = k.reshape(b, h, w, WINDOW, d)
            bv = v.reshape(b, h, w, WINDOW, d)

            def look_around(t):
                p = jnp.pad(t, ((0, 0), (0, 0), (1, 0), (0, 0), (0, 0)))
                return jnp.concatenate([p[:, :, :w], p[:, :, 1:]], axis=3)
            bk, bv = (look_around(bk), look_around(bv))
            bt = jnp.arange(n).reshape(w, WINDOW)
            btp = jnp.pad(bt, ((1, 0), (0, 0)), constant_values=-1)
            btk = jnp.concatenate([btp[:w], btp[1:]], axis=1)
            sim = jnp.einsum('bhwid,bhwjd->bhwij', bq, bk)
            i = bt[:, :, None]
            j = btk[:, None, :]
            mask = (i < j) | (i > j + WINDOW) | (j == -1)
            sim = jnp.where(mask, -jnp.finfo(sim.dtype).max, sim)
            attn = jax.nn.softmax(sim, axis=-1)
            out = jnp.einsum('bhwij,bhwjd->bhwid', attn, bv)
            return out.reshape(b, h, n, d)

        def _layer(x, wqkv, qs, ksc, wo, lg, lb, w1, b1, w2, b2):
            b, n, _ = x.shape
            h = shift_token(x)
            qkv = h @ wqkv
            q, k, v = jnp.split(qkv, 3, axis=-1)
            to_heads = lambda t: t.reshape(b, n, HEADS, DIM_HEAD).transpose(0, 2, 1, 3)
            q, k, v = (to_heads(q), to_heads(k), to_heads(v))
            q = l2norm(q) * qs
            k = l2norm(k) * ksc
            q, k = rotary_xpos(q, k)
            o = local_attention(q, k, v)
            o = o.transpose(0, 2, 1, 3).reshape(b, n, INNER)
            x = x + o @ wo
            h = shift_token(x)
            mu = h.mean(-1, keepdims=True)
            var = h.var(-1, keepdims=True)
            h = (h - mu) / jnp.sqrt(var + 1e-05) * lg + lb
            h = h @ w1 + b1
            a, g = jnp.split(h, 2, axis=-1)
            h = a * jax.nn.gelu(g, approximate=False)
            x = x + h @ w2 + b2
            return x
        for l in range(DEPTH):
            x = _layer(x, wqkv[l], q_scale[l], k_scale[l], wo[l], ln_g[l], ln_b[l], w1[l], b1[l], w2[l], b2[l])
        return x

    def _L1_xattn_ref(x, historical_data, Wq, Wk, Wv, hist_W, hist_b, hist_ln_g, hist_ln_b, ctx_W1, ctx_b1, ctx_W2, ctx_b2, kg_W1, kg_b1, kg_ln_g, kg_ln_b, kg_W2, kg_b2, proj_W, proj_b, causal_mask):
        import jax, jax.numpy as jnp
        import numpy as np
        from jax import lax
        H = 16
        K1, K2 = (3, 3)
        LN_EPS = 1e-05

        def _ln(x, g, b):
            m = jnp.mean(x, axis=-1, keepdims=True)
            v = jnp.mean(jnp.square(x - m), axis=-1, keepdims=True)
            return (x - m) * lax.rsqrt(v + LN_EPS) * g + b

        def _gelu(x):
            return jax.nn.gelu(x, approximate=False)
        B, T, D = x.shape
        hd = D // H
        scale = hd ** (-0.5)
        q = (x @ Wq).reshape(B, T, H, hd).transpose(0, 2, 1, 3)
        k = (x @ Wk).reshape(B, T, H, hd).transpose(0, 2, 1, 3)
        v = (x @ Wv).reshape(B, T, H, hd).transpose(0, 2, 1, 3)
        attn = jnp.einsum('bhqd,bhkd->bhqk', q, k) * scale
        eh = _gelu(_ln(historical_data @ hist_W + hist_b, hist_ln_g, hist_ln_b))
        aw = _gelu(eh @ ctx_W1 + ctx_b1) @ ctx_W2 + ctx_b2
        aw = jax.nn.softmax(aw, axis=1)
        cc = jnp.sum(eh * aw, axis=1)
        kp = _gelu(_ln(cc @ kg_W1 + kg_b1, kg_ln_g, kg_ln_b)) @ kg_W2 + kg_b2
        kernels = jax.nn.softmax(kp.reshape(B, H, K1 * K2), axis=-1)
        kernels = kernels.reshape(B * H, 1, K1, K2)
        mask = causal_mask[None, None]
        attn0 = jnp.where(mask, 0.0, attn).reshape(1, B * H, T, T)
        attn = lax.conv_general_dilated(attn0, kernels, window_strides=(1, 1), padding=((K1 // 2, K1 // 2), (K2 // 2, K2 // 2)), feature_group_count=B * H, dimension_numbers=('NCHW', 'OIHW', 'NCHW')).reshape(B, H, T, T)
        attn = jnp.where(mask, -jnp.inf, attn)
        p = jax.nn.softmax(attn, axis=-1)
        out = jnp.einsum('bhqk,bhkd->bhqd', p, v)
        out = out.transpose(0, 2, 1, 3).reshape(B, T, D)
        return out @ proj_W + proj_b

    def _L1_ffn_ref(x, W_r, W_k, W_v, mu_r, mu_k):
        import jax, jax.numpy as jnp
        import numpy as np
        DIM = 256

        def _reference_tuple_inner(x, W_r, W_k, W_v, mu_r, mu_k):
            B, T, C = x.shape
            x_prev = jnp.concatenate([jnp.zeros((B, 1, C), x.dtype), x[:, :-1, :]], axis=1)
            xr = mu_r * x + (1.0 - mu_r) * x_prev
            xk = mu_k * x + (1.0 - mu_k) * x_prev
            r = jax.nn.sigmoid(jnp.einsum('btc,dc->btd', xr, W_r))
            k = jnp.einsum('btc,dc->btd', xk, W_k)
            k_act = jnp.square(jax.nn.relu(k))
            out = r * jnp.einsum('btc,dc->btd', k_act, W_v)
            new_state = x[:, -1, :]
            return (out, new_state)
        return _reference_tuple_inner(x, W_r, W_k, W_v, mu_r, mu_k)[0]
    x = x + _L0_xattn_ref(_layernorm(x, axis=-1), ctx_1024, ctx_1024, mask_1x1xSxS2_ik0, L0_xattn_Wq, L0_xattn_bq, L0_xattn_Wk, L0_xattn_bk, L0_xattn_Wv, L0_xattn_bv, L0_xattn_Wo, L0_xattn_bo)
    x = x + _L0_ffn_ref(_layernorm(x, axis=-1), L0_ffn_wqkv, L0_ffn_q_scale, L0_ffn_k_scale, L0_ffn_wo, L0_ffn_ln_g, L0_ffn_ln_b, L0_ffn_w1, L0_ffn_b1, L0_ffn_w2, L0_ffn_b2)
    x = x + _L1_xattn_ref(_layernorm(x, axis=-1), ctx_1024, L1_xattn_Wq, L1_xattn_Wk, L1_xattn_Wv, L1_xattn_hist_W, L1_xattn_hist_b, L1_xattn_hist_ln_g, L1_xattn_hist_ln_b, L1_xattn_ctx_W1, L1_xattn_ctx_b1, L1_xattn_ctx_W2, L1_xattn_ctx_b2, L1_xattn_kg_W1, L1_xattn_kg_b1, L1_xattn_kg_ln_g, L1_xattn_kg_ln_b, L1_xattn_kg_W2, L1_xattn_kg_b2, L1_xattn_proj_W, L1_xattn_proj_b, mask_SxS_bc0)
    x = x + _L1_ffn_ref(_layernorm(x, axis=-1), L1_ffn_W_r, L1_ffn_W_k, L1_ffn_W_v, L1_ffn_mu_r, L1_ffn_mu_k)
    return x

_drawn_inputs = setup_inputs


def setup_inputs(seed=0):
    import zlib

    import numpy as np

    out = dict(_drawn_inputs(seed))
    spreads = {'L0_xattn_bq': (0.0, 0.281),
     'L0_xattn_bk': (0.0, 0.8),
     'L0_xattn_bv': (0.0, 0.1),
     'L0_xattn_bo': (0.0, 0.1),
     'L0_ffn_q_scale': (1.0, 0.6),
     'L0_ffn_k_scale': (1.0, 0.6),
     'L0_ffn_ln_g': (1.0, 0.6),
     'L0_ffn_ln_b': (0.0, 0.8),
     'L0_ffn_b1': (0.0, 0.8),
     'L0_ffn_b2': (0.0, 0.1),
     'L1_xattn_hist_b': (0.0, 0.8),
     'L1_xattn_hist_ln_g': (1.0, 0.6),
     'L1_xattn_hist_ln_b': (0.0, 0.8),
     'L1_xattn_ctx_b1': (0.0, 0.8),
     'L1_xattn_kg_b1': (0.0, 0.8),
     'L1_xattn_kg_ln_g': (1.0, 0.6),
     'L1_xattn_kg_ln_b': (0.0, 0.8),
     'L1_xattn_kg_b2': (0.0, 0.8),
     'L1_xattn_proj_b': (0.0, 0.1)}
    factors = {'L1_xattn_Wq': 3.239,
     'L1_xattn_Wk': 3.233,
     'L1_xattn_hist_W': 8.0,
     'L1_xattn_ctx_W1': 8.0,
     'L1_xattn_ctx_W2': 8.0,
     'L1_xattn_kg_W1': 7.799,
     'L1_xattn_kg_W2': 6.802,
     'L1_ffn_W_r': 5.893,
     'L1_ffn_mu_r': 8.0,
     'L1_ffn_mu_k': 3.309}
    for name, (base, spread) in spreads.items():
        noise = np.random.default_rng([zlib.crc32(name.encode()), seed]).standard_normal(out[name].shape)
        drawn = base * np.exp(spread * noise) if base else spread * noise
        out[name] = jnp.asarray(drawn.astype(out[name].dtype))
    for name, factor in factors.items():
        out[name] = (out[name] * factor).astype(out[name].dtype)
    return out
```

```python
from contextlib import ExitStack

import numpy as np

import concourse.bass as bass
from concourse import mybir

F32 = mybir.dt.float32
U8 = mybir.dt.uint8
I32 = mybir.dt.int32
ALU = mybir.AluOpType
ACT = mybir.ActivationFunctionType
AX_X = mybir.AxisListType.X

P = 128
B, T, D = 32, 256, 256
KD = D // P
C = 77
H, HD = 16, 16
H2, HD2 = 8, 64
INNER = H2 * HD2
DEPTH = 2
HID = 682
HF = HID // P
HR = HID - HF * P
HIST = 512
NB = 2
STEPS = B // NB
NT = NB * T // P
PAR = 2
GW = P + 2
EPS = 1e-5
NEG = -1e9
FAR = -1e30
ER, PR = 4, 3
RING = 6

ITERS, STAGES = STEPS, 4
LAG1, LAG2 = 3, 2


def local_groups(t):
    if t % 2 == 0:
        return [(par, [par, par + 2, par + 4, par + 6], [t]) for par in range(2)]
    return [(par, [par + 4 * hf, par + 4 * hf + 2], [t - 1, t]) for hf in range(2) for par in range(2)]


LOCAL = [(t, g) for t in range(NT) for g in range(len(local_groups(t)))]
CROSS = [(t, r) for t in range(NT) for r in range(4)]
CONV = [(bb, h) for bb in range(NB) for h in range(H)]


def bass_cross_local_conv_mix_kernel(nc, a, out):
    with ExitStack() as ctx:
        def sb(name, shape, dt=F32):
            return ctx.enter_context(nc.sbuf_tensor(name, shape, dt))

        def sem(name):
            return ctx.enter_context(nc.semaphore(name))

        def carve(whole, lo, shape):
            n = int(np.prod(shape[1:]))
            ap = whole[0:shape[0], lo:lo + n]
            names = "abcd"[:len(shape) - 1]
            sizes = dict(zip(names, shape[1:]))
            return ap if len(shape) == 2 else ap.rearrange(f"p ({' '.join(names)}) -> p {' '.join(names)}", **sizes)

        qk_cols = sb("qk_cols", [P, 2 * 4 * NT * P])
        e_cols = sb("e_cols", [P, (ER + PR) * 512])
        o_cols = sb("o_cols", [P, 2 * NT * INNER])
        h_cols = sb("h_cols", [P, (2 + HF + 1) * NT * P])

        bank = [ctx.enter_context(nc.psum_tensor(f"bank{b}", [P, 512], F32)) for b in range(8)]

        W = {}
        loads = []

        def weight(name, shape, src, dt=F32, at=None):
            W[name] = sb("w_" + name, shape, dt) if at is None else carve(*at, shape)
            loads.append((W[name], src))
            return W[name]

        def kmaj(ap):
            return ap.rearrange("(k p) n -> p k n", p=P)

        def column(ap, n):
            return ap.rearrange("(k p) -> p k", p=P) if n * P == ap.shape[0] else ap

        ident = weight("ident", [P, P], a["ident"])
        shiftm = weight("shift", [P, 2, P], a["shift"])
        diag = weight("diag", [P, 3, GW], a["diag"])
        causal = weight("causal", [P, 2, P], a["causal"])
        parity = weight("parity", [P, PAR], a["parity"])
        rot = weight("rot", [P, 2, 4, HD2], a["rot"])
        for name in ("L0_xattn_Wq", "L0_xattn_Wk", "L0_xattn_Wv", "L0_xattn_Wo", "L1_xattn_Wq", "L1_xattn_Wk",
                     "L1_xattn_Wv", "L1_xattn_proj_W", "L1_ffn_W_r", "L1_ffn_W_k", "L1_ffn_W_v"):
            weight(name, [P, KD, D], kmaj(a[name]))
        for l in range(DEPTH):
            weight(f"qkv{l}", [P, KD, 3 * INNER], kmaj(a["L0_ffn_wqkv"][l]))
            weight(f"wo{l}", [P, INNER // P, D], kmaj(a["L0_ffn_wo"][l]))
            weight(f"w1{l}", [P, KD, 2 * HF * P + P], kmaj(a["w1p"][l]))
            w2 = weight(f"w2{l}", [P, HF + 1, D], kmaj(a["w2p"][l]))
            weight(f"g{l}", [P, KD], a["L0_ffn_ln_g"][l])
            weight(f"b{l}", [P, KD], a["L0_ffn_ln_b"][l])
            weight(f"b1{l}", [P, 2 * HF + 1], a["b1p"][l])
            for n in ("q", "k"):
                weight(f"{n}s{l}", [P, HD2], a[f"L0_ffn_{n}_scale"][l].partition_broadcast(P))
        for name in ("L0_xattn_bq", "L0_xattn_bk", "L1_ffn_mu_r", "L1_ffn_mu_k"):
            weight(name, [P, KD], a[name])
        for name in ("L0_xattn_bv", "L0_xattn_bo", "L1_xattn_proj_b"):
            weight(name, [P, D], a[name].partition_broadcast(P))
        mask_i = weight("mask_i", [P, 2, C], a["mask_1x1xSxS2_ik0"].rearrange("(k p) n -> p k n", p=P), I32)
        weight("far_u", [P, 2, T // 4], a["far"].rearrange("(k p) n -> p k n", p=P), I32)
        weight("farT_u", [P, 2, T // 4], a["farT"].rearrange("(k p) n -> p k n", p=P), I32)
        weight("histW", [P, KD, HIST], kmaj(a["L1_xattn_hist_W"]), at=(e_cols, 0))
        weight("histb", [P, HIST], a["L1_xattn_hist_b"].partition_broadcast(P), at=(e_cols, 1024))
        weight("histg", [P, HIST], a["L1_xattn_hist_ln_g"].partition_broadcast(P), at=(e_cols, 1536))
        weight("histB", [P, HIST], a["L1_xattn_hist_ln_b"].partition_broadcast(P), at=(e_cols, 2048))
        weight("ctxW1", [P, HIST // P, P], kmaj(a["L1_xattn_ctx_W1"]), at=(qk_cols, 0))
        weight("ctxb1", [P, 1], a["L1_xattn_ctx_b1"])
        weight("ctxW2", [P, 1], a["L1_xattn_ctx_W2"])
        weight("ctxb2", [1, 1], a["L1_xattn_ctx_b2"])
        weight("kgW1", [P, HIST // P, D], kmaj(a["L1_xattn_kg_W1"]), at=(qk_cols, 512))
        weight("kgW2", [P, KD, H * 9], kmaj(a["L1_xattn_kg_W2"]), at=(qk_cols, 1536))
        weight("kgb1", [B, D], a["L1_xattn_kg_b1"].partition_broadcast(B), at=(qk_cols, 1824))
        weight("kgg", [B, D], a["L1_xattn_kg_ln_g"].partition_broadcast(B), at=(qk_cols, 2080))
        weight("kgB", [B, D], a["L1_xattn_kg_ln_b"].partition_broadcast(B), at=(qk_cols, 2336))
        weight("kgb2", [B, H * 9], a["L1_xattn_kg_b2"].partition_broadcast(B), at=(qk_cols, 2592))

        negm = sb("negm", [P, 2, C])
        far = sb("far_m", [P, 2, T])
        keepT = sb("keepT", [P, 2, T])
        rotl = sb("rotl", [P, DEPTH, 2, 4, HD2])
        omr = sb("omr", [P, 2, KD])
        half = sb("half", [P, H2])

        xin = sb("xin", [P, NT, D])
        x = sb("x", [P, NT, D])
        y = sb("y", [P, NT, D])
        xo = y
        xn = sb("xn", [P, NT, D])
        ctxT = sb("ctxT", [P, KD, NB * C])
        F = sb("F", [P, KD, NB, T + 1])
        QT = carve(h_cols, 2900, [P, KD, NB * T])
        KT1 = carve(o_cols, 2 * NT * P, [P, KD, NB, PAR, C])
        V1 = sb("V1", [P, NB, H, HD + 1])
        E = carve(e_cols, 0, [P, ER, 512])
        PT = carve(e_cols, ER * 512, [P, PR, 512])
        stats = sb("stats", [P, NT, 2, 6])
        mv = sb("mv", [P, NT, 2])
        rstd = sb("rstd", [P, NT])
        mx = sb("mx", [P, 2, 4])
        rz = sb("rz", [P, 2 * H])
        sq = carve(h_cols, 0, [P, 2, INNER])
        ss = sb("ss", [P, 2, H2])
        rr = sb("rr", [P, 2, H2])
        qn = carve(h_cols, 2 * INNER, [P, 2, INNER])
        qa = carve(h_cols, 4 * INNER, [P, 2, INNER])
        qb = carve(h_cols, 6 * INNER, [P, 2, INNER])
        QT2 = carve(qk_cols, 0, [P, 4, NT * P])
        KT2 = carve(qk_cols, 4 * NT * P, [P, 4, NT * P])
        V2 = sb("V2", [P, NT, H2, HD2 + 1])
        O2 = carve(o_cols, 0, [P, NT, INNER])
        OT = carve(o_cols, NT * INNER, [P, INNER // P, NT * P])
        G = carve(h_cols, 0, [P, 2, NT * P])
        HH = carve(h_cols, 2 * NT * P, [P, HF + 1, NT * P])
        KT3 = carve(qk_cols, 0, [P, KD, PAR, NB * T])
        V3 = carve(h_cols, 1812, [P, NT, H, HD + 1])
        S0 = carve(h_cols, 0, [P, 2, 2, T + 2])
        band = carve(h_cols, 1032, [P, 2, 3, GW])
        kern = sb("kern", [P, NB, H * 9])
        XR = carve(qk_cols, 4 * NT * P, [P, 2, KD, NB * T])
        KA = carve(o_cols, 0, [P, KD, NB * T])
        sg = carve(h_cols, 0, [P, 2, D])
        kern_d = nc.dram_tensor("kernels_of_all", [B, H * 9], F32).ap()

        eh = carve(o_cols, 0, [P, NB, HIST])
        ehs = carve(o_cols, 1024, [P, NB, HIST])
        ehT = carve(o_cols, 2048, [P, HIST // P, NB, C])
        h1 = carve(o_cols, 3072, [P, NB * C])
        aw = sb("aw", [1, NB, C])
        awc = sb("awc", [P, NB])
        am = sb("am", [1, NB, 3])
        cc = sb("cc", [P, HIST // P, B])
        one = sb("one", [1, 1])
        spare = sb("spare", [1, 1])
        fence = sb("fence", [1, 1])
        kg = sb("kg", [B, D])
        kgT = sb("kgT", [P, KD, B])
        kp = sb("kp", [B, H, 9])
        km = sb("km", [B, 2, H])

        per_step, given = {}, {}

        def signal(name, count=1, by=1):
            s = sem(name)
            per_step[s], given[s] = (count, by), 0
            return s

        def due(s, it, n):
            count, by = per_step[s]
            return (it * count + n + 1) * by

        def own(s, it):
            given[s] += 1
            return due(s, it, given[s] - 1)

        place, fills = {}, [0] * 8
        bank_full = [sem(f"bank_full{b}") for b in range(8)]

        def full_of(key):
            return bank_full[place[key][0]]

        def full_at(key, it):
            b, n = place[key]
            return it * fills[b] + n + 1

        def bank_of(key):
            return bank[place[key][0]]

        LN = 6
        NF = 9
        weights_in, consts_set, kern_out = sem("weights_in"), sem("consts_set"), sem("kern_out")
        x_in, ctx_in, kern_in = signal("x_in", 1, 16), signal("ctx_in", 1, 16), signal("kern_in", 1, 16)
        x_out = signal("x_out", 1, 16)
        xo_ready = signal("xo_ready", NT)
        hist_in = signal("hist_in", 1, 16)
        hist_go = signal("hist_go")
        hist_h, hist_T, hist_1 = signal("hist_h"), signal("hist_T"), signal("hist_1")
        hist_2, hist_w, hist_c = signal("hist_2"), signal("hist_w"), signal("hist_c")
        hist_dve = signal("hist_dve", 10)
        hist_var, hist_rstd = signal("hist_var"), signal("hist_rstd")
        ehs_ready, eh_ready, ehT_ready, h1_ready = signal("ehs_ready"), signal("eh_ready"), signal("ehT_ready"), signal("h1_ready")
        aws_ready, awe_ready, aw_ready, awc_ready = signal("aws_ready"), signal("awe_ready"), signal("aw_ready"), signal("awc_ready")
        cc_ready = signal("cc_ready")
        kg_1, kg_T, kg_2, kg_dve = signal("kg_1"), signal("kg_T"), signal("kg_2"), signal("kg_dve")
        kg_var, kg_rstd = signal("kg_var"), signal("kg_rstd")
        kgs_ready, kg_ready, kgT_ready = signal("kgs_ready"), signal("kg_ready"), signal("kgT_ready")
        kps_ready, kpe_ready, kp_ready = signal("kps_ready"), signal("kpe_ready"), signal("kp_ready")
        ln_stats, ln_moments = signal("ln_stats", LN), signal("ln_moments", LN)
        var_ready, rstd_ready = signal("var_ready", LN), signal("rstd_ready", LN)
        tok_ready = signal("tok_ready", NF * NT)
        feat_a, feat_v = signal("feat_a", NF), signal("feat_v", NF)
        NSM = len(CROSS) + DEPTH * len(LOCAL) + len(CONV)
        sm_masked, sm_max = signal("sm_masked", NSM), signal("sm_max", NSM)
        rz_ready = signal("rz_ready", NT + DEPTH * NT * 2 + NT)
        e1_ready, p1_ready, pt1_ready = signal("e1_ready", len(CROSS)), signal("p1_ready", len(CROSS)), signal("pt1_ready", len(CROSS))
        e2_ready, p2_ready, pt2_ready = signal("e2_ready", DEPTH * len(LOCAL)), signal("p2_ready", DEPTH * len(LOCAL)), signal("pt2_ready", DEPTH * len(LOCAL))
        e3_ready, p3_ready, pt3_ready = signal("e3_ready", len(CONV)), signal("p3_ready", len(CONV)), signal("pt3_ready", len(CONV))
        qk1_ready = signal("qk1_ready", KD + 1 + NB)
        xb_ready = signal("xb_ready", NT)
        x1_ready = signal("x1_ready", NT)
        sq_ready = signal("sq_ready", DEPTH * NT * 2)
        ss_sum, ss_ready = signal("ss_sum", DEPTH * NT * 2), signal("ss_ready", DEPTH * NT * 2)
        rr_ready = signal("rr_ready", DEPTH * NT * 2)
        qn_ready, qa_ready = signal("qn_ready", DEPTH * NT * 2), signal("qa_ready", DEPTH * NT * 2)
        qb_ready = signal("qb_ready", DEPTH * NT * 2)
        qr_ready = signal("qr_ready", DEPTH * NT * 2)
        qkT_ready, v2_ready = signal("qkT_ready", DEPTH * NT * 2), signal("v2_ready", DEPTH * NT)
        o2_ready, oT_ready = signal("o2_ready", DEPTH * NT), signal("oT_ready", DEPTH * NT)
        y_ready, w2_read = signal("y_ready", DEPTH * NT), signal("w2_read", DEPTH * NT)
        ones_row = signal("ones_row", DEPTH)
        g_ready, hh_ready = signal("g_ready", DEPTH * (HF + 1)), signal("hh_ready", DEPTH * (HF + 1))
        x2_ready = signal("x2_ready")
        qk3_ready, v3_ready, ones3_ready = signal("qk3_ready", 2 * KD), signal("v3_ready", NT), signal("ones3_ready")
        s0_ready = signal("s0_ready", len(CONV))
        band_part, band_ready = signal("band_part", 2 * len(CONV)), signal("band_ready", len(CONV))
        x3_ready, x3_done = signal("x3_ready", NT), signal("x3_done")
        xr_part, xr_ready = signal("xr_part", 2), signal("xr_ready", 2)
        ka_part, ka_ready = signal("ka_part", KD), signal("ka_ready", KD)
        sg_ready, sg_part = signal("sg_ready", NT), signal("sg_part", NT)

        def tile_cols(t, shift=0):
            return slice((t % 2) * P + 1 - shift, (t % 2) * P + P + 1 - shift)

        def wide(ap, shape, axis):
            return ap.unsqueeze(axis).broadcast_to(shape)

        L = range(DEPTH) if STAGES >= 2 else range(0)
        block = ctx.enter_context(nc.Block())

        @block.tensor
        def _(pe):
            pe.wait_ge(weights_in, 16 * len(loads))
            pe.wait_ge(consts_set, 2)
            mm = nc.tensor.matmul
            tp = nc.tensor.transpose

            if STAGES >= 3:
                with pe.Fori(0, STEPS) as it:
                    pe.wait_ge(hist_in, due(hist_in, it, 0))
                    pe.wait_ge(hist_go, due(hist_go, it, 0))
                    for bb in range(NB):
                        for k in range(KD):
                            last = mm(bank[bb][0:C, :], ctxT[:, k, bb * C:(bb + 1) * C], W["histW"][:, k, :],
                                      start=k == 0, stop=k == KD - 1)
                    last.then_inc(hist_h, 1)
                    pe.wait_ge(eh_ready, due(eh_ready, it, 0))
                    for bb in range(NB):
                        for c in range(HIST // P):
                            last = tp(bank[2 + bb][:, c * P:c * P + C], eh[0:C, bb, c * P:(c + 1) * P], ident[0:C, 0:C])
                    last.then_inc(hist_T, 1)
                    pe.wait_ge(ehT_ready, due(ehT_ready, it, 0))
                    for c in range(HIST // P):
                        last = mm(bank[4][:, 0:NB * C], W["ctxW1"][:, c, :], ehT[:, c, :, :].rearrange("p b n -> p (b n)"),
                                  start=c == 0, stop=c == HIST // P - 1)
                    last.then_inc(hist_1, 1)
                    pe.wait_ge(h1_ready, due(h1_ready, it, 0))
                    mm(bank[5][0:1, 0:NB * C], W["ctxW2"][:, 0:1], h1[:, :], start=True, stop=True).then_inc(hist_2, 1)
                    pe.wait_ge(aw_ready, due(aw_ready, it, 0))
                    for bb in range(NB):
                        last = mm(bank[6][0:C, bb:bb + 1], aw[0:1, bb, :], one[0:1, 0:1], start=True, stop=True)
                    last.then_inc(hist_w, 1)
                    pe.wait_ge(awc_ready, due(awc_ready, it, 0))
                    for c in range(HIST // P):
                        for bb in range(NB):
                            last = mm(bank[7][:, c * NB + bb:c * NB + bb + 1], eh[0:C, bb, c * P:(c + 1) * P],
                                      awc[0:C, bb:bb + 1], start=True, stop=True)
                    last.then_inc(hist_c, 1)
                it = 0
                pe.wait_ge(cc_ready, due(cc_ready, it, 0))
                for c in range(HIST // P):
                    last = mm(bank[0][0:B, 0:D], cc[:, c, :], W["kgW1"][:, c, :], start=c == 0, stop=c == HIST // P - 1)
                last.then_inc(kg_1, 1)
                pe.wait_ge(kg_ready, due(kg_ready, it, 0))
                for k in range(KD):
                    last = tp(bank[1][:, k * B:(k + 1) * B], kg[:, k * P:(k + 1) * P], ident[0:B, 0:B])
                last.then_inc(kg_T, 1)
                pe.wait_ge(kgT_ready, due(kgT_ready, it, 0))
                for k in range(KD):
                    last = mm(bank[2][0:B, 0:H * 9], kgT[:, k, :], W["kgW2"][:, k, :], start=k == 0, stop=k == KD - 1)
                last.then_inc(kg_2, 1)
                pe.wait_ge(kp_ready, due(kp_ready, it, 0))

            with pe.Fori(0, ITERS) as it:
                turn, readers = [0, 0], {}

                def take(key, read, ring=0):
                    b = turn[0] % RING if ring == 0 else RING + turn[1] % (8 - RING)
                    turn[ring] += 1
                    if b in readers:
                        pe.wait_ge(readers[b][0], due(readers[b][0], it, readers[b][1]))
                    readers[b] = read
                    place[key] = (b, fills[b])
                    fills[b] += 1
                    return bank[b]

                def seq(m, shift=0):
                    return F[:, m, :, 1 - shift:T + 1 - shift]

                def to_features(n, src):
                    pe.wait_ge(tok_ready, due(tok_ready, it, n * NT))
                    for m in range(KD):
                        b = take(("fT", n, m), ((feat_a, feat_v)[m], n))
                        for t in range(NT):
                            if m == 0 and t:
                                pe.wait_ge(tok_ready, due(tok_ready, it, n * NT + t))
                            last = tp(b[:, t * P:(t + 1) * P], src[:, t, m * P:(m + 1) * P], ident[:])
                        last.then_inc(full_of(("fT", n, m)), 1)
                    pe.wait_ge(feat_a, due(feat_a, it, n))
                    pe.wait_ge(feat_v, due(feat_v, it, n))

                def to_tokens(key, reader, w, n=D, shift=False, src=None, col=0):
                    t = key[-1]
                    b = take(key, reader)
                    for k in range(KD):
                        if src is None:
                            lhs = F[:, k, t // 2, tile_cols(t, 1 if shift and k == 1 else 0)]
                        else:
                            lhs = src(k)[:, t * P:(t + 1) * P]
                        last = mm(b[:, 0:n], lhs, w[:, k, col:col + n], start=k == 0, stop=k == KD - 1)
                    last.then_inc(full_of(key), 1)

                def to_columns(key, reader, w, m, rhs):
                    b = take(key, reader)
                    for k in range(KD):
                        last = mm(b[:, :].rearrange("p (b t) -> p b t", b=NB), w[:, k, m * P:(m + 1) * P], rhs(k),
                                  start=k == 0, stop=k == KD - 1)
                    last.then_inc(full_of(key), 1)

                to_features(0, xn)
                for m in range(KD):
                    to_columns(("q1", m), (qk1_ready, m), W["L0_xattn_Wq"], m, seq)
                pe.wait_ge(ctx_in, due(ctx_in, it, 0))
                b = take(("k1",), (qk1_ready, KD))
                for m in range(KD):
                    for k in range(KD):
                        last = mm(b[:, m * 256:m * 256 + NB * C], W["L0_xattn_Wk"][:, k, m * P:(m + 1) * P], ctxT[:, k, :],
                                  start=k == 0, stop=k == KD - 1)
                last.then_inc(full_of(("k1",)), 1)
                for bb in range(NB):
                    b = take(("v1", bb), (qk1_ready, KD + 1 + bb))
                    for k in range(KD):
                        last = mm(b[0:C, 0:D], ctxT[:, k, bb * C:(bb + 1) * C], W["L0_xattn_Wv"][:, k, :],
                                  start=k == 0, stop=k == KD - 1)
                    last.then_inc(full_of(("v1", bb)), 1)
                pe.wait_ge(qk1_ready, due(qk1_ready, it, KD + NB))
                for u in range(-LAG1, len(CROSS) + 1):
                    if u + LAG1 < len(CROSS):
                        t, r = CROSS[u + LAG1]
                        b = take(("s1", u + LAG1), (e1_ready, u + LAG1))
                        rows = slice(32 * r, 32 * r + 32)
                        for m in range(KD):
                            last = mm(b[:, m * 2 * C:(m + 1) * 2 * C], QT[rows, m, t * P:(t + 1) * P],
                                      KT1[rows, m, t // 2, :, :].rearrange("p a n -> p (a n)"), start=True, stop=True)
                        last.then_inc(full_of(("s1", u + LAG1)), 1)
                    if 0 <= u < len(CROSS):
                        b = take(("t1", u), (pt1_ready, u))
                        pe.wait_ge(p1_ready, due(p1_ready, it, u))
                        for i in range(4):
                            last = tp(b[0:C, i * P:(i + 1) * P], E[:, u % ER, i * C:(i + 1) * C], ident[:])
                        last.then_inc(full_of(("t1", u)), 1)
                    if u >= 1:
                        t, r = CROSS[u - 1]
                        if r == 0:
                            z = take(("z1", t), (tok_ready, NT + t), ring=1)
                        pe.wait_ge(pt1_ready, due(pt1_ready, it, u - 1))
                        for i, h in enumerate((2 * r, 2 * r + 1, 2 * r + 8, 2 * r + 9)):
                            last = mm(z[:, h * (HD + 1):(h + 1) * (HD + 1)], PT[0:C, (u - 1) % PR, i * P:(i + 1) * P],
                                      V1[0:C, t // 2, h, :], start=True, stop=True)
                        if r == 3:
                            last.then_inc(full_of(("z1", t)), 1)
                to_features(1, xn)
                for t in range(NT):
                    to_tokens(("o1", t), (x1_ready, t), W["L0_xattn_Wo"])

                for l in L:
                    to_features(2 + 2 * l, y)

                    def turn_qk(t):
                        for i, k in enumerate(("qT", "kT")):
                            n = l * 2 * NT + 2 * t + i
                            pe.wait_ge(qr_ready, due(qr_ready, it, n))
                            b = take((k, l, t), (qkT_ready, n))
                            for hp in range(4):
                                last = tp(b[:, hp * P:(hp + 1) * P], qa[:, i, hp * P:(hp + 1) * P], ident[:])
                            last.then_inc(full_of((k, l, t)), 1)

                    for t in range(NT):
                        for i, k in enumerate(("q2", "k2", "v2")):
                            reader = (v2_ready, l * NT + t) if i == 2 else (qn_ready, l * 2 * NT + 2 * t + i)
                            to_tokens((k, l, t), reader, W[f"qkv{l}"], n=INNER, shift=True, col=i * INNER)
                        if t >= 1:
                            turn_qk(t - 1)
                    turn_qk(NT - 1)
                    pe.wait_ge(v2_ready, due(v2_ready, it, l * NT + NT - 1))
                    pe.wait_ge(qkT_ready, due(qkT_ready, it, l * 2 * NT + 2 * NT - 1))
                    for u in range(-LAG2, len(LOCAL) + 1):
                        if u + LAG2 < len(LOCAL):
                            t, g = LOCAL[u + LAG2]
                            b = take(("s2", l, u + LAG2), (e2_ready, l * len(LOCAL) + u + LAG2))
                            par, heads, tiles = local_groups(t)[g]
                            rows = slice(64 * par, 64 * par + 64)
                            w = P * len(tiles)
                            for i, h in enumerate(heads):
                                last = mm(b[:, i * w:(i + 1) * w], QT2[rows, h // 2, t * P:(t + 1) * P],
                                          KT2[rows, h // 2, tiles[0] * P:tiles[0] * P + w], start=True, stop=True)
                            last.then_inc(full_of(("s2", l, u + LAG2)), 1)
                        if 0 <= u < len(LOCAL):
                            b = take(("t2", l, u), (pt2_ready, l * len(LOCAL) + u))
                            pe.wait_ge(p2_ready, due(p2_ready, it, l * len(LOCAL) + u))
                            for i in range(4):
                                last = tp(b[:, i * P:(i + 1) * P], E[:, u % ER, i * P:(i + 1) * P], ident[:])
                            last.then_inc(full_of(("t2", l, u)), 1)
                        if u >= 1:
                            t, g = LOCAL[u - 1]
                            if g == 0:
                                zs = [take(("z2", l, t, hf), (o2_ready, l * NT + t), ring=1) for hf in range(2)]
                            pe.wait_ge(pt2_ready, due(pt2_ready, it, l * len(LOCAL) + u - 1))
                            par, heads, tiles = local_groups(t)[g]
                            blk = 0
                            for h in heads:
                                for j, kt in enumerate(tiles):
                                    last = mm(zs[h // 4][:, (h % 4) * (HD2 + 1):(h % 4 + 1) * (HD2 + 1)],
                                              PT[:, (u - 1) % PR, blk * P:(blk + 1) * P], V2[:, kt, h, :],
                                              start=j == 0, stop=j == len(tiles) - 1)
                                    blk += 1
                                if h in (3, 7):
                                    last.then_inc(full_of(("z2", l, t, h // 4)), 1)
                    for t in range(NT):
                        pe.wait_ge(o2_ready, due(o2_ready, it, l * NT + t))
                        b = take(("oT", l, t), (oT_ready, l * NT + t))
                        for k in range(INNER // P):
                            last = tp(b[:, k * P:(k + 1) * P], O2[:, t, k * P:(k + 1) * P], ident[:])
                        last.then_inc(full_of(("oT", l, t)), 1)
                    for t in range(NT):
                        pe.wait_ge(oT_ready, due(oT_ready, it, l * NT + t))
                        b = take(("wo", l, t), (y_ready, l * NT + t))
                        for k in range(INNER // P):
                            last = mm(b[:, 0:D], OT[:, k, t * P:(t + 1) * P], W[f"wo{l}"][:, k, :],
                                      start=k == 0, stop=k == INNER // P - 1)
                        last.then_inc(full_of(("wo", l, t)), 1)
                    b = take(("sh", l), (tok_ready, (3 + 2 * l) * NT + NT - 1))
                    for t in range(NT):
                        pe.wait_ge(y_ready, due(y_ready, it, l * NT + t))
                        last = mm(b[:, t * P:(t + 1) * P], shiftm[:, 0, :], y[:, t, P:D], start=True, stop=t % 2 == 0)
                        if t % 2:
                            last = mm(b[:, t * P:(t + 1) * P], shiftm[:, 1, :], y[:, t - 1, P:D], start=False, stop=True)
                    last.then_inc(full_of(("sh", l)), 1)
                    to_features(3 + 2 * l, xn)
                    for j in range(HF):
                        for i, k in enumerate(("g", "a")):
                            to_columns((k, l, j), (hh_ready, l * (HF + 1) + j), W[f"w1{l}"], 2 * j + i, seq)
                    to_columns(("r", l), (hh_ready, l * (HF + 1) + HF), W[f"w1{l}"], 2 * HF, seq)
                    for t in range(NT):
                        b = take(("w2", l, t), (w2_read, l * NT + t))
                        for k in range(HF + 1):
                            if t == 0:
                                pe.wait_ge(hh_ready, due(hh_ready, it, l * (HF + 1) + k))
                            r = P if k < HF else HR + 1
                            last = mm(b[:, 0:D], HH[0:r, k, t * P:(t + 1) * P], W[f"w2{l}"][0:r, k, :],
                                      start=k == 0, stop=k == HF)
                        last.then_inc(full_of(("w2", l, t)), 1)

                if STAGES >= 3:
                    to_features(6, xn)
                    for m in range(KD):
                        to_columns(("q3", m), (qk3_ready, m), W["L1_xattn_Wq"], m, seq)
                    for m in range(KD):
                        to_columns(("k3", m), (qk3_ready, KD + m), W["L1_xattn_Wk"], m, seq)
                    for t in range(NT):
                        to_tokens(("v3", t), (v3_ready, t), W["L1_xattn_Wv"])
                    pe.wait_ge(qk3_ready, due(qk3_ready, it, 2 * KD - 1))
                    pe.wait_ge(v3_ready, due(v3_ready, it, NT - 1))
                    pe.wait_ge(ones3_ready, due(ones3_ready, it, 0))
                    for u in range(-2, len(CONV) + 1):
                        if u + 2 < len(CONV):
                            bb, h = CONV[u + 2]
                            b = take(("s3", u + 2), (s0_ready, u + 2))
                            r = (h // 2) % 4
                            rows = slice(32 * r, 32 * r + 32)
                            for jt in range(2):
                                last = mm(b[:, jt * T:(jt + 1) * T],
                                          KT3[rows, h // 8, h % 2, bb * T + jt * P:bb * T + (jt + 1) * P],
                                          QT[rows, h // 8, bb * T:(bb + 1) * T], start=True, stop=True)
                            last.then_inc(full_of(("s3", u + 2)), 1)
                        if 0 <= u + 1 < len(CONV):
                            b = take(("c3", u + 1), (e3_ready, u + 1))
                            pe.wait_ge(band_ready, due(band_ready, it, u + 1))
                            pe.wait_ge(s0_ready, due(s0_ready, it, u + 1))
                            for i2 in range(2):
                                n = 0
                                for jt in range(2):
                                    for tap in range(3):
                                        lo = jt * (P - 1)
                                        last = mm(b[:, i2 * T + lo:i2 * T + lo + P + 1],
                                                  S0[:, (u + 1) % 2, jt, i2 * P + tap:i2 * P + tap + P],
                                                  band[:, (u + 1) % 2, tap, 1 - jt:1 - jt + P + 1],
                                                  start=n == 0, stop=n == 5, skip_group_check=True)
                                        n += 1
                            last.then_inc(full_of(("c3", u + 1)), 1)
                        if 0 <= u < len(CONV):
                            b = take(("t3", u), (pt3_ready, u))
                            pe.wait_ge(p3_ready, due(p3_ready, it, u))
                            for jt in range(2):
                                for i2 in range(2):
                                    last = tp(b[:, (jt * 2 + i2) * P:(jt * 2 + i2 + 1) * P],
                                              E[:, u % ER, i2 * T + jt * P:i2 * T + (jt + 1) * P], ident[:])
                            last.then_inc(full_of(("t3", u)), 1)
                        if u >= 1:
                            bb, h = CONV[u - 1]
                            if h == 0:
                                zs = [take(("z3", bb, i2), (tok_ready, 7 * NT + 2 * bb + i2), ring=1) for i2 in range(2)]
                            pe.wait_ge(pt3_ready, due(pt3_ready, it, u - 1))
                            for i2 in range(2):
                                for jt in range(2):
                                    last = mm(zs[i2][:, h * (HD + 1):(h + 1) * (HD + 1)],
                                              PT[:, (u - 1) % PR, (jt * 2 + i2) * P:(jt * 2 + i2 + 1) * P],
                                              V3[:, 2 * bb + jt, h, :], start=jt == 0, stop=jt == 1)
                                if h == H - 1:
                                    last.then_inc(full_of(("z3", bb, i2)), 1)
                    to_features(7, xn)
                    for t in range(NT):
                        to_tokens(("p3", t), (x3_ready, t), W["L1_xattn_proj_W"])

                if STAGES >= 4:
                    to_features(8, xn)
                    pe.wait_ge(xr_ready, due(xr_ready, it, 0))
                    for m in range(KD):
                        to_columns(("kk", m), (ka_ready, m), W["L1_ffn_W_k"], m,
                                   lambda k: XR[:, 0, k, :].rearrange("p (b t) -> p b t", b=NB))
                    pe.wait_ge(xr_ready, due(xr_ready, it, 1))
                    for t in range(NT):
                        to_tokens(("r4", t), (sg_ready, t), W["L1_ffn_W_r"], src=lambda k: XR[:, 1, k, :])
                    pe.wait_ge(ka_ready, due(ka_ready, it, KD - 1))
                    for t in range(NT):
                        to_tokens(("v4", t), (xo_ready, t), W["L1_ffn_W_v"], src=lambda k: KA[:, k, :])

        @block.scalar
        def _(act):
            act.wait_ge(weights_in, 16 * len(loads))
            act.wait_ge(consts_set, 2)
            f, copy = nc.scalar.activation, nc.scalar.copy
            if STAGES >= 3:
                with act.Fori(0, STEPS) as it:
                    act.wait_ge(ehs_ready, due(ehs_ready, it, 0))
                    f(eh[0:C], ehs[0:C], ACT.Gelu).then_inc(eh_ready, 1)
                    act.wait_ge(hist_1, due(hist_1, it, 0))
                    f(h1[:, :], bank[4][:, 0:NB * C], ACT.Gelu, bias=W["ctxb1"][:, 0:1]).then_inc(h1_ready, 1)
                    act.wait_ge(aws_ready, due(aws_ready, it, 0))
                    f(aw[:], aw[:], ACT.Exp).then_inc(awe_ready, 1)
                it = 0
                act.wait_ge(kgs_ready, due(kgs_ready, it, 0))
                f(kg[:], kg[:], ACT.Gelu).then_inc(kg_ready, 1)
                act.wait_ge(kps_ready, due(kps_ready, it, 0))
                f(kp[:], kp[:], ACT.Exp).then_inc(kpe_ready, 1)

            with act.Fori(0, ITERS) as it:

                def features(n, l=None):
                    act.wait_ge(full_of(("fT", n, 0)), full_at(("fT", n, 0), it))
                    b = bank_of(("fT", n, 0))
                    src = b[:, :].rearrange("p (b t) -> p b t", b=NB)
                    if l is None:
                        ins = copy(F[:, 0, :, 1:T + 1], src)
                    else:
                        ins = f(F[:, 0, :, 1:T + 1], src, ACT.Identity, bias=W[f"b{l}"][:, 0:1], scale=W[f"g{l}"][:, 0:1])
                    ins.then_inc(feat_a, 1)

                def exponentials(u, n, width, scores, probs):
                    act.wait_ge(scores, due(scores, it, n))
                    f(E[:, u % ER, 0:width], E[:, u % ER, 0:width], ACT.Exp).then_inc(probs, 1)

                def turned(u, key, rows, probs_turned):
                    act.wait_ge(full_of(key), full_at(key, it))
                    copy(PT[0:rows, u % PR, :], bank_of(key)[0:rows, :]).then_inc(probs_turned, 1)

                features(0)
                for u in range(len(CROSS) + 1):
                    if u < len(CROSS):
                        exponentials(u, u, 4 * C, e1_ready, p1_ready)
                    if u >= 1:
                        turned(u - 1, ("t1", u - 1), C, pt1_ready)
                features(1)
                for l in L:
                    features(2 + 2 * l)

                    def turn_qk(t):
                        for i, (k, dst) in enumerate((("qT", QT2), ("kT", KT2))):
                            act.wait_ge(full_of((k, l, t)), full_at((k, l, t), it))
                            b = bank_of((k, l, t))
                            copy(dst[:, :, t * P:(t + 1) * P], b[:, :].rearrange("p (h t) -> p h t", h=4)).then_inc(qkT_ready, 1)

                    for t in range(NT):
                        for i, k in enumerate(("q2", "k2")):
                            act.wait_ge(full_of((k, l, t)), full_at((k, l, t), it))
                            b = bank_of((k, l, t))
                            if t >= 1:
                                act.wait_ge(ss_sum, due(ss_sum, it, l * 2 * NT + 2 * (t - 1) + i))
                            f(sq[:, i, :], b[:, :], ACT.Square).then_inc(sq_ready, 1)
                        act.wait_ge(full_of(("v2", l, t)), full_at(("v2", l, t), it))
                        b = bank_of(("v2", l, t))
                        copy(V2[:, t, :, 0:HD2], b[:, :].rearrange("p (h d) -> p h d", h=H2)).then_inc(v2_ready, 1)
                        if t >= 1:
                            turn_qk(t - 1)
                    turn_qk(NT - 1)
                    for u in range(len(LOCAL) + 1):
                        if u < len(LOCAL):
                            exponentials(u, l * len(LOCAL) + u, 512, e2_ready, p2_ready)
                        if u >= 1:
                            turned(u - 1, ("t2", l, u - 1), P, pt2_ready)
                    for t in range(NT):
                        act.wait_ge(full_of(("oT", l, t)), full_at(("oT", l, t), it))
                        b = bank_of(("oT", l, t))
                        copy(OT[:, :, t * P:(t + 1) * P], b[:, :].rearrange("p (k t) -> p k t", k=INNER // P)).then_inc(oT_ready, 1)
                    features(3 + 2 * l, l)
                    for j in range(HF):
                        act.wait_ge(full_of(("g", l, j)), full_at(("g", l, j), it))
                        b = bank_of(("g", l, j))
                        if j >= 2:
                            act.wait_ge(hh_ready, due(hh_ready, it, l * (HF + 1) + j - 2))
                        f(G[:, j % 2, :], b[:, :], ACT.Gelu, bias=W[f"b1{l}"][:, 2 * j:2 * j + 1]).then_inc(g_ready, 1)
                    act.wait_ge(full_of(("r", l)), full_at(("r", l), it))
                    b = bank_of(("r", l))
                    act.wait_ge(hh_ready, due(hh_ready, it, l * (HF + 1) + HF - 2))
                    f(G[0:HR, HF % 2, :], b[64:64 + HR, :], ACT.Gelu, bias=W[f"b1{l}"][64:64 + HR, 2 * HF:2 * HF + 1]).then_inc(g_ready, 1)
                if STAGES >= 3:
                    features(6)
                    for t in range(NT):
                        act.wait_ge(full_of(("v3", t)), full_at(("v3", t), it))
                        b = bank_of(("v3", t))
                        copy(V3[:, t, :, 0:HD], b[:, 0:D].rearrange("p (h d) -> p h d", h=H)).then_inc(v3_ready, 1)
                    for u in range(len(CONV) + 1):
                        if u < len(CONV):
                            exponentials(u, u, 512, e3_ready, p3_ready)
                        if u >= 1:
                            turned(u - 1, ("t3", u - 1), P, pt3_ready)
                    features(7)
                if STAGES >= 4:
                    features(8)
                    for t in range(NT):
                        act.wait_ge(full_of(("r4", t)), full_at(("r4", t), it))
                        b = bank_of(("r4", t))
                        if t >= 2:
                            act.wait_ge(xo_ready, due(xo_ready, it, t - 2))
                        f(sg[:, t % 2, :], b[:, 0:D], ACT.Sigmoid).then_inc(sg_ready, 1)

        @block.vector
        def _(dve):
            dve.wait_ge(weights_in, 16 * len(loads))
            dve.wait_ge(consts_set, 1)
            v = nc.vector
            tt, ts, stt = v.tensor_tensor, v.tensor_scalar, v.scalar_tensor_tensor
            ts(negm[:], W["mask_i"][:], 0.0, NEG, ALU.is_equal, ALU.mult)
            ts(far[:], W["far_u"][:].bitcast(U8), FAR, None, ALU.mult)
            ts(keepT[:], W["farT_u"][:].bitcast(U8), -1.0, 1.0, ALU.mult, ALU.add)
            for l in range(DEPTH):
                for hf in range(2):
                    for i, n in enumerate(("q", "k")):
                        sc = W[f"{n}s{l}"]
                        tt(rotl[:, l, hf, 2 * i, :], rot[:, hf, 2 * i, :], sc[:], ALU.mult)
                        for lo, hi in ((0, HD2 // 2), (HD2 // 2, 0)):
                            tt(rotl[:, l, hf, 2 * i + 1, lo:lo + HD2 // 2], rot[:, hf, 2 * i + 1, lo:lo + HD2 // 2],
                               sc[:, hi:hi + HD2 // 2], ALU.mult)
            for i, n in enumerate(("k", "r")):
                last = ts(omr[:, i, :], W[f"L1_ffn_mu_{n}"][:], -1.0, 1.0, ALU.mult, ALU.add)
            last.then_inc(consts_set, 1)
            dve.wait_ge(consts_set, 2)

            def normalised(s, dst, src, m, r, rows=P):
                return ts(dst, src, m, r, ALU.subtract, ALU.mult)

            if STAGES >= 3:
                with dve.Fori(0, STEPS) as it:
                    v.tensor_copy(one[0:1, 0:1], ident[0:1, 0:1]).then_inc(hist_go, 1)
                    dve.wait_ge(hist_h, due(hist_h, it, 0))
                    for bb in range(NB):
                        last = tt(ehs[0:C, bb, :], bank[bb][0:C, :], W["histb"][0:C], ALU.add)
                    last.then_inc(hist_dve, 1)
                    dve.wait_ge(hist_dve, own(hist_dve, it))
                    for bb in range(NB):
                        last = v.bn_stats(stats[0:C, bb, 0, :], ehs[0:C, bb, :])
                    last.then_inc(hist_dve, 1)
                    dve.wait_ge(hist_dve, own(hist_dve, it))
                    v.memset(fence[:], 0.0)
                    for bb in range(NB):
                        last = v.bn_aggr(mv[0:C, bb, :], stats[0:C, bb, 0, :])
                    last.then_inc(hist_dve, 1)
                    dve.wait_ge(hist_dve, own(hist_dve, it))
                    ts(rstd[0:C, 0:NB], mv[0:C, 0:NB, 1], EPS, None, ALU.add).then_inc(hist_var, 1)
                    dve.wait_ge(hist_rstd, due(hist_rstd, it, 0))
                    for bb in range(NB):
                        last = ts(ehs[0:C, bb, :], ehs[0:C, bb, :], mv[0:C, bb, 0:1], rstd[0:C, bb:bb + 1], ALU.subtract, ALU.mult)
                    last.then_inc(hist_dve, 1)
                    dve.wait_ge(hist_dve, own(hist_dve, it))
                    tt(ehs[0:C], ehs[0:C], wide(W["histg"][0:C], [C, NB, HIST], 1), ALU.mult).then_inc(hist_dve, 1)
                    dve.wait_ge(hist_dve, own(hist_dve, it))
                    tt(ehs[0:C], ehs[0:C], wide(W["histB"][0:C], [C, NB, HIST], 1), ALU.add).then_inc(ehs_ready, 1)
                    dve.wait_ge(hist_T, due(hist_T, it, 0))
                    for bb in range(NB):
                        last = v.tensor_copy(ehT[:, :, bb, :], bank[2 + bb][:, :].rearrange("p (c n) -> p c n", c=4)[:, :, 0:C])
                    last.then_inc(ehT_ready, 1)
                    dve.wait_ge(hist_2, due(hist_2, it, 0))
                    ts(aw[0:1].rearrange("p b n -> p (b n)"), bank[5][0:1, 0:NB * C], W["ctxb2"][0:1, 0:1], None, ALU.add).then_inc(hist_dve, 1)
                    dve.wait_ge(hist_dve, own(hist_dve, it))
                    v.tensor_reduce(am[0:1, :, 0], aw[0:1], AX_X, ALU.max).then_inc(hist_dve, 1)
                    dve.wait_ge(hist_dve, own(hist_dve, it))
                    tt(aw[0:1], aw[0:1], am[0:1, :, 0:1].broadcast_to([1, NB, C]), ALU.subtract).then_inc(aws_ready, 1)
                    dve.wait_ge(awe_ready, due(awe_ready, it, 0))
                    v.tensor_reduce(am[0:1, :, 1], aw[0:1], AX_X, ALU.add).then_inc(hist_dve, 1)
                    dve.wait_ge(hist_dve, own(hist_dve, it))
                    v.reciprocal(am[0:1, :, 2], am[0:1, :, 1]).then_inc(hist_dve, 1)
                    dve.wait_ge(hist_dve, own(hist_dve, it))
                    tt(aw[0:1], aw[0:1], am[0:1, :, 2:3].broadcast_to([1, NB, C]), ALU.mult).then_inc(aw_ready, 1)
                    dve.wait_ge(hist_w, due(hist_w, it, 0))
                    v.tensor_copy(awc[0:C, :], bank[6][0:C, 0:NB]).then_inc(awc_ready, 1)
                    dve.wait_ge(hist_c, due(hist_c, it, 0))
                    v.tensor_copy(cc[:, :, bass.ds(it * NB, NB)],
                                          bank[7][:, 0:4 * NB].rearrange("p (c b) -> p c b", b=NB)).then_inc(hist_dve, 1)
                    dve.wait_ge(hist_dve, own(hist_dve, it))
                it = 0
                v.tensor_copy(one[0:1, 0:1], ident[0:1, 0:1]).then_inc(cc_ready, 1)
                dve.wait_ge(kg_1, due(kg_1, it, 0))
                tt(kg[:], bank[0][0:B, 0:D], W["kgb1"][:], ALU.add).then_inc(kg_dve, 1)
                dve.wait_ge(kg_dve, own(kg_dve, it))
                v.bn_stats(stats[0:B, 0, 0, :], kg[:]).then_inc(kg_dve, 1)
                dve.wait_ge(kg_dve, own(kg_dve, it))
                v.bn_aggr(mv[0:B, 0, :], stats[0:B, 0, 0, :]).then_inc(kg_dve, 1)
                dve.wait_ge(kg_dve, own(kg_dve, it))
                ts(rstd[0:B, 0:1], mv[0:B, 0, 1:2], EPS, None, ALU.add).then_inc(kg_var, 1)
                dve.wait_ge(kg_rstd, due(kg_rstd, it, 0))
                ts(kg[:], kg[:], mv[0:B, 0, 0:1], rstd[0:B, 0:1], ALU.subtract, ALU.mult).then_inc(kg_dve, 1)
                dve.wait_ge(kg_dve, own(kg_dve, it))
                tt(kg[:], kg[:], W["kgg"][:], ALU.mult).then_inc(kg_dve, 1)
                dve.wait_ge(kg_dve, own(kg_dve, it))
                tt(kg[:], kg[:], W["kgB"][:], ALU.add).then_inc(kgs_ready, 1)
                dve.wait_ge(kg_T, due(kg_T, it, 0))
                v.tensor_copy(kgT[:], bank[1][:, 0:KD * B].rearrange("p (k b) -> p k b", k=KD)).then_inc(kgT_ready, 1)
                dve.wait_ge(kg_2, due(kg_2, it, 0))
                tt(kp[:].rearrange("b h n -> b (h n)"), bank[2][0:B, 0:H * 9], W["kgb2"][:], ALU.add).then_inc(kg_dve, 1)
                dve.wait_ge(kg_dve, own(kg_dve, it))
                v.tensor_reduce(km[:, 0, :], kp[:], AX_X, ALU.max).then_inc(kg_dve, 1)
                dve.wait_ge(kg_dve, own(kg_dve, it))
                tt(kp[:], kp[:], wide(km[:, 0, :], [B, H, 9], 2), ALU.subtract).then_inc(kps_ready, 1)
                dve.wait_ge(kpe_ready, due(kpe_ready, it, 0))
                v.tensor_reduce(km[:, 0, :], kp[:], AX_X, ALU.add).then_inc(kg_dve, 1)
                dve.wait_ge(kg_dve, own(kg_dve, it))
                v.reciprocal(km[:, 1, :], km[:, 0, :]).then_inc(kg_dve, 1)
                dve.wait_ge(kg_dve, own(kg_dve, it))
                tt(kp[:], kp[:], wide(km[:, 1, :], [B, H, 9], 2), ALU.mult).then_inc(kp_ready, 1)

            with dve.Fori(0, ITERS) as it:

                def statistics(first, second, t):
                    v.bn_stats(stats[:, t, 0, :], first)
                    return v.bn_stats(stats[:, t, 1, :], second)

                def scales(n, last):
                    last.then_inc(ln_stats, 1)
                    dve.wait_ge(ln_stats, own(ln_stats, it))
                    v.memset(fence[:], 0.0)
                    for t in range(NT):
                        last = v.bn_aggr(mv[:, t, :], stats[:, t].rearrange("p a b -> p (a b)"))
                    last.then_inc(ln_moments, 1)
                    dve.wait_ge(ln_moments, own(ln_moments, it))
                    ts(rstd[:], mv[:, :, 1], EPS, None, ALU.add).then_inc(var_ready, 1)
                    dve.wait_ge(rstd_ready, due(rstd_ready, it, n))

                def layernorm(n, src, dst, ready=tok_ready):
                    for t in range(NT):
                        last = statistics(src[:, t, 0:P], src[:, t, P:D], t)
                    scales(n, last)
                    for t in range(NT):
                        ts(dst[:, t, :], src[:, t, :], mv[:, t, 0:1], rstd[:, t:t + 1], ALU.subtract, ALU.mult).then_inc(ready, 1)

                def features(n, l=None):
                    dve.wait_ge(full_of(("fT", n, 1)), full_at(("fT", n, 1), it))
                    b = bank_of(("fT", n, 1))
                    src = b[:, :].rearrange("p (b t) -> p b t", b=NB)
                    if l is None:
                        ins = v.tensor_copy(F[:, 1, :, 1:T + 1], src)
                    else:
                        ins = ts(F[:, 1, :, 1:T + 1], src, W[f"g{l}"][:, 1:2], W[f"b{l}"][:, 1:2], ALU.mult, ALU.add)
                    ins.then_inc(feat_v, 1)

                def head_outputs(dst, src, heads, width, lo=0):
                    v.reciprocal(rz[:, lo:lo + heads], src[:, :, width]).then_inc(rz_ready, 1)
                    dve.wait_ge(rz_ready, own(rz_ready, it))
                    return tt(dst, src[:, :, 0:width], wide(rz[:, lo:lo + heads], [P, heads, width], 2), ALU.mult)

                def softmax_input(u, b, groups, width, mask, ready):
                    e = E[:, u % ER, 0:groups * width].rearrange("p (g n) -> p g n", g=groups)
                    m = mx[:, u % 2, 0:groups]
                    tt(e, b[:, 0:groups * width].rearrange("p (g n) -> p g n", g=groups), mask, ALU.add).then_inc(sm_masked, 1)
                    dve.wait_ge(sm_masked, own(sm_masked, it))
                    v.tensor_reduce(m, e, AX_X, ALU.max).then_inc(sm_max, 1)
                    dve.wait_ge(sm_max, own(sm_max, it))
                    tt(e, e, wide(m, [P, groups, width], 2), ALU.subtract).then_inc(ready, 1)

                dve.wait_ge(x_in, due(x_in, it, 0))
                layernorm(0, xin, xn)
                features(0)
                for m in range(KD):
                    dve.wait_ge(full_of(("q1", m)), full_at(("q1", m), it))
                    b = bank_of(("q1", m))
                    ts(QT[:, m, :], b[:, :], W["L0_xattn_bq"][:, m:m + 1], HD ** -0.5, ALU.add, ALU.mult).then_inc(qk1_ready, 1)
                dve.wait_ge(full_of(("k1",)), full_at(("k1",), it))
                b = bank_of(("k1",))
                for m in range(KD):
                    for par in range(PAR):
                        last = ts(KT1[:, m, :, par, :], b[:, m * 256:m * 256 + NB * C].rearrange("p (b n) -> p b n", b=NB),
                                  W["L0_xattn_bk"][:, m:m + 1], parity[:, par:par + 1], ALU.add, ALU.mult)
                last.then_inc(qk1_ready, 1)
                for bb in range(NB):
                    dve.wait_ge(full_of(("v1", bb)), full_at(("v1", bb), it))
                    b = bank_of(("v1", bb))
                    tt(V1[0:C, bb, :, 0:HD], b[0:C, 0:D].rearrange("p (h d) -> p h d", h=H),
                             W["L0_xattn_bv"][0:C].rearrange("p (h d) -> p h d", h=H), ALU.add).then_inc(qk1_ready, 1)
                for u in range(len(CROSS) + 2):
                    if u < len(CROSS):
                        dve.wait_ge(full_of(("s1", u)), full_at(("s1", u), it))
                        b = bank_of(("s1", u))
                        softmax_input(u, b, 4, C, wide(negm[:, CROSS[u][0] % 2, :], [P, 4, C], 1), e1_ready)
                    if u >= 5 and (u - 5) % 4 == 0:
                        t = (u - 5) // 4
                        dve.wait_ge(full_of(("z1", t)), full_at(("z1", t), it))
                        b = bank_of(("z1", t))
                        z = b[:, 0:H * (HD + 1)].rearrange("p (h d) -> p h d", h=H)
                        head_outputs(xn[:, t, :].rearrange("p (h d) -> p h d", h=H), z, H, HD).then_inc(tok_ready, 1)
                features(1)
                for t in range(NT):
                    dve.wait_ge(xb_ready, due(xb_ready, it, t))
                    dve.wait_ge(full_of(("o1", t)), full_at(("o1", t), it))
                    b = bank_of(("o1", t))
                    tt(x[:, t, :], x[:, t, :], b[:, 0:D], ALU.add).then_inc(x1_ready, 1)
                dve.wait_ge(x1_ready, due(x1_ready, it, NT - 1))
                dve.wait_ge(x_out, due(x_out, it, 0))
                if STAGES >= 2:
                    layernorm(1, x, y)
                for l in L:
                    features(2 + 2 * l)

                    def rotate(t, i):
                        n = l * 2 * NT + 2 * t + i
                        dve.wait_ge(full_of((("q2", "k2")[i], l, t)), full_at((("q2", "k2")[i], l, t), it))
                        b = bank_of((("q2", "k2")[i], l, t))
                        dve.wait_ge(sq_ready, due(sq_ready, it, n))
                        v.tensor_reduce(ss[:, i, :], sq[:, i, :].rearrange("p (h d) -> p h d", h=H2), AX_X, ALU.add).then_inc(ss_sum, 1)
                        dve.wait_ge(ss_sum, own(ss_sum, it))
                        ts(ss[:, i, :], ss[:, i, :], 1e-24, None, ALU.max).then_inc(ss_ready, 1)
                        dve.wait_ge(rr_ready, due(rr_ready, it, n))
                        q4 = qn[:, i, :].rearrange("p (h d) -> p h d", h=H2)
                        if n - l * 2 * NT >= 2:
                            dve.wait_ge(qb_ready, due(qb_ready, it, n - 2))
                        tt(q4, b[:, :].rearrange("p (h d) -> p h d", h=H2), wide(rr[:, i, :], [P, H2, HD2], 2), ALU.mult).then_inc(qn_ready, 1)
                        dve.wait_ge(qn_ready, own(qn_ready, it))
                        if t >= 1:
                            dve.wait_ge(full_of((("qT", "kT")[i], l, t - 1)), full_at((("qT", "kT")[i], l, t - 1), it))
                        q3 = qa[:, i, :].rearrange("p (h d) -> p h d", h=H2)
                        tt(q3, q4, wide(rotl[:, l, t % 2, 2 * i, :], [P, H2, HD2], 1), ALU.mult).then_inc(qa_ready, 1)
                        dve.wait_ge(qb_ready, due(qb_ready, it, n))
                        dve.wait_ge(qa_ready, due(qa_ready, it, n))
                        tt(qa[:, i, :], qa[:, i, :], qb[:, i, :], ALU.add).then_inc(qr_ready, 1)

                    for t in range(NT):
                        for i in range(2):
                            rotate(t, i)
                    for u in range(len(LOCAL) + 2):
                        if u < len(LOCAL):
                            t, g = LOCAL[u]
                            dve.wait_ge(full_of(("s2", l, u)), full_at(("s2", l, u), it))
                            b = bank_of(("s2", l, u))
                            if t % 2 == 0:
                                softmax_input(u, b, 4, P, wide(W["causal"][:, 1, :], [P, 4, P], 1), e2_ready)
                            else:
                                softmax_input(u, b, 2, 2 * P, wide(W["causal"][:].rearrange("p a n -> p (a n)"), [P, 2, 2 * P], 1), e2_ready)
                        if u >= 2 and LOCAL[u - 2][1] == len(local_groups(LOCAL[u - 2][0])) - 1:
                            t = LOCAL[u - 2][0]
                            for hf in range(2):
                                dve.wait_ge(full_of(("z2", l, t, hf)), full_at(("z2", l, t, hf), it))
                                b = bank_of(("z2", l, t, hf))
                                z = b[:, 0:4 * (HD2 + 1)].rearrange("p (h d) -> p h d", h=4)
                                last = head_outputs(O2[:, t, hf * 256:(hf + 1) * 256].rearrange("p (h d) -> p h d", h=4), z, 4, HD2, 4 * hf)
                            last.then_inc(o2_ready, 1)
                    for t in range(NT):
                        dve.wait_ge(full_of(("wo", l, t)), full_at(("wo", l, t), it))
                        b = bank_of(("wo", l, t))
                        tt(y[:, t, :], y[:, t, :], b[:, 0:D], ALU.add).then_inc(y_ready, 1)
                    dve.wait_ge(full_of(("sh", l)), full_at(("sh", l), it))
                    sh = bank_of(("sh", l))
                    for t in range(NT):
                        last = statistics(y[:, t, 0:P], sh[:, t * P:(t + 1) * P], t)
                    scales(2 + l, last)
                    for t in range(NT):
                        ts(xn[:, t, 0:P], y[:, t, 0:P], mv[:, t, 0:1], rstd[:, t:t + 1], ALU.subtract, ALU.mult)
                        ts(xn[:, t, P:D], sh[:, t * P:(t + 1) * P], mv[:, t, 0:1], rstd[:, t:t + 1], ALU.subtract, ALU.mult).then_inc(tok_ready, 1)
                    features(3 + 2 * l, l)
                    v.memset(HH[32:64, HF, :], 1.0).then_inc(ones_row, 1)
                    dve.wait_ge(ones_row, own(ones_row, it))
                    for j in range(HF + 1):
                        dve.wait_ge(full_of(("a", l, j) if j < HF else ("r", l)), full_at(("a", l, j) if j < HF else ("r", l), it))
                        b = bank_of(("a", l, j) if j < HF else ("r", l))
                        r = P if j < HF else HR
                        dve.wait_ge(g_ready, due(g_ready, it, l * (HF + 1) + j))
                        stt(HH[0:r, j, :], b[0:r, :], W[f"b1{l}"][0:r, 2 * j + (j < HF):2 * j + (j < HF) + 1], G[0:r, j % 2, :],
                                  ALU.add, ALU.mult).then_inc(hh_ready, 1)
                    for t in range(NT):
                        dve.wait_ge(full_of(("w2", l, t)), full_at(("w2", l, t), it))
                        b = bank_of(("w2", l, t))
                        tt(y[:, t, :], y[:, t, :], b[:, 0:D], ALU.add).then_inc(w2_read, 1)
                        if l < DEPTH - 1:
                            dve.wait_ge(w2_read, due(w2_read, it, l * NT + t))
                            v.tensor_copy(y[0:1, t, 0:1], y[0:1, t, 0:1]).then_inc(tok_ready, 1)
                    dve.wait_ge(w2_read, due(w2_read, it, l * NT + NT - 1))
                if STAGES >= 2:
                    tt(x[:], x[:], y[:], ALU.add).then_inc(x2_ready, 1)
                    dve.wait_ge(x2_ready, own(x2_ready, it))
                if STAGES >= 3:
                    layernorm(4, x, xn)
                    features(6)
                    for m in range(KD):
                        dve.wait_ge(full_of(("q3", m)), full_at(("q3", m), it))
                        b = bank_of(("q3", m))
                        ts(QT[:, m, :], b[:, :], HD ** -0.5, None, ALU.mult).then_inc(qk3_ready, 1)
                    for m in range(KD):
                        dve.wait_ge(full_of(("k3", m)), full_at(("k3", m), it))
                        b = bank_of(("k3", m))
                        for par in range(PAR):
                            last = ts(KT3[:, m, par, :], b[:, :], parity[:, par:par + 1], None, ALU.mult)
                        last.then_inc(qk3_ready, 1)
                    for edge in (0, T + 1):
                        v.memset(S0[:, :, :, edge:edge + 1], 0.0)
                    v.memset(V3[:, :, :, HD:HD + 1], 1.0).then_inc(ones3_ready, 1)
                    dve.wait_ge(kern_in, due(kern_in, it, 0))
                    for u in range(-2, len(CONV)):
                        if u + 2 < len(CONV):
                            bb, h = CONV[u + 2]
                            dve.wait_ge(full_of(("s3", u + 2)), full_at(("s3", u + 2), it))
                            b = bank_of(("s3", u + 2))
                            tt(S0[:, u % 2, :, 1:T + 1], b[:, :].rearrange("p (j i) -> p j i", j=2), keepT[:], ALU.mult).then_inc(s0_ready, 1)
                            for c in range(3):
                                for tap in range(3):
                                    k = kern[:, bb, h * 9 + tap * 3 + c:h * 9 + tap * 3 + c + 1]
                                    dst = band[:, u % 2, tap, :]
                                    if c == 0:
                                        last = ts(dst, diag[:, c, :], k, None, ALU.mult)
                                    else:
                                        last = stt(dst, diag[:, c, :], k, dst, ALU.mult, ALU.add)
                                if c < 2:
                                    last.then_inc(band_part, 1)
                                    dve.wait_ge(band_part, own(band_part, it))
                            last.then_inc(band_ready, 1)
                        if 0 <= u + 1 < len(CONV):
                            dve.wait_ge(full_of(("c3", u + 1)), full_at(("c3", u + 1), it))
                            b = bank_of(("c3", u + 1))
                            softmax_input(u + 1, b, 2, T, far[:], e3_ready)
                        if u >= 1 and (u - 1) % H == H - 1:
                            bb = (u - 1) // H
                            for i2 in range(2):
                                dve.wait_ge(full_of(("z3", bb, i2)), full_at(("z3", bb, i2), it))
                                b = bank_of(("z3", bb, i2))
                                z = b[:, 0:H * (HD + 1)].rearrange("p (h d) -> p h d", h=H)
                                head_outputs(xn[:, 2 * bb + i2, :].rearrange("p (h d) -> p h d", h=H), z, H, HD, H * i2).then_inc(tok_ready, 1)
                    bb = NB - 1
                    for i2 in range(2):
                        dve.wait_ge(full_of(("z3", bb, i2)), full_at(("z3", bb, i2), it))
                        b = bank_of(("z3", bb, i2))
                        z = b[:, 0:H * (HD + 1)].rearrange("p (h d) -> p h d", h=H)
                        head_outputs(xn[:, 2 * bb + i2, :].rearrange("p (h d) -> p h d", h=H), z, H, HD, H * i2).then_inc(tok_ready, 1)
                    features(7)
                    for t in range(NT):
                        dve.wait_ge(full_of(("p3", t)), full_at(("p3", t), it))
                        b = bank_of(("p3", t))
                        tt(x[:, t, :], x[:, t, :], b[:, 0:D], ALU.add).then_inc(x3_ready, 1)
                        dve.wait_ge(x3_ready, own(x3_ready, it))
                        last = tt(x[:, t, :], x[:, t, :], W["L1_xattn_proj_b"][:], ALU.add)
                    last.then_inc(x3_done, 1)
                    dve.wait_ge(x3_done, own(x3_done, it))
                if STAGES >= 4:
                    layernorm(5, x, xn)
                    features(8)
                    dve.wait_ge(feat_a, due(feat_a, it, 8))
                    dve.wait_ge(feat_v, due(feat_v, it, 8))
                    for i, n in enumerate(("k", "r")):
                        for k in range(KD):
                            last = ts(XR[:, i, k, :].rearrange("p (b t) -> p b t", b=NB), F[:, k, :, 0:T], omr[:, i, k:k + 1], None, ALU.mult)
                        last.then_inc(xr_part, 1)
                        dve.wait_ge(xr_part, own(xr_part, it))
                        for k in range(KD):
                            dst = XR[:, i, k, :].rearrange("p (b t) -> p b t", b=NB)
                            last = stt(dst, F[:, k, :, 1:T + 1], W[f"L1_ffn_mu_{n}"][:, k:k + 1], dst, ALU.mult, ALU.add)
                        last.then_inc(xr_ready, 1)
                    for m in range(KD):
                        dve.wait_ge(full_of(("kk", m)), full_at(("kk", m), it))
                        b = bank_of(("kk", m))
                        ts(KA[:, m, :], b[:, :], 0.0, None, ALU.max).then_inc(ka_part, 1)
                        dve.wait_ge(ka_part, own(ka_part, it))
                        tt(KA[:, m, :], KA[:, m, :], KA[:, m, :], ALU.mult).then_inc(ka_ready, 1)
                    for t in range(NT):
                        dve.wait_ge(sg_ready, due(sg_ready, it, t))
                        g = sg[:, t % 2, :]
                        dve.wait_ge(full_of(("v4", t)), full_at(("v4", t), it))
                        b = bank_of(("v4", t))
                        tt(g, g, b[:, 0:D], ALU.mult).then_inc(sg_part, 1)
                        dve.wait_ge(sg_part, own(sg_part, it))
                        tt(xo[:, t, :], x[:, t, :], g, ALU.add).then_inc(xo_ready, 1)
                else:
                    for t in range(NT):
                        v.tensor_copy(xo[:, t, :], x[:, t, :]).then_inc(xo_ready, 1)

        @block.gpsimd
        def _(pool):
            g = nc.gpsimd
            g.memset(half[:], -0.5)
            g.memset(F[:], 0.0)
            g.memset(V1[:], 1.0)
            g.memset(V2[:], 1.0)
            g.memset(one[:], 1.0).then_inc(consts_set, 1)
            pool.wait_ge(weights_in, 16 * len(loads))
            pool.wait_ge(consts_set, 2)
            if STAGES >= 3:
                with pool.Fori(0, STEPS) as it:
                    pool.wait_ge(hist_var, due(hist_var, it, 0))
                    g.tensor_tensor(rstd[0:C, 0:NB], rstd[0:C, 0:NB], half[0:C, 0:NB], ALU.pow).then_inc(hist_rstd, 1)
                it = 0
                pool.wait_ge(kg_var, due(kg_var, it, 0))
                g.tensor_tensor(rstd[0:B, 0:1], rstd[0:B, 0:1], half[0:B, 0:1], ALU.pow).then_inc(kg_rstd, 1)
            with pool.Fori(0, ITERS) as it:

                def scales(n):
                    pool.wait_ge(var_ready, due(var_ready, it, n))
                    g.tensor_tensor(rstd[:], rstd[:], half[:, 0:NT], ALU.pow).then_inc(rstd_ready, 1)

                scales(0)
                for t in range(NT):
                    g.tensor_tensor(x[:, t, :], xin[:, t, :], W["L0_xattn_bo"][:], ALU.add).then_inc(xb_ready, 1)
                if STAGES >= 2:
                    scales(1)
                for l in L:
                    for t in range(NT):
                        for i in range(2):
                            n = l * 2 * NT + 2 * t + i
                            pool.wait_ge(ss_ready, due(ss_ready, it, n))
                            g.tensor_tensor(rr[:, i, :], ss[:, i, :], half[:], ALU.pow).then_inc(rr_ready, 1)
                            pool.wait_ge(qn_ready, due(qn_ready, it, n))
                            if t >= 1:
                                pool.wait_ge(qr_ready, due(qr_ready, it, n - 2))
                            q4 = qn[:, i, :].rearrange("p (h d) -> p h d", h=H2)
                            b4 = qb[:, i, :].rearrange("p (h d) -> p h d", h=H2)
                            for lo, hi in ((0, HD2 // 2), (HD2 // 2, 0)):
                                last = g.tensor_tensor(b4[:, :, lo:lo + HD2 // 2], q4[:, :, hi:hi + HD2 // 2],
                                                       wide(rotl[:, l, t % 2, 2 * i + 1, lo:lo + HD2 // 2], [P, H2, HD2 // 2], 1), ALU.mult)
                            last.then_inc(qb_ready, 1)
                    scales(2 + l)
                if STAGES >= 3:
                    scales(4)
                if STAGES >= 4:
                    scales(5)

        @block.sync
        def _(sp):
            for dst, src in loads:
                sp.dma_start(dst[:], src).then_inc(weights_in, 16)
            if STAGES >= 3:
                with sp.Fori(0, STEPS) as it:
                    sp.wait_ge(hist_go, due(hist_go, it, 0))
                    sp.dma_start(ctxT[:], a["ctxT"][bass.ds(it, 1)].rearrange("o (k p) n -> p (o k) n", p=P)).then_inc(hist_in, 16)
                it = 0
                sp.wait_ge(kp_ready, due(kp_ready, it, 0))
                sp.dma_start(kern_d, kp[:].rearrange("b h n -> b (h n)")).then_inc(kern_out, 16)
                sp.wait_ge(kern_out, 16)
            sp.dma_start(spare[:], a["L1_xattn_ctx_b2"]).then_inc(x_out, 16)

            def load(step):
                sp.dma_start(xin[:], a["x"][bass.ds(step, 1)].rearrange("o (t p) n -> p (o t) n", p=P)).then_inc(x_in, 16)
                sp.dma_start(ctxT[:], a["ctxT"][bass.ds(step, 1)].rearrange("o (k p) n -> p (o k) n", p=P)).then_inc(ctx_in, 16)
                if STAGES >= 3:
                    sp.dma_start(kern[:], kern_d.rearrange("(s b) n -> s (b n)", b=NB)[bass.ds(step, 1)].rearrange(
                        "o n -> (o n)").partition_broadcast(P).rearrange("p (b n) -> p b n", b=NB)).then_inc(kern_in, 16)

            def store(it):
                sp.wait_ge(xo_ready, due(xo_ready, it, NT - 1))
                sp.dma_start(out[bass.ds(it, 1)].rearrange("o (t p) n -> p (o t) n", p=P), y[:]).then_inc(x_out, 16)

            load(0)
            if ITERS > 1:
                with sp.Fori(0, ITERS - 1) as it:
                    sp.wait_ge(tok_ready, due(tok_ready, it, NT - 1))
                    sp.wait_ge(xb_ready, due(xb_ready, it, NT - 1))
                    sp.wait_ge(full_of(("v1", NB - 1)), full_at(("v1", NB - 1), it))
                    if STAGES >= 3:
                        sp.wait_ge(band_ready, due(band_ready, it, len(CONV) - 1))
                    load(it + 1)
                    store(it)
            store(ITERS - 1)
            sp.wait_ge(x_out, 16 * (ITERS + 1))


def _constants():
    f = np.float32
    p = np.arange(P)
    ident = np.eye(P, dtype=f)
    shift = np.zeros((P, 2, P), f)
    shift[p[:-1], 0, p[:-1] + 1] = 1
    shift[P - 1, 1, 0] = 1
    diag = np.zeros((P, 3, GW), f)
    for c in range(3):
        diag[p, c, p + 2 - c] = 1
    causal = np.zeros((P, 2, P), f)
    causal[:, 0, :] = np.where(p[:, None] > p[None, :], FAR, 0)
    causal[:, 1, :] = np.where(p[:, None] < p[None, :], FAR, 0)
    parity = np.stack([(p // HD) % 2 == 0, (p // HD) % 2 == 1], 1).astype(f)
    half_idx = np.arange(0, HD2, 2, dtype=f)
    inv = (1.0 / 10000.0 ** (half_idx / HD2)).astype(f)
    t = np.arange(T, dtype=f)
    fr = t[:, None] * inv[None, :]
    fr = np.concatenate([fr, fr], -1)
    base = ((half_idx + 0.4 * HD2) / (1.4 * HD2)).astype(f)
    sc = base[None, :] ** ((t - T // 2) / f(64))[:, None]
    sc = np.concatenate([sc, sc], -1).astype(f)
    sign = np.where(np.arange(HD2) < HD2 // 2, -1, 1).astype(f)
    cos, sin = np.cos(fr), np.sin(fr) * sign
    rot = np.stack([cos * sc * 8, sin * sc * 8, cos / sc, sin / sc], 1).astype(f)
    rot = rot.reshape(2, P, 4, HD2).transpose(1, 0, 2, 3).copy()
    return {"ident": ident, "shift": shift, "diag": diag, "causal": causal, "parity": parity, "rot": rot}


def kernel(**inputs):
    import concourse.bacc as _bacc
    from concourse.bass_utils import run_bass_kernel_spmd as _run

    arrays = _constants()
    plain = {k: np.asarray(v) for k, v in inputs.items()}
    arrays["x"] = plain.pop("x").reshape(STEPS, NB * T, D)
    arrays["ctxT"] = plain.pop("ctx_1024").reshape(STEPS, NB * C, D).transpose(0, 2, 1)
    arrays["mask_1x1xSxS2_ik0"] = plain.pop("mask_1x1xSxS2_ik0").reshape(T, C)
    far = plain.pop("mask_SxS_bc0")
    arrays["far"], arrays["farT"] = (np.ascontiguousarray(m).view(np.int32) for m in (far, far.T))
    for name in ("L0_xattn_Wq", "L0_xattn_Wk", "L0_xattn_Wv", "L0_xattn_Wo", "L1_ffn_W_r", "L1_ffn_W_k", "L1_ffn_W_v"):
        arrays[name] = plain.pop(name).T
    w1, b1, w2, b2 = (plain.pop(f"L0_ffn_{n}") for n in ("w1", "b1", "w2", "b2"))
    w1p = np.zeros((DEPTH, D, (2 * HF + 1) * P), np.float32)
    b1p = np.zeros((DEPTH, (2 * HF + 1) * P), np.float32)
    for j in range(HF):
        w1p[:, :, 2 * j * P:(2 * j + 1) * P] = w1[:, :, HID + j * P:HID + (j + 1) * P]
        b1p[:, 2 * j * P:(2 * j + 1) * P] = b1[:, HID + j * P:HID + (j + 1) * P]
        w1p[:, :, (2 * j + 1) * P:(2 * j + 2) * P] = w1[:, :, j * P:(j + 1) * P]
        b1p[:, (2 * j + 1) * P:(2 * j + 2) * P] = b1[:, j * P:(j + 1) * P]
    lo = 2 * HF * P
    w1p[:, :, lo:lo + HR], w1p[:, :, lo + 64:lo + 64 + HR] = w1[:, :, HF * P:HID], w1[:, :, HID + HF * P:]
    b1p[:, lo:lo + HR], b1p[:, lo + 64:lo + 64 + HR] = b1[:, HF * P:HID], b1[:, HID + HF * P:]
    w2p = np.zeros((DEPTH, (HF + 1) * P, D), np.float32)
    w2p[:, :HID] = w2
    w2p[:, HID] = b2
    arrays |= {"w1p": w1p, "w2p": w2p}
    for name in ("L0_ffn_ln_g", "L0_ffn_ln_b", "L0_xattn_bq", "L0_xattn_bk", "L1_ffn_mu_r", "L1_ffn_mu_k", "L1_xattn_ctx_b1"):
        plain[name] = np.swapaxes(plain[name].reshape(*plain[name].shape[:-1], -1, P), -1, -2)
    arrays["b1p"] = np.swapaxes(b1p.reshape(DEPTH, -1, P), -1, -2)
    plain["L1_xattn_ctx_b2"] = plain["L1_xattn_ctx_b2"].reshape(1, 1)
    arrays |= plain
    arrays = {k: np.ascontiguousarray(v) for k, v in arrays.items()}

    nc = _bacc.Bacc("TRN2", target_bir_lowering=False, num_devices=1)
    aps = {n: nc.dram_tensor(f"in_{n}", v.shape, mybir.dt.from_np(v.dtype), kind="ExternalInput").ap() for n, v in arrays.items()}
    out = nc.dram_tensor("out_0", (STEPS, NB * T, D), F32, kind="ExternalOutput").ap()
    bass_cross_local_conv_mix_kernel(nc, aps, out)
    r = _run(nc, [{f"in_{k}": v for k, v in arrays.items()}], core_ids=[0])
    return r.results[0]["out_0"].reshape(B, T, D)
```

```python
from contextlib import ExitStack

import numpy as np

import concourse.bass as bass
from concourse import mybir

F32 = mybir.dt.float32
U8 = mybir.dt.uint8
I32 = mybir.dt.int32
ALU = mybir.AluOpType
ACT = mybir.ActivationFunctionType
AX_X = mybir.AxisListType.X

P = 128
B, T, D = 32, 256, 256
KD = D // P
C = 77
H, HD = 16, 16
H2, HD2 = 8, 64
INNER = H2 * HD2
DEPTH = 2
HID = 682
HF = HID // P
HR = HID - HF * P
HIST = 512
NB = 2
STEPS = B // NB
HB = 4
NT = NB * T // P
HK = P // HD
PAR = 2
GW = P + 2
EPS = 1e-5
NEG = -1e9
FAR = -1e30
ER, PR = 4, 3
SR = 3
RING = 6

ITERS = STEPS
LAG1, LAG2 = 3, 2


def local_groups(t):
    if t % 2 == 0:
        return [(par, [par, par + 2, par + 4, par + 6], [t]) for par in range(2)]
    return [(par, [par + 4 * hf, par + 4 * hf + 2], [t - 1, t]) for hf in range(2) for par in range(2)]


LOCAL = [(t, g) for t in range(NT) for g in range(len(local_groups(t)))]
CROSS = [(t, r) for t in range(NT) for r in range(4)]
CONV = [(bb, h) for bb in range(NB) for h in range(H)]


def bass_cross_local_conv_mix_kernel(nc, a, out):
    with ExitStack() as ctx:
        def sb(name, shape, dt=F32):
            return ctx.enter_context(nc.sbuf_tensor(name, shape, dt))

        def sem(name):
            return ctx.enter_context(nc.semaphore(name))

        def carve(whole, lo, shape):
            n = int(np.prod(shape[1:]))
            ap = whole[0:shape[0], lo:lo + n]
            names = "abcd"[:len(shape) - 1]
            sizes = dict(zip(names, shape[1:]))
            return ap if len(shape) == 2 else ap.rearrange(f"p ({' '.join(names)}) -> p {' '.join(names)}", **sizes)

        qk_cols = sb("qk_cols", [P, 2 * 4 * NT * P + P])
        e_cols = sb("e_cols", [P, (ER + PR) * 512])
        o_cols = sb("o_cols", [P, 2 * NT * INNER])
        h_cols = sb("h_cols", [P, (2 + HF + 1) * NT * P])

        bank = [ctx.enter_context(nc.psum_tensor(f"bank{b}", [P, 512], F32)) for b in range(8)]

        W = {}
        first_loads, loads = [], []

        def weight(name, shape, src, dt=F32, at=None, first=False):
            W[name] = sb("w_" + name, shape, dt) if at is None else carve(*at, shape)
            (first_loads if first else loads).append((W[name], src))
            return W[name]

        def kmaj(ap):
            return ap.rearrange("(k p) n -> p k n", p=P)

        def column(ap, n):
            return ap.rearrange("(k p) -> p k", p=P) if n * P == ap.shape[0] else ap

        ident = weight("ident", [P, P], a["ident"], first=True)
        shiftm = weight("shift", [P, 2, P], a["shift"])
        diag = weight("diag", [P, 3, GW], a["diag"])
        causal = weight("causal", [P, 2, P], a["causal"])
        parity = weight("parity", [P, PAR], a["parity"])
        weight("head_rows", [P, HK], a["head_rows"])
        weight("upper", [P, 2], a["upper"])
        rot = weight("rot", [P, 2, 4, HD2], a["rot"])
        for name in ("L0_xattn_Wq", "L0_xattn_Wk", "L0_xattn_Wv", "L0_xattn_Wo", "L1_xattn_Wq", "L1_xattn_Wk",
                     "L1_xattn_Wv", "L1_xattn_proj_W", "L1_ffn_W_r", "L1_ffn_W_k", "L1_ffn_W_v"):
            weight(name, [P, KD, D], kmaj(a[name]))
        for l in range(DEPTH):
            weight(f"qkv{l}", [P, KD, 3 * INNER], kmaj(a["L0_ffn_wqkv"][l]))
            weight(f"wo{l}", [P, INNER // P, D], kmaj(a["L0_ffn_wo"][l]))
            weight(f"w1{l}", [P, KD, 2 * HF * P + P], kmaj(a["w1p"][l]))
            w2 = weight(f"w2{l}", [P, HF + 1, D], kmaj(a["w2p"][l]))
            weight(f"g{l}", [P, KD], a["L0_ffn_ln_g"][l])
            weight(f"b{l}", [P, KD], a["L0_ffn_ln_b"][l])
            weight(f"b1{l}", [P, 2 * HF + 1], a["b1p"][l])
            for n in ("q", "k"):
                weight(f"{n}s{l}", [P, HD2], a[f"L0_ffn_{n}_scale"][l].partition_broadcast(P))
        for name in ("L0_xattn_bq", "L0_xattn_bk", "L1_ffn_mu_r", "L1_ffn_mu_k"):
            weight(name, [P, KD], a[name])
        for name in ("L0_xattn_bv", "L0_xattn_bo", "L1_xattn_proj_b"):
            weight(name, [P, D], a[name].partition_broadcast(P))
        mask_i = weight("mask_i", [P, 2, C], a["mask_1x1xSxS2_ik0"].rearrange("(k p) n -> p k n", p=P), I32)
        weight("far_u", [P, 2, T // 4], a["far"].rearrange("(k p) n -> p k n", p=P), I32)
        weight("farT_u", [P, 2, T // 4], a["farT"].rearrange("(k p) n -> p k n", p=P), I32)
        weight("histW", [P, KD, HIST], kmaj(a["L1_xattn_hist_W"]), at=(e_cols, 0), first=True)
        weight("histb", [P, HIST], a["L1_xattn_hist_b"].partition_broadcast(P), at=(e_cols, 1024), first=True)
        weight("histg", [P, HIST], a["L1_xattn_hist_ln_g"].partition_broadcast(P), at=(e_cols, 1536), first=True)
        weight("histB", [P, HIST], a["L1_xattn_hist_ln_b"].partition_broadcast(P), at=(e_cols, 2048), first=True)
        weight("ctxW1", [P, HIST // P, P], kmaj(a["L1_xattn_ctx_W1"]), at=(qk_cols, 0), first=True)
        weight("ctxb1", [P, 1], a["L1_xattn_ctx_b1"], first=True)
        weight("ctxW2", [P, 1], a["L1_xattn_ctx_W2"], first=True)
        weight("ctxb2", [1, 1], a["L1_xattn_ctx_b2"], first=True)
        weight("kgW1", [P, HIST // P, D], kmaj(a["L1_xattn_kg_W1"]), at=(qk_cols, 512))
        weight("kgW2", [P, KD, H * 9], kmaj(a["L1_xattn_kg_W2"]), at=(qk_cols, 1536))
        weight("kgb1", [B, D], a["L1_xattn_kg_b1"].partition_broadcast(B), at=(qk_cols, 1824))
        weight("kgg", [B, D], a["L1_xattn_kg_ln_g"].partition_broadcast(B), at=(qk_cols, 2080))
        weight("kgB", [B, D], a["L1_xattn_kg_ln_b"].partition_broadcast(B), at=(qk_cols, 2336))
        weight("kgb2", [B, H * 9], a["L1_xattn_kg_b2"].partition_broadcast(B), at=(qk_cols, 2592))

        negm = sb("negm", [P, 2, C])
        far = sb("far_m", [P, 2, T])
        keepT = sb("keepT", [P, 2, T])
        rotl = sb("rotl", [P, DEPTH, 2, 4, HD2])
        omr = sb("omr", [P, 2, KD])
        half = sb("half", [P, H2])

        xin = sb("xin", [P, NT, D])
        x = sb("x", [P, NT, D])
        y = sb("y", [P, NT, D])
        xo = y
        xn = sb("xn", [P, NT, D])
        ctxT = sb("ctxT", [P, KD, NB * C])
        F = sb("F", [P, KD, NB, T + 1])
        QT = carve(h_cols, 2900, [P, KD, NB * T])
        KT1 = carve(o_cols, 2 * NT * P, [P, KD, NB, HK, C])
        V1 = carve(qk_cols, 0, [P, NB * KD * HK * P + P])
        E = carve(e_cols, 0, [P, ER, 512])
        PT = carve(e_cols, ER * 512, [P, PR, 512])
        stats = sb("stats", [P, NT, 2, 6])
        mv = sb("mv", [P, NT, 2])
        rstd = sb("rstd", [P, NT])
        mx = sb("mx", [P, ER, 4])
        sums = sb("sums", [P, ER, 4])
        rsums = sb("rsums", [P, ER, 4])
        rz = sb("rz", [P, 2 * H])
        sq = carve(h_cols, 0, [P, 2, INNER])
        ss = sb("ss", [P, 2, H2])
        rr = sb("rr", [P, 2, H2])
        qn = carve(h_cols, 2 * INNER, [P, 2, INNER])
        qa = carve(h_cols, 4 * INNER, [P, 2, INNER])
        qb = carve(h_cols, 6 * INNER, [P, 2, INNER])
        QT2 = carve(qk_cols, 0, [P, 4, NT * P])
        KT2 = [carve(qk_cols, 4 * NT * P, [P, 4, NT * P]), carve(o_cols, NT * INNER, [P, 4, NT * P])]
        V2 = sb("V2", [P, NT, H2, HD2 + 1])
        O2 = carve(o_cols, 0, [P, NT, INNER])
        OT = carve(o_cols, NT * INNER, [P, INNER // P, NT * P])
        G = carve(h_cols, 0, [P, 2, NT * P])
        HH = carve(h_cols, 2 * NT * P, [P, HF + 1, NT * P])
        KT3 = carve(qk_cols, 0, [P, KD, PAR, NB * T])
        V3 = carve(h_cols, 1812, [P, NT, H, HD + 1])
        S0 = carve(h_cols, 0, [P, SR, 2, T + 2])
        band = carve(qk_cols, 4 * NT * P, [P, SR, 3, GW])
        diag_k = carve(qk_cols, 4 * NT * P + SR * 3 * GW, [P, 2, 3, GW])
        kern = sb("kern", [P, NB, H * 9])
        XR = carve(qk_cols, 4 * NT * P, [P, 2, KD, NB * T])
        KA = carve(o_cols, 0, [P, KD, NB * T])
        sg = carve(h_cols, 0, [P, 2, D])
        kern_d = nc.dram_tensor("kernels_of_all", [B, H * 9], F32).ap()

        eh = carve(o_cols, 0, [P, HB, HIST])
        ehs = carve(o_cols, HB * HIST, [P, HB, HIST])
        ehT = carve(h_cols, 0, [P, HIST // P, HB, C])
        h1 = carve(h_cols, HIST // P * HB * C, [P, HB * C])
        hctx = carve(h_cols, (HIST // P + 1) * HB * C, [P, KD, HB // NB, NB * C])
        aw = sb("aw", [1, HB, C])
        awc = sb("awc", [P, HB])
        am = sb("am", [1, HB, 3])
        cc = sb("cc", [P, HIST // P, B])
        one = sb("one", [1, 1])
        spare = sb("spare", [1, 1])
        spare_v = sb("spare_v", [1, 1])
        fence = sb("fence", [1, 1])
        pool_fence = sb("pool_fence", [1, 1])
        kg = sb("kg", [B, D])
        kgT = sb("kgT", [P, KD, B])
        kp = sb("kp", [B, H, 9])
        km = sb("km", [B, 2, H])

        per_step, given = {}, {}

        def signal(name, count=1, by=1):
            s = sem(name)
            per_step[s], given[s] = (count, by), 0
            return s

        def due(s, it, n):
            count, by = per_step[s]
            return (it * count + n + 1) * by

        def own(s, it):
            given[s] += 1
            return due(s, it, given[s] - 1)

        place, fills = {}, [0] * 8
        bank_full = [sem(f"bank_full{b}") for b in range(8)]

        def full_of(key):
            return bank_full[place[key][0]]

        def full_at(key, it):
            b, n = place[key]
            return it * fills[b] + n + 1

        def bank_of(key):
            return bank[place[key][0]]

        LN = 6
        NF = 9
        first_in, weights_in, consts_set, kern_out = sem("first_in"), sem("weights_in"), sem("consts_set"), sem("kern_out")
        x_in, ctx_in, kern_in = signal("x_in", 1, 16), signal("ctx_in", 1, 16), signal("kern_in", 1, 16)
        x_out = signal("x_out", 1, 16)
        xo_ready = signal("xo_ready", NT)
        hist_in = signal("hist_in", HB // NB, 16)
        hist_go = signal("hist_go")
        hist_h, hist_T, hist_1 = signal("hist_h"), signal("hist_T"), signal("hist_1")
        hist_2, hist_w, hist_c = signal("hist_2"), signal("hist_w"), signal("hist_c")
        hist_dve = signal("hist_dve", 9)
        hist_var, hist_rstd = signal("hist_var"), signal("hist_rstd")
        ehs_ready, eh_ready, ehT_ready, h1_ready = signal("ehs_ready"), signal("eh_ready"), signal("ehT_ready"), signal("h1_ready")
        aws_ready, awe_ready, aw_ready, awc_ready = signal("aws_ready"), signal("awe_ready"), signal("aw_ready"), signal("awc_ready")
        cc_ready = signal("cc_ready")
        kg_1, kg_T, kg_2, kg_dve = signal("kg_1"), signal("kg_T"), signal("kg_2"), signal("kg_dve")
        kg_var, kg_rstd = signal("kg_var"), signal("kg_rstd")
        kgs_ready, kg_ready, kgT_ready = signal("kgs_ready"), signal("kg_ready"), signal("kgT_ready")
        kps_ready, kpe_ready, kp_ready = signal("kps_ready"), signal("kpe_ready"), signal("kp_ready")
        ln_stats, ln_moments = signal("ln_stats", LN), signal("ln_moments", LN)
        var_ready, rstd_ready = signal("var_ready", LN), signal("rstd_ready", LN)
        tok_ready = signal("tok_ready", (NF - 1) * NT)

        def tok_at(n, t):
            return (n - (n > 0)) * NT + t

        feat_a, feat_v = signal("feat_a", NF), signal("feat_v", NF)
        NSM = len(CROSS) + DEPTH * len(LOCAL) + len(CONV)
        sm_masked = signal("sm_masked", NSM)
        rz_ready = signal("rz_ready", DEPTH * NT * 2 + NT)
        e1_ready, p1_ready, pt1_ready = signal("e1_ready", len(CROSS)), signal("p1_ready", len(CROSS)), signal("pt1_ready", len(CROSS))
        e2_ready, p2_ready, pt2_ready = signal("e2_ready", DEPTH * len(LOCAL)), signal("p2_ready", DEPTH * len(LOCAL)), signal("pt2_ready", DEPTH * len(LOCAL))
        e3_ready, p3_ready, pt3_ready = signal("e3_ready", len(CONV)), signal("p3_ready", len(CONV)), signal("pt3_ready", len(CONV))
        rs1_ready = signal("rs1_ready", len(CROSS))
        pn1_ready = signal("pn1_ready", len(CROSS))
        v1_zero = signal("v1_zero")
        qk1_ready = signal("qk1_ready", KD + 1 + NB)
        xb_ready = signal("xb_ready", NT)
        x1_ready = signal("x1_ready", NT)
        sq_ready = signal("sq_ready", DEPTH * NT * 2)
        ss_sum, ss_ready = signal("ss_sum", DEPTH * NT * 2), signal("ss_ready", DEPTH * NT * 2)
        rr_ready = signal("rr_ready", DEPTH * NT * 2)
        qn_ready, qa_ready = signal("qn_ready", DEPTH * NT * 2), signal("qa_ready", DEPTH * NT * 2)
        qb_ready = signal("qb_ready", DEPTH * NT * 2)
        qr_ready = signal("qr_ready", DEPTH * NT * 2)
        qkT_ready, v2_ready = signal("qkT_ready", DEPTH * NT * 2), signal("v2_ready", DEPTH * NT)
        o2_ready, oT_ready = signal("o2_ready", DEPTH * NT), signal("oT_ready", DEPTH * NT)
        y_ready, w2_read = signal("y_ready", DEPTH * NT), signal("w2_read", DEPTH * NT)
        ones_row = signal("ones_row", DEPTH)
        g_ready, hh_ready = signal("g_ready", DEPTH * (HF + 1)), signal("hh_ready", DEPTH * (HF + 1))
        x2_ready = signal("x2_ready")
        qk3_ready, v3_ready, ones3_ready = signal("qk3_ready", 2 * KD), signal("v3_ready", NT), signal("ones3_ready")
        s0_ready = signal("s0_ready", len(CONV))
        band_part, band_ready = signal("band_part", 2 * len(CONV)), signal("band_ready", len(CONV))
        x3_ready, x3_done = signal("x3_ready", NT), signal("x3_done")
        xr_part, xr_ready = signal("xr_part", 2), signal("xr_ready", 2)
        ka_part, ka_ready = signal("ka_part", KD), signal("ka_ready", KD)
        sg_ready, sg_part = signal("sg_ready", NT), signal("sg_part", NT)

        def tile_cols(t, shift=0):
            return slice((t % 2) * P + 1 - shift, (t % 2) * P + P + 1 - shift)

        def wide(ap, shape, axis):
            return ap.unsqueeze(axis).broadcast_to(shape)

        L = range(DEPTH)
        block = ctx.enter_context(nc.Block())

        @block.tensor
        def _(pe):
            pe.wait_ge(first_in, 16 * len(first_loads))
            pe.wait_ge(consts_set, 1)
            mm = nc.tensor.matmul
            tp = nc.tensor.transpose

            with pe.Fori(0, B // HB) as it:
                pe.wait_ge(hist_in, due(hist_in, it, HB // NB - 1))
                pe.wait_ge(hist_go, due(hist_go, it, 0))
                for bb in range(HB):
                    for k in range(KD):
                        last = mm(bank[bb][0:C, :], hctx[:, k, bb // NB, (bb % NB) * C:(bb % NB + 1) * C], W["histW"][:, k, :],
                                  start=k == 0, stop=k == KD - 1)
                last.then_inc(hist_h, 1)
                pe.wait_ge(eh_ready, due(eh_ready, it, 0))
                for bb in range(HB):
                    for c in range(HIST // P):
                        last = tp(bank[HB + bb][:, c * P:c * P + C], eh[0:C, bb, c * P:(c + 1) * P], ident[0:C, 0:C])
                last.then_inc(hist_T, 1)
                pe.wait_ge(ehT_ready, due(ehT_ready, it, 0))
                for c in range(HIST // P):
                    last = mm(bank[0][:, 0:HB * C], W["ctxW1"][:, c, :], ehT[:, c, :, :].rearrange("p b n -> p (b n)"),
                              start=c == 0, stop=c == HIST // P - 1)
                last.then_inc(hist_1, 1)
                pe.wait_ge(h1_ready, due(h1_ready, it, 0))
                mm(bank[1][0:1, 0:HB * C], W["ctxW2"][:, 0:1], h1[:, :], start=True, stop=True).then_inc(hist_2, 1)
                pe.wait_ge(aw_ready, due(aw_ready, it, 0))
                for bb in range(HB):
                    last = mm(bank[2][0:C, bb:bb + 1], aw[0:1, bb, :], one[0:1, 0:1], start=True, stop=True)
                last.then_inc(hist_w, 1)
                pe.wait_ge(awc_ready, due(awc_ready, it, 0))
                for c in range(HIST // P):
                    for bb in range(HB):
                        last = mm(bank[3][:, c * HB + bb:c * HB + bb + 1], eh[0:C, bb, c * P:(c + 1) * P],
                                  awc[0:C, bb:bb + 1], start=True, stop=True)
                last.then_inc(hist_c, 1)
            pe.wait_ge(weights_in, 16 * len(loads))
            pe.wait_ge(consts_set, 2)
            it = 0
            pe.wait_ge(cc_ready, due(cc_ready, it, 0))
            for c in range(HIST // P):
                last = mm(bank[0][0:B, 0:D], cc[:, c, :], W["kgW1"][:, c, :], start=c == 0, stop=c == HIST // P - 1)
            last.then_inc(kg_1, 1)
            pe.wait_ge(kg_ready, due(kg_ready, it, 0))
            for k in range(KD):
                last = tp(bank[1][:, k * B:(k + 1) * B], kg[:, k * P:(k + 1) * P], ident[0:B, 0:B])
            last.then_inc(kg_T, 1)
            pe.wait_ge(kgT_ready, due(kgT_ready, it, 0))
            for k in range(KD):
                last = mm(bank[2][0:B, 0:H * 9], kgT[:, k, :], W["kgW2"][:, k, :], start=k == 0, stop=k == KD - 1)
            last.then_inc(kg_2, 1)
            pe.wait_ge(kp_ready, due(kp_ready, it, 0))

            with pe.Fori(0, ITERS) as it:
                turn, readers = [0, 0], {}

                def take(key, read, ring=0):
                    b = turn[0] % RING if ring == 0 else RING + turn[1] % (8 - RING)
                    turn[ring] += 1
                    if b in readers:
                        pe.wait_ge(readers[b][0], due(readers[b][0], it, readers[b][1]))
                    readers[b] = read
                    place[key] = (b, fills[b])
                    fills[b] += 1
                    return bank[b]

                def seq(m, shift=0):
                    return F[:, m, :, 1 - shift:T + 1 - shift]

                def to_features(n, src):
                    pe.wait_ge(tok_ready, due(tok_ready, it, tok_at(n, 0)))
                    for m in range(KD):
                        b = take(("fT", n, m), ((feat_a, feat_v)[m], n))
                        for t in range(NT):
                            if m == 0 and t:
                                pe.wait_ge(tok_ready, due(tok_ready, it, tok_at(n, t)))
                            last = tp(b[:, t * P:(t + 1) * P], src[:, t, m * P:(m + 1) * P], ident[:])
                        last.then_inc(full_of(("fT", n, m)), 1)
                    pe.wait_ge(feat_a, due(feat_a, it, n))
                    pe.wait_ge(feat_v, due(feat_v, it, n))

                def to_tokens(key, reader, w, n=D, shift=False, src=None, col=0):
                    t = key[-1]
                    b = take(key, reader)
                    for k in range(KD):
                        if src is None:
                            lhs = F[:, k, t // 2, tile_cols(t, 1 if shift and k == 1 else 0)]
                        else:
                            lhs = src(k)[:, t * P:(t + 1) * P]
                        last = mm(b[:, 0:n], lhs, w[:, k, col:col + n], start=k == 0, stop=k == KD - 1)
                    last.then_inc(full_of(key), 1)

                def to_columns(key, reader, w, m, rhs):
                    b = take(key, reader)
                    for k in range(KD):
                        last = mm(b[:, :].rearrange("p (b t) -> p b t", b=NB), w[:, k, m * P:(m + 1) * P], rhs(k),
                                  start=k == 0, stop=k == KD - 1)
                    last.then_inc(full_of(key), 1)

                to_features(0, xn)
                for m in range(KD):
                    to_columns(("q1", m), (qk1_ready, m), W["L0_xattn_Wq"], m, seq)
                pe.wait_ge(ctx_in, due(ctx_in, it, 0))
                b = take(("k1",), (qk1_ready, KD))
                for m in range(KD):
                    for k in range(KD):
                        last = mm(b[:, m * 256:m * 256 + NB * C], W["L0_xattn_Wk"][:, k, m * P:(m + 1) * P], ctxT[:, k, :],
                                  start=k == 0, stop=k == KD - 1)
                last.then_inc(full_of(("k1",)), 1)
                for bb in range(NB):
                    b = take(("v1", bb), (qk1_ready, KD + 1 + bb))
                    for k in range(KD):
                        last = mm(b[0:C, 0:D], ctxT[:, k, bb * C:(bb + 1) * C], W["L0_xattn_Wv"][:, k, :],
                                  start=k == 0, stop=k == KD - 1)
                    last.then_inc(full_of(("v1", bb)), 1)
                pe.wait_ge(qk1_ready, due(qk1_ready, it, KD + NB))
                for u in range(-LAG1, len(CROSS) + 1):
                    if u + LAG1 < len(CROSS):
                        t, r = CROSS[u + LAG1]
                        b = take(("s1", u + LAG1), (e1_ready, u + LAG1))
                        m, lo = 4 * r // HK, 4 * r % HK
                        mm(b[:, 0:4 * C], QT[:, m, t * P:(t + 1) * P], KT1[:, m, t // 2, lo:lo + 4, :].rearrange("p a n -> p (a n)"),
                           start=True, stop=True).then_inc(full_of(("s1", u + LAG1)), 1)
                    if 0 <= u < len(CROSS):
                        b = take(("t1", u), (pt1_ready, u))
                        pe.wait_ge(pn1_ready, due(pn1_ready, it, u))
                        for i in range(4):
                            last = tp(b[0:C, i * P:(i + 1) * P], E[:, u % ER, i * C:(i + 1) * C], ident[:])
                        last.then_inc(full_of(("t1", u)), 1)
                    if u >= 1:
                        t, r = CROSS[u - 1]
                        m = 4 * r // HK
                        if u == 1:
                            z = [take(("fT", 1, k), ((feat_a, feat_v)[k], 1), ring=1) for k in range(KD)]
                        pe.wait_ge(pt1_ready, due(pt1_ready, it, u - 1))
                        for i in range(4):
                            h = 4 * r + i
                            col = ((t // 2) * H + h) * P
                            last = mm(z[m][:, t * P:(t + 1) * P], V1[0:C, col:col + P], PT[0:C, (u - 1) % PR, i * P:(i + 1) * P],
                                      start=h % HK == 0, stop=h % HK == HK - 1)
                        if t == NT - 1 and h % HK == HK - 1:
                            last.then_inc(full_of(("fT", 1, m)), 1)
                pe.wait_ge(feat_a, due(feat_a, it, 1))
                pe.wait_ge(feat_v, due(feat_v, it, 1))
                for t in range(NT):
                    to_tokens(("o1", t), (x1_ready, t), W["L0_xattn_Wo"])

                for l in L:
                    to_features(2 + 2 * l, y)

                    def turn_qk(t):
                        for i, k in enumerate(("qT", "kT")):
                            n = l * 2 * NT + 2 * t + i
                            pe.wait_ge(qr_ready, due(qr_ready, it, n))
                            b = take((k, l, t), (qkT_ready, n), ring=1)
                            for hp in range(4):
                                last = tp(b[:, hp * P:(hp + 1) * P], qa[:, i, hp * P:(hp + 1) * P], ident[:])
                            last.then_inc(full_of((k, l, t)), 1)

                    for t in range(NT):
                        for i, k in enumerate(("q2", "k2", "v2")):
                            reader = (v2_ready, l * NT + t) if i == 2 else (qn_ready, l * 2 * NT + 2 * t + i)
                            to_tokens((k, l, t), reader, W[f"qkv{l}"], n=INNER, shift=True, col=i * INNER)
                        if t >= 2:
                            turn_qk(t - 2)
                    turn_qk(NT - 2)
                    turn_qk(NT - 1)
                    pe.wait_ge(v2_ready, due(v2_ready, it, l * NT + NT - 1))
                    pe.wait_ge(qkT_ready, due(qkT_ready, it, l * 2 * NT + 2 * NT - 1))
                    for u in range(-LAG2, len(LOCAL) + 1):
                        if u + LAG2 < len(LOCAL):
                            t, g = LOCAL[u + LAG2]
                            b = take(("s2", l, u + LAG2), (e2_ready, l * len(LOCAL) + u + LAG2))
                            par, heads, tiles = local_groups(t)[g]
                            w = P * len(tiles)
                            for i, h in enumerate(heads):
                                last = mm(b[:, i * w:(i + 1) * w], QT2[:, h // 2, t * P:(t + 1) * P],
                                          KT2[par][:, h // 2, tiles[0] * P:tiles[0] * P + w], start=True, stop=True)
                            last.then_inc(full_of(("s2", l, u + LAG2)), 1)
                        if 0 <= u < len(LOCAL):
                            b = take(("t2", l, u), (pt2_ready, l * len(LOCAL) + u))
                            pe.wait_ge(p2_ready, due(p2_ready, it, l * len(LOCAL) + u))
                            for i in range(4):
                                last = tp(b[:, i * P:(i + 1) * P], E[:, u % ER, i * P:(i + 1) * P], ident[:])
                            last.then_inc(full_of(("t2", l, u)), 1)
                        if u >= 1:
                            t, g = LOCAL[u - 1]
                            if g == 0:
                                zs = [take(("z2", l, t, hf), (o2_ready, l * NT + t), ring=1) for hf in range(2)]
                            pe.wait_ge(pt2_ready, due(pt2_ready, it, l * len(LOCAL) + u - 1))
                            par, heads, tiles = local_groups(t)[g]
                            blk = 0
                            for h in heads:
                                for j, kt in enumerate(tiles):
                                    last = mm(zs[h // 4][:, (h % 4) * (HD2 + 1):(h % 4 + 1) * (HD2 + 1)],
                                              PT[:, (u - 1) % PR, blk * P:(blk + 1) * P], V2[:, kt, h, :],
                                              start=j == 0, stop=j == len(tiles) - 1)
                                    blk += 1
                                if h in (3, 7):
                                    last.then_inc(full_of(("z2", l, t, h // 4)), 1)
                    for t in range(NT):
                        pe.wait_ge(o2_ready, due(o2_ready, it, l * NT + t))
                        b = take(("oT", l, t), (oT_ready, l * NT + t))
                        for k in range(INNER // P):
                            last = tp(b[:, k * P:(k + 1) * P], O2[:, t, k * P:(k + 1) * P], ident[:])
                        last.then_inc(full_of(("oT", l, t)), 1)
                    for t in range(NT):
                        pe.wait_ge(oT_ready, due(oT_ready, it, l * NT + t))
                        b = take(("wo", l, t), (y_ready, l * NT + t))
                        for k in range(INNER // P):
                            last = mm(b[:, 0:D], OT[:, k, t * P:(t + 1) * P], W[f"wo{l}"][:, k, :],
                                      start=k == 0, stop=k == INNER // P - 1)
                        last.then_inc(full_of(("wo", l, t)), 1)
                    b = take(("sh", l), (tok_ready, tok_at(3 + 2 * l, NT - 1)))
                    for t in range(NT):
                        pe.wait_ge(y_ready, due(y_ready, it, l * NT + t))
                        last = mm(b[:, t * P:(t + 1) * P], shiftm[:, 0, :], y[:, t, P:D], start=True, stop=t % 2 == 0)
                        if t % 2:
                            last = mm(b[:, t * P:(t + 1) * P], shiftm[:, 1, :], y[:, t - 1, P:D], start=False, stop=True)
                    last.then_inc(full_of(("sh", l)), 1)
                    to_features(3 + 2 * l, xn)
                    for j in range(HF):
                        for i, k in enumerate(("g", "a")):
                            to_columns((k, l, j), (hh_ready, l * (HF + 1) + j), W[f"w1{l}"], 2 * j + i, seq)
                    to_columns(("r", l), (hh_ready, l * (HF + 1) + HF), W[f"w1{l}"], 2 * HF, seq)
                    for t in range(NT):
                        b = take(("w2", l, t), (w2_read, l * NT + t))
                        for k in range(HF + 1):
                            if t == 0:
                                pe.wait_ge(hh_ready, due(hh_ready, it, l * (HF + 1) + k))
                            r = P if k < HF else HR + 1
                            last = mm(b[:, 0:D], HH[0:r, k, t * P:(t + 1) * P], W[f"w2{l}"][0:r, k, :],
                                      start=k == 0, stop=k == HF)
                        last.then_inc(full_of(("w2", l, t)), 1)

                to_features(6, xn)
                for m in range(KD):
                    to_columns(("q3", m), (qk3_ready, m), W["L1_xattn_Wq"], m, seq)
                for m in range(KD):
                    to_columns(("k3", m), (qk3_ready, KD + m), W["L1_xattn_Wk"], m, seq)
                for t in range(NT):
                    to_tokens(("v3", t), (v3_ready, t), W["L1_xattn_Wv"])
                pe.wait_ge(qk3_ready, due(qk3_ready, it, 2 * KD - 1))
                pe.wait_ge(v3_ready, due(v3_ready, it, NT - 1))
                pe.wait_ge(ones3_ready, due(ones3_ready, it, 0))
                for u in range(-2, len(CONV) + 1):
                    if u + 2 < len(CONV):
                        bb, h = CONV[u + 2]
                        b = take(("s3", u + 2), (s0_ready, u + 2))
                        r = (h // 2) % 4
                        rows = slice(32 * r, 32 * r + 32)
                        for jt in range(2):
                            last = mm(b[:, jt * T:(jt + 1) * T],
                                      KT3[rows, h // 8, h % 2, bb * T + jt * P:bb * T + (jt + 1) * P],
                                      QT[rows, h // 8, bb * T:(bb + 1) * T], start=True, stop=True)
                        last.then_inc(full_of(("s3", u + 2)), 1)
                    if 0 <= u + 1 < len(CONV):
                        b = take(("c3", u + 1), (e3_ready, u + 1))
                        pe.wait_ge(band_ready, due(band_ready, it, u + 1))
                        pe.wait_ge(s0_ready, due(s0_ready, it, u + 1))
                        for i2 in range(2):
                            n = 0
                            for jt in range(2):
                                for tap in range(3):
                                    lo = jt * (P - 1)
                                    last = mm(b[:, i2 * T + lo:i2 * T + lo + P + 1],
                                              S0[:, (u + 1) % SR, jt, i2 * P + tap:i2 * P + tap + P],
                                              band[:, (u + 1) % SR, tap, 1 - jt:1 - jt + P + 1],
                                              start=n == 0, stop=n == 5, skip_group_check=True)
                                    n += 1
                        last.then_inc(full_of(("c3", u + 1)), 1)
                    if 0 <= u < len(CONV):
                        b = take(("t3", u), (pt3_ready, u))
                        pe.wait_ge(p3_ready, due(p3_ready, it, u))
                        for jt in range(2):
                            for i2 in range(2):
                                last = tp(b[:, (jt * 2 + i2) * P:(jt * 2 + i2 + 1) * P],
                                          E[:, u % ER, i2 * T + jt * P:i2 * T + (jt + 1) * P], ident[:])
                        last.then_inc(full_of(("t3", u)), 1)
                    if u >= 1:
                        bb, h = CONV[u - 1]
                        if h == 0:
                            zs = [take(("z3", bb, i2), (tok_ready, tok_at(7, 2 * bb + i2)), ring=1) for i2 in range(2)]
                        pe.wait_ge(pt3_ready, due(pt3_ready, it, u - 1))
                        for i2 in range(2):
                            for jt in range(2):
                                last = mm(zs[i2][:, h * (HD + 1):(h + 1) * (HD + 1)],
                                          PT[:, (u - 1) % PR, (jt * 2 + i2) * P:(jt * 2 + i2 + 1) * P],
                                          V3[:, 2 * bb + jt, h, :], start=jt == 0, stop=jt == 1)
                            if h == H - 1:
                                last.then_inc(full_of(("z3", bb, i2)), 1)
                to_features(7, xn)
                for t in range(NT):
                    to_tokens(("p3", t), (x3_ready, t), W["L1_xattn_proj_W"])

                to_features(8, xn)
                pe.wait_ge(xr_ready, due(xr_ready, it, 0))
                for m in range(KD):
                    to_columns(("kk", m), (ka_ready, m), W["L1_ffn_W_k"], m,
                               lambda k: XR[:, 0, k, :].rearrange("p (b t) -> p b t", b=NB))
                pe.wait_ge(xr_ready, due(xr_ready, it, 1))
                for t in range(NT):
                    to_tokens(("r4", t), (sg_ready, t), W["L1_ffn_W_r"], src=lambda k: XR[:, 1, k, :])
                pe.wait_ge(ka_ready, due(ka_ready, it, KD - 1))
                for t in range(NT):
                    to_tokens(("v4", t), (xo_ready, t), W["L1_ffn_W_v"], src=lambda k: KA[:, k, :])

        @block.scalar
        def _(act):
            act.wait_ge(first_in, 16 * len(first_loads))
            f, copy = nc.scalar.activation, nc.scalar.copy
            with act.Fori(0, B // HB) as it:
                act.wait_ge(ehs_ready, due(ehs_ready, it, 0))
                f(eh[0:C], ehs[0:C], ACT.Gelu).then_inc(eh_ready, 1)
                act.wait_ge(hist_1, due(hist_1, it, 0))
                f(h1[:, :], bank[0][:, 0:HB * C], ACT.Gelu, bias=W["ctxb1"][:, 0:1]).then_inc(h1_ready, 1)
                act.wait_ge(aws_ready, due(aws_ready, it, 0))
                f(aw[:], aw[:], ACT.Exp).then_inc(awe_ready, 1)
            it = 0
            act.wait_ge(weights_in, 16 * len(loads))
            act.wait_ge(consts_set, 2)
            act.wait_ge(kgs_ready, due(kgs_ready, it, 0))
            f(kg[:], kg[:], ACT.Gelu).then_inc(kg_ready, 1)
            act.wait_ge(kps_ready, due(kps_ready, it, 0))
            f(kp[:], kp[:], ACT.Exp).then_inc(kpe_ready, 1)

            with act.Fori(0, ITERS) as it:

                def features(n, l=None):
                    act.wait_ge(full_of(("fT", n, 0)), full_at(("fT", n, 0), it))
                    b = bank_of(("fT", n, 0))
                    src = b[:, :].rearrange("p (b t) -> p b t", b=NB)
                    if l is None:
                        ins = copy(F[:, 0, :, 1:T + 1], src)
                    else:
                        ins = f(F[:, 0, :, 1:T + 1], src, ACT.Identity, bias=W[f"b{l}"][:, 0:1], scale=W[f"g{l}"][:, 0:1])
                    ins.then_inc(feat_a, 1)

                def exponentials(u, n, groups, width, scores, probs, total=None):
                    act.wait_ge(scores, due(scores, it, n))
                    for g in range(groups):
                        e = E[:, u % ER, g * width:(g + 1) * width]
                        if total is None:
                            last = f(e, e, ACT.Exp, bias=mx[:, u % ER, g:g + 1])
                        else:
                            last = f(e, e, ACT.Exp, bias=mx[:, u % ER, g:g + 1], accum_out=total[:, u % ER, g:g + 1])
                    last.then_inc(probs, 1)

                def turned(u, key, rows, probs_turned):
                    act.wait_ge(full_of(key), full_at(key, it))
                    copy(PT[0:rows, u % PR, :], bank_of(key)[0:rows, :]).then_inc(probs_turned, 1)

                features(0)
                for u in range(len(CROSS) + 2):
                    if u < len(CROSS):
                        exponentials(u, u, 4, C, e1_ready, p1_ready, sums)
                    if u >= 2:
                        turned(u - 2, ("t1", u - 2), C, pt1_ready)
                features(1)
                for l in L:
                    features(2 + 2 * l)

                    def turn_qk(t):
                        act.wait_ge(full_of(("qT", l, t)), full_at(("qT", l, t), it))
                        copy(QT2[:, :, t * P:(t + 1) * P], bank_of(("qT", l, t))[:, :].rearrange("p (h t) -> p h t", h=4)).then_inc(qkT_ready, 1)
                        act.wait_ge(full_of(("kT", l, t)), full_at(("kT", l, t), it))
                        b = bank_of(("kT", l, t))
                        for par in range(2):
                            last = f(KT2[par][:, :, t * P:(t + 1) * P], b[:, :].rearrange("p (h t) -> p h t", h=4), ACT.Copy, scale=W["upper"][:, par:par + 1])
                        last.then_inc(qkT_ready, 1)

                    for t in range(NT):
                        for i, k in enumerate(("q2", "k2")):
                            act.wait_ge(full_of((k, l, t)), full_at((k, l, t), it))
                            b = bank_of((k, l, t))
                            if t >= 1:
                                act.wait_ge(ss_sum, due(ss_sum, it, l * 2 * NT + 2 * (t - 1) + i))
                            f(sq[:, i, :], b[:, :], ACT.Square).then_inc(sq_ready, 1)
                        act.wait_ge(full_of(("v2", l, t)), full_at(("v2", l, t), it))
                        b = bank_of(("v2", l, t))
                        copy(V2[:, t, :, 0:HD2], b[:, :].rearrange("p (h d) -> p h d", h=H2)).then_inc(v2_ready, 1)
                        if t >= 2:
                            turn_qk(t - 2)
                    turn_qk(NT - 2)
                    turn_qk(NT - 1)
                    for u in range(len(LOCAL) + 1):
                        if u < len(LOCAL):
                            heads = len(local_groups(LOCAL[u][0])[0][1])
                            exponentials(u, l * len(LOCAL) + u, heads, 512 // heads, e2_ready, p2_ready)
                        if u >= 1:
                            turned(u - 1, ("t2", l, u - 1), P, pt2_ready)
                    for t in range(NT):
                        act.wait_ge(full_of(("oT", l, t)), full_at(("oT", l, t), it))
                        b = bank_of(("oT", l, t))
                        copy(OT[:, :, t * P:(t + 1) * P], b[:, :].rearrange("p (k t) -> p k t", k=INNER // P)).then_inc(oT_ready, 1)
                    features(3 + 2 * l, l)
                    for j in range(HF):
                        act.wait_ge(full_of(("g", l, j)), full_at(("g", l, j), it))
                        b = bank_of(("g", l, j))
                        if j >= 2:
                            act.wait_ge(hh_ready, due(hh_ready, it, l * (HF + 1) + j - 2))
                        f(G[:, j % 2, :], b[:, :], ACT.Gelu, bias=W[f"b1{l}"][:, 2 * j:2 * j + 1]).then_inc(g_ready, 1)
                    act.wait_ge(full_of(("r", l)), full_at(("r", l), it))
                    b = bank_of(("r", l))
                    act.wait_ge(hh_ready, due(hh_ready, it, l * (HF + 1) + HF - 2))
                    f(G[0:HR, HF % 2, :], b[64:64 + HR, :], ACT.Gelu, bias=W[f"b1{l}"][64:64 + HR, 2 * HF:2 * HF + 1]).then_inc(g_ready, 1)
                features(6)
                for t in range(NT):
                    act.wait_ge(full_of(("v3", t)), full_at(("v3", t), it))
                    b = bank_of(("v3", t))
                    copy(V3[:, t, :, 0:HD], b[:, 0:D].rearrange("p (h d) -> p h d", h=H)).then_inc(v3_ready, 1)
                for u in range(len(CONV) + 1):
                    if u < len(CONV):
                        exponentials(u, u, 2, T, e3_ready, p3_ready)
                    if u >= 1:
                        turned(u - 1, ("t3", u - 1), P, pt3_ready)
                features(7)
                features(8)
                for t in range(NT):
                    act.wait_ge(full_of(("r4", t)), full_at(("r4", t), it))
                    b = bank_of(("r4", t))
                    if t >= 2:
                        act.wait_ge(xo_ready, due(xo_ready, it, t - 2))
                    f(sg[:, t % 2, :], b[:, 0:D], ACT.Sigmoid).then_inc(sg_ready, 1)

        @block.vector
        def _(dve):
            dve.wait_ge(first_in, 16 * len(first_loads))
            v = nc.vector
            tt, ts, stt = v.tensor_tensor, v.tensor_scalar, v.scalar_tensor_tensor
            with dve.Fori(0, B // HB) as it:
                v.tensor_copy(spare_v[:], ident[0:1, 0:1]).then_inc(hist_go, 1)
                dve.wait_ge(hist_h, due(hist_h, it, 0))
                for bb in range(HB):
                    last = tt(ehs[0:C, bb, :], bank[bb][0:C, :], W["histb"][0:C], ALU.add)
                last.then_inc(hist_dve, 1)
                dve.wait_ge(hist_dve, own(hist_dve, it))
                for bb in range(HB):
                    last = v.bn_stats(stats[0:C, bb, 0, :], ehs[0:C, bb, :])
                last.then_inc(hist_dve, 1)
                dve.wait_ge(hist_dve, own(hist_dve, it))
                v.memset(fence[:], 0.0)
                for bb in range(HB):
                    last = v.bn_aggr(mv[0:C, bb, :], stats[0:C, bb, 0, :])
                last.then_inc(hist_dve, 1)
                dve.wait_ge(hist_dve, own(hist_dve, it))
                ts(rstd[0:C, 0:HB], mv[0:C, 0:HB, 1], EPS, None, ALU.add).then_inc(hist_var, 1)
                for bb in range(HB):
                    last = stt(ehs[0:C, bb, :], ehs[0:C, bb, :], mv[0:C, bb, 0:1], W["histg"][0:C], ALU.subtract, ALU.mult)
                last.then_inc(hist_dve, 1)
                dve.wait_ge(hist_rstd, due(hist_rstd, it, 0))
                dve.wait_ge(hist_dve, own(hist_dve, it))
                for bb in range(HB):
                    last = stt(ehs[0:C, bb, :], ehs[0:C, bb, :], rstd[0:C, bb:bb + 1], W["histB"][0:C], ALU.mult, ALU.add)
                last.then_inc(ehs_ready, 1)
                dve.wait_ge(hist_T, due(hist_T, it, 0))
                for bb in range(HB):
                    last = v.tensor_copy(ehT[:, :, bb, :], bank[HB + bb][:, :].rearrange("p (c n) -> p c n", c=HIST // P)[:, :, 0:C])
                last.then_inc(ehT_ready, 1)
                dve.wait_ge(hist_2, due(hist_2, it, 0))
                ts(aw[0:1].rearrange("p b n -> p (b n)"), bank[1][0:1, 0:HB * C], W["ctxb2"][0:1, 0:1], None, ALU.add).then_inc(hist_dve, 1)
                dve.wait_ge(hist_dve, own(hist_dve, it))
                v.tensor_reduce(am[0:1, :, 0], aw[0:1], AX_X, ALU.max).then_inc(hist_dve, 1)
                dve.wait_ge(hist_dve, own(hist_dve, it))
                tt(aw[0:1], aw[0:1], am[0:1, :, 0:1].broadcast_to([1, HB, C]), ALU.subtract).then_inc(aws_ready, 1)
                dve.wait_ge(awe_ready, due(awe_ready, it, 0))
                v.tensor_reduce(am[0:1, :, 1], aw[0:1], AX_X, ALU.add).then_inc(hist_dve, 1)
                dve.wait_ge(hist_dve, own(hist_dve, it))
                v.reciprocal(am[0:1, :, 2], am[0:1, :, 1]).then_inc(hist_dve, 1)
                dve.wait_ge(hist_dve, own(hist_dve, it))
                tt(aw[0:1], aw[0:1], am[0:1, :, 2:3].broadcast_to([1, HB, C]), ALU.mult).then_inc(aw_ready, 1)
                dve.wait_ge(hist_w, due(hist_w, it, 0))
                v.tensor_copy(awc[0:C, :], bank[2][0:C, 0:HB]).then_inc(awc_ready, 1)
                dve.wait_ge(hist_c, due(hist_c, it, 0))
                v.tensor_copy(cc[:, :, bass.ds(it * HB, HB)],
                              bank[3][:, 0:HIST // P * HB].rearrange("p (c b) -> p c b", b=HB)).then_inc(hist_dve, 1)
                dve.wait_ge(hist_dve, own(hist_dve, it))

            dve.wait_ge(weights_in, 16 * len(loads))
            ts(negm[:], W["mask_i"][:], 0.0, NEG, ALU.is_equal, ALU.mult)
            ts(far[:], W["far_u"][:].bitcast(U8), FAR, None, ALU.mult)
            ts(keepT[:], W["farT_u"][:].bitcast(U8), -1.0, 1.0, ALU.mult, ALU.add)
            for l in range(DEPTH):
                for hf in range(2):
                    for i, n in enumerate(("q", "k")):
                        sc = W[f"{n}s{l}"]
                        tt(rotl[:, l, hf, 2 * i, :], rot[:, hf, 2 * i, :], sc[:], ALU.mult)
                        for lo, hi in ((0, HD2 // 2), (HD2 // 2, 0)):
                            tt(rotl[:, l, hf, 2 * i + 1, lo:lo + HD2 // 2], rot[:, hf, 2 * i + 1, lo:lo + HD2 // 2],
                               sc[:, hi:hi + HD2 // 2], ALU.mult)
            for i, n in enumerate(("k", "r")):
                last = ts(omr[:, i, :], W[f"L1_ffn_mu_{n}"][:], -1.0, 1.0, ALU.mult, ALU.add)
            last.then_inc(consts_set, 1)
            dve.wait_ge(consts_set, 2)
            it = 0
            v.tensor_copy(spare_v[:], ident[0:1, 0:1]).then_inc(cc_ready, 1)
            dve.wait_ge(kg_1, due(kg_1, it, 0))
            tt(kg[:], bank[0][0:B, 0:D], W["kgb1"][:], ALU.add).then_inc(kg_dve, 1)
            dve.wait_ge(kg_dve, own(kg_dve, it))
            v.bn_stats(stats[0:B, 0, 0, :], kg[:]).then_inc(kg_dve, 1)
            dve.wait_ge(kg_dve, own(kg_dve, it))
            v.bn_aggr(mv[0:B, 0, :], stats[0:B, 0, 0, :]).then_inc(kg_dve, 1)
            dve.wait_ge(kg_dve, own(kg_dve, it))
            ts(rstd[0:B, 0:1], mv[0:B, 0, 1:2], EPS, None, ALU.add).then_inc(kg_var, 1)
            dve.wait_ge(kg_rstd, due(kg_rstd, it, 0))
            ts(kg[:], kg[:], mv[0:B, 0, 0:1], rstd[0:B, 0:1], ALU.subtract, ALU.mult).then_inc(kg_dve, 1)
            dve.wait_ge(kg_dve, own(kg_dve, it))
            tt(kg[:], kg[:], W["kgg"][:], ALU.mult).then_inc(kg_dve, 1)
            dve.wait_ge(kg_dve, own(kg_dve, it))
            tt(kg[:], kg[:], W["kgB"][:], ALU.add).then_inc(kgs_ready, 1)
            dve.wait_ge(kg_T, due(kg_T, it, 0))
            v.tensor_copy(kgT[:], bank[1][:, 0:KD * B].rearrange("p (k b) -> p k b", k=KD)).then_inc(kgT_ready, 1)
            dve.wait_ge(kg_2, due(kg_2, it, 0))
            tt(kp[:].rearrange("b h n -> b (h n)"), bank[2][0:B, 0:H * 9], W["kgb2"][:], ALU.add).then_inc(kg_dve, 1)
            dve.wait_ge(kg_dve, own(kg_dve, it))
            v.tensor_reduce(km[:, 0, :], kp[:], AX_X, ALU.max).then_inc(kg_dve, 1)
            dve.wait_ge(kg_dve, own(kg_dve, it))
            tt(kp[:], kp[:], wide(km[:, 0, :], [B, H, 9], 2), ALU.subtract).then_inc(kps_ready, 1)
            dve.wait_ge(kpe_ready, due(kpe_ready, it, 0))
            v.tensor_reduce(km[:, 0, :], kp[:], AX_X, ALU.add).then_inc(kg_dve, 1)
            dve.wait_ge(kg_dve, own(kg_dve, it))
            v.reciprocal(km[:, 1, :], km[:, 0, :]).then_inc(kg_dve, 1)
            dve.wait_ge(kg_dve, own(kg_dve, it))
            tt(kp[:], kp[:], wide(km[:, 1, :], [B, H, 9], 2), ALU.mult).then_inc(kp_ready, 1)

            with dve.Fori(0, ITERS) as it:

                def statistics(first, second, t):
                    v.bn_stats(stats[:, t, 0, :], first)
                    return v.bn_stats(stats[:, t, 1, :], second)

                def scales(n, last):
                    last.then_inc(ln_stats, 1)
                    dve.wait_ge(ln_stats, own(ln_stats, it))
                    v.memset(fence[:], 0.0)
                    for t in range(NT):
                        last = v.bn_aggr(mv[:, t, :], stats[:, t].rearrange("p a b -> p (a b)"))
                    last.then_inc(ln_moments, 1)
                    dve.wait_ge(ln_moments, own(ln_moments, it))
                    ts(rstd[:], mv[:, :, 1], EPS, None, ALU.add).then_inc(var_ready, 1)
                    dve.wait_ge(rstd_ready, due(rstd_ready, it, n))

                def layernorm(n, src, dst, ready=tok_ready):
                    for t in range(NT):
                        last = statistics(src[:, t, 0:P], src[:, t, P:D], t)
                    scales(n, last)
                    for t in range(NT):
                        ts(dst[:, t, :], src[:, t, :], mv[:, t, 0:1], rstd[:, t:t + 1], ALU.subtract, ALU.mult).then_inc(ready, 1)

                def features(n, l=None):
                    dve.wait_ge(full_of(("fT", n, 1)), full_at(("fT", n, 1), it))
                    b = bank_of(("fT", n, 1))
                    src = b[:, :].rearrange("p (b t) -> p b t", b=NB)
                    if l is None:
                        ins = v.tensor_copy(F[:, 1, :, 1:T + 1], src)
                    else:
                        ins = ts(F[:, 1, :, 1:T + 1], src, W[f"g{l}"][:, 1:2], W[f"b{l}"][:, 1:2], ALU.mult, ALU.add)
                    ins.then_inc(feat_v, 1)

                def head_outputs(dst, src, heads, width, lo=0):
                    v.reciprocal(rz[:, lo:lo + heads], src[:, :, width]).then_inc(rz_ready, 1)
                    dve.wait_ge(rz_ready, own(rz_ready, it))
                    return tt(dst, src[:, :, 0:width], wide(rz[:, lo:lo + heads], [P, heads, width], 2), ALU.mult)

                def softmax_input(u, b, groups, width, mask, ready):
                    e = E[:, u % ER, 0:groups * width].rearrange("p (g n) -> p g n", g=groups)
                    m = mx[:, u % ER, 0:groups]
                    tt(e, b[:, 0:groups * width].rearrange("p (g n) -> p g n", g=groups), mask, ALU.add).then_inc(sm_masked, 1)
                    dve.wait_ge(sm_masked, own(sm_masked, it))
                    v.tensor_reduce(m, e, AX_X, ALU.max, negate=True).then_inc(ready, 1)

                dve.wait_ge(x_in, due(x_in, it, 0))
                layernorm(0, xin, xn)
                features(0)
                for m in range(KD):
                    dve.wait_ge(full_of(("q1", m)), full_at(("q1", m), it))
                    b = bank_of(("q1", m))
                    ts(QT[:, m, :], b[:, :], W["L0_xattn_bq"][:, m:m + 1], HD ** -0.5, ALU.add, ALU.mult).then_inc(qk1_ready, 1)
                dve.wait_ge(full_of(("k1",)), full_at(("k1",), it))
                b = bank_of(("k1",))
                for m in range(KD):
                    for bb in range(NB):
                        last = stt(KT1[:, m, bb], wide(b[:, m * 256 + bb * C:m * 256 + (bb + 1) * C], [P, HK, C], 1), W["L0_xattn_bk"][:, m:m + 1],
                                   wide(W["head_rows"][:], [P, HK, C], 2), ALU.add, ALU.mult)
                last.then_inc(qk1_ready, 1)
                dve.wait_ge(v1_zero, due(v1_zero, it, 0))
                for bb in range(NB):
                    dve.wait_ge(full_of(("v1", bb)), full_at(("v1", bb), it))
                    b = bank_of(("v1", bb))
                    for m in range(KD):
                        lo = (bb * KD + m) * HK * P
                        own_cols = V1[0:C, lo:lo + HK * (P + HD)].rearrange("p (h d) -> p h d", h=HK)[:, :, 0:HD]
                        last = tt(own_cols, b[0:C, m * P:(m + 1) * P].rearrange("p (h d) -> p h d", h=HK),
                                  W["L0_xattn_bv"][0:C, m * P:(m + 1) * P].rearrange("p (h d) -> p h d", h=HK), ALU.add)
                    last.then_inc(qk1_ready, 1)
                for u in range(len(CROSS) + 1):
                    if u < len(CROSS):
                        dve.wait_ge(full_of(("s1", u)), full_at(("s1", u), it))
                        b = bank_of(("s1", u))
                        softmax_input(u, b, 4, C, wide(negm[:, CROSS[u][0] % 2, :], [P, 4, C], 1), e1_ready)
                    if u >= 1:
                        dve.wait_ge(p1_ready, due(p1_ready, it, u - 1))
                        v.reciprocal(rsums[:, (u - 1) % ER, :], sums[:, (u - 1) % ER, :]).then_inc(rs1_ready, 1)
                features(1)
                for t in range(NT):
                    dve.wait_ge(xb_ready, due(xb_ready, it, t))
                    dve.wait_ge(full_of(("o1", t)), full_at(("o1", t), it))
                    b = bank_of(("o1", t))
                    tt(x[:, t, :], x[:, t, :], b[:, 0:D], ALU.add).then_inc(x1_ready, 1)
                dve.wait_ge(x1_ready, due(x1_ready, it, NT - 1))
                dve.wait_ge(x_out, due(x_out, it, 0))
                layernorm(1, x, y)
                for l in L:
                    features(2 + 2 * l)

                    base = l * 2 * NT
                    for r in range(-2, 2 * NT):
                        if r + 2 < 2 * NT:
                            t, i = divmod(r + 2, 2)
                            dve.wait_ge(sq_ready, due(sq_ready, it, base + r + 2))
                            v.tensor_reduce(ss[:, i, :], sq[:, i, :].rearrange("p (h d) -> p h d", h=H2), AX_X, ALU.add).then_inc(ss_sum, 1)
                            dve.wait_ge(ss_sum, own(ss_sum, it))
                            ts(ss[:, i, :], ss[:, i, :], 1e-24, None, ALU.max).then_inc(ss_ready, 1)
                        if 0 <= r + 1 < 2 * NT:
                            t, i = divmod(r + 1, 2)
                            b = bank_of((("q2", "k2")[i], l, t))
                            dve.wait_ge(full_of((("q2", "k2")[i], l, t)), full_at((("q2", "k2")[i], l, t), it))
                            dve.wait_ge(rr_ready, due(rr_ready, it, base + r + 1))
                            q4 = qn[:, i, :].rearrange("p (h d) -> p h d", h=H2)
                            if r + 1 >= 2:
                                dve.wait_ge(qb_ready, due(qb_ready, it, base + r - 1))
                            tt(q4, b[:, :].rearrange("p (h d) -> p h d", h=H2), wide(rr[:, i, :], [P, H2, HD2], 2), ALU.mult).then_inc(qn_ready, 1)
                            dve.wait_ge(qn_ready, own(qn_ready, it))
                            if t >= 1:
                                dve.wait_ge(full_of((("qT", "kT")[i], l, t - 1)), full_at((("qT", "kT")[i], l, t - 1), it))
                            q3 = qa[:, i, :].rearrange("p (h d) -> p h d", h=H2)
                            tt(q3, q4, wide(rotl[:, l, t % 2, 2 * i, :], [P, H2, HD2], 1), ALU.mult).then_inc(qa_ready, 1)
                        if r >= 0:
                            i = r % 2
                            dve.wait_ge(qb_ready, due(qb_ready, it, base + r))
                            dve.wait_ge(qa_ready, due(qa_ready, it, base + r))
                            tt(qa[:, i, :], qa[:, i, :], qb[:, i, :], ALU.add).then_inc(qr_ready, 1)

                    for u in range(len(LOCAL) + 2):
                        if u < len(LOCAL):
                            t, g = LOCAL[u]
                            dve.wait_ge(full_of(("s2", l, u)), full_at(("s2", l, u), it))
                            b = bank_of(("s2", l, u))
                            if t % 2 == 0:
                                softmax_input(u, b, 4, P, wide(W["causal"][:, 1, :], [P, 4, P], 1), e2_ready)
                            else:
                                softmax_input(u, b, 2, 2 * P, wide(W["causal"][:].rearrange("p a n -> p (a n)"), [P, 2, 2 * P], 1), e2_ready)
                        if u >= 2 and LOCAL[u - 2][1] == len(local_groups(LOCAL[u - 2][0])) - 1:
                            t = LOCAL[u - 2][0]
                            for hf in range(2):
                                dve.wait_ge(full_of(("z2", l, t, hf)), full_at(("z2", l, t, hf), it))
                                b = bank_of(("z2", l, t, hf))
                                z = b[:, 0:4 * (HD2 + 1)].rearrange("p (h d) -> p h d", h=4)
                                last = head_outputs(O2[:, t, hf * 256:(hf + 1) * 256].rearrange("p (h d) -> p h d", h=4), z, 4, HD2, 4 * hf)
                            last.then_inc(o2_ready, 1)
                    for t in range(NT):
                        dve.wait_ge(full_of(("wo", l, t)), full_at(("wo", l, t), it))
                        b = bank_of(("wo", l, t))
                        tt(y[:, t, :], y[:, t, :], b[:, 0:D], ALU.add).then_inc(y_ready, 1)
                    dve.wait_ge(full_of(("sh", l)), full_at(("sh", l), it))
                    sh = bank_of(("sh", l))
                    for t in range(NT):
                        last = statistics(y[:, t, 0:P], sh[:, t * P:(t + 1) * P], t)
                    scales(2 + l, last)
                    for t in range(NT):
                        ts(xn[:, t, 0:P], y[:, t, 0:P], mv[:, t, 0:1], rstd[:, t:t + 1], ALU.subtract, ALU.mult)
                        ts(xn[:, t, P:D], sh[:, t * P:(t + 1) * P], mv[:, t, 0:1], rstd[:, t:t + 1], ALU.subtract, ALU.mult).then_inc(tok_ready, 1)
                    features(3 + 2 * l, l)
                    v.memset(HH[32:64, HF, :], 1.0).then_inc(ones_row, 1)
                    dve.wait_ge(ones_row, own(ones_row, it))
                    for j in range(HF + 1):
                        dve.wait_ge(full_of(("a", l, j) if j < HF else ("r", l)), full_at(("a", l, j) if j < HF else ("r", l), it))
                        b = bank_of(("a", l, j) if j < HF else ("r", l))
                        r = P if j < HF else HR
                        dve.wait_ge(g_ready, due(g_ready, it, l * (HF + 1) + j))
                        stt(HH[0:r, j, :], b[0:r, :], W[f"b1{l}"][0:r, 2 * j + (j < HF):2 * j + (j < HF) + 1], G[0:r, j % 2, :],
                                  ALU.add, ALU.mult).then_inc(hh_ready, 1)
                    for t in range(NT):
                        dve.wait_ge(full_of(("w2", l, t)), full_at(("w2", l, t), it))
                        b = bank_of(("w2", l, t))
                        tt(y[:, t, :], y[:, t, :], b[:, 0:D], ALU.add).then_inc(w2_read, 1)
                        if l < DEPTH - 1:
                            dve.wait_ge(w2_read, due(w2_read, it, l * NT + t))
                            v.tensor_copy(y[0:1, t, 0:1], y[0:1, t, 0:1]).then_inc(tok_ready, 1)
                    dve.wait_ge(w2_read, due(w2_read, it, l * NT + NT - 1))
                tt(x[:], x[:], y[:], ALU.add).then_inc(x2_ready, 1)
                dve.wait_ge(x2_ready, own(x2_ready, it))
                layernorm(4, x, xn)
                features(6)
                for m in range(KD):
                    dve.wait_ge(full_of(("q3", m)), full_at(("q3", m), it))
                    b = bank_of(("q3", m))
                    ts(QT[:, m, :], b[:, :], HD ** -0.5, None, ALU.mult).then_inc(qk3_ready, 1)
                for m in range(KD):
                    dve.wait_ge(full_of(("k3", m)), full_at(("k3", m), it))
                    b = bank_of(("k3", m))
                    for par in range(PAR):
                        last = ts(KT3[:, m, par, :], b[:, :], parity[:, par:par + 1], None, ALU.mult)
                    last.then_inc(qk3_ready, 1)
                for edge in (0, T + 1):
                    v.memset(S0[:, :, :, edge:edge + 1], 0.0)
                v.memset(V3[:, :, :, HD:HD + 1], 1.0).then_inc(ones3_ready, 1)
                for u in range(-2, len(CONV)):
                    if u + 2 < len(CONV):
                        bb, h = CONV[u + 2]
                        dve.wait_ge(full_of(("s3", u + 2)), full_at(("s3", u + 2), it))
                        b = bank_of(("s3", u + 2))
                        tt(S0[:, (u + 2) % SR, :, 1:T + 1], b[:, :].rearrange("p (j i) -> p j i", j=2), keepT[:], ALU.mult).then_inc(s0_ready, 1)
                    if 0 <= u + 1 < len(CONV):
                        dve.wait_ge(full_of(("c3", u + 1)), full_at(("c3", u + 1), it))
                        b = bank_of(("c3", u + 1))
                        softmax_input(u + 1, b, 2, T, far[:], e3_ready)
                    if u >= 1 and (u - 1) % H == H - 1:
                        bb = (u - 1) // H
                        for i2 in range(2):
                            dve.wait_ge(full_of(("z3", bb, i2)), full_at(("z3", bb, i2), it))
                            b = bank_of(("z3", bb, i2))
                            z = b[:, 0:H * (HD + 1)].rearrange("p (h d) -> p h d", h=H)
                            head_outputs(xn[:, 2 * bb + i2, :].rearrange("p (h d) -> p h d", h=H), z, H, HD, H * i2).then_inc(tok_ready, 1)
                bb = NB - 1
                for i2 in range(2):
                    dve.wait_ge(full_of(("z3", bb, i2)), full_at(("z3", bb, i2), it))
                    b = bank_of(("z3", bb, i2))
                    z = b[:, 0:H * (HD + 1)].rearrange("p (h d) -> p h d", h=H)
                    head_outputs(xn[:, 2 * bb + i2, :].rearrange("p (h d) -> p h d", h=H), z, H, HD, H * i2).then_inc(tok_ready, 1)
                features(7)
                for t in range(NT):
                    dve.wait_ge(full_of(("p3", t)), full_at(("p3", t), it))
                    b = bank_of(("p3", t))
                    tt(x[:, t, :], x[:, t, :], b[:, 0:D], ALU.add).then_inc(x3_ready, 1)
                    dve.wait_ge(x3_ready, own(x3_ready, it))
                    last = tt(x[:, t, :], x[:, t, :], W["L1_xattn_proj_b"][:], ALU.add)
                last.then_inc(x3_done, 1)
                dve.wait_ge(x3_done, own(x3_done, it))
                layernorm(5, x, xn)
                features(8)
                dve.wait_ge(feat_a, due(feat_a, it, 8))
                dve.wait_ge(feat_v, due(feat_v, it, 8))
                for i, n in enumerate(("k", "r")):
                    for k in range(KD):
                        last = ts(XR[:, i, k, :].rearrange("p (b t) -> p b t", b=NB), F[:, k, :, 0:T], omr[:, i, k:k + 1], None, ALU.mult)
                    last.then_inc(xr_part, 1)
                    dve.wait_ge(xr_part, own(xr_part, it))
                    for k in range(KD):
                        dst = XR[:, i, k, :].rearrange("p (b t) -> p b t", b=NB)
                        last = stt(dst, F[:, k, :, 1:T + 1], W[f"L1_ffn_mu_{n}"][:, k:k + 1], dst, ALU.mult, ALU.add)
                    last.then_inc(xr_ready, 1)
                for m in range(KD):
                    dve.wait_ge(full_of(("kk", m)), full_at(("kk", m), it))
                    b = bank_of(("kk", m))
                    ts(KA[:, m, :], b[:, :], 0.0, None, ALU.max).then_inc(ka_part, 1)
                    dve.wait_ge(ka_part, own(ka_part, it))
                    tt(KA[:, m, :], KA[:, m, :], KA[:, m, :], ALU.mult).then_inc(ka_ready, 1)
                for t in range(NT):
                    dve.wait_ge(sg_ready, due(sg_ready, it, t))
                    g = sg[:, t % 2, :]
                    dve.wait_ge(full_of(("v4", t)), full_at(("v4", t), it))
                    b = bank_of(("v4", t))
                    tt(g, g, b[:, 0:D], ALU.mult).then_inc(sg_part, 1)
                    dve.wait_ge(sg_part, own(sg_part, it))
                    tt(xo[:, t, :], x[:, t, :], g, ALU.add).then_inc(xo_ready, 1)

        @block.gpsimd
        def _(pool):
            g = nc.gpsimd
            g.memset(half[:], -0.5)
            g.memset(F[:], 0.0)
            g.memset(V2[:], 1.0)
            g.memset(one[:], 1.0).then_inc(consts_set, 1)
            with pool.Fori(0, B // HB) as it:
                pool.wait_ge(hist_var, due(hist_var, it, 0))
                g.tensor_tensor(rstd[0:C, 0:HB], rstd[0:C, 0:HB], half[0:C, 0:HB], ALU.pow).then_inc(hist_rstd, 1)
            it = 0
            pool.wait_ge(kg_var, due(kg_var, it, 0))
            g.tensor_tensor(rstd[0:B, 0:1], rstd[0:B, 0:1], half[0:B, 0:1], ALU.pow).then_inc(kg_rstd, 1)
            pool.wait_ge(weights_in, 16 * len(loads))
            pool.wait_ge(consts_set, 2)
            pool.wait_ge(kp_ready, due(kp_ready, 0, 0))
            g.memset(V1[0:C, :], 0.0).then_inc(v1_zero, 1)
            with pool.Fori(0, ITERS) as it:

                def scales(n):
                    pool.wait_ge(var_ready, due(var_ready, it, n))
                    g.tensor_tensor(rstd[:], rstd[:], half[:, 0:NT], ALU.pow).then_inc(rstd_ready, 1)

                scales(0)
                for t in range(NT):
                    g.tensor_tensor(x[:, t, :], xin[:, t, :], W["L0_xattn_bo"][:], ALU.add).then_inc(xb_ready, 1)
                for u in range(len(CROSS)):
                    pool.wait_ge(rs1_ready, due(rs1_ready, it, u))
                    e = E[:, u % ER, 0:4 * C].rearrange("p (g n) -> p g n", g=4)
                    g.tensor_tensor(e, e, wide(rsums[:, u % ER, :], [P, 4, C], 2), ALU.mult).then_inc(pn1_ready, 1)
                scales(1)
                for l in L:
                    for r in range(-2, 2 * NT):
                        if r >= 0:
                            t, i = divmod(r, 2)
                            pool.wait_ge(qn_ready, due(qn_ready, it, l * 2 * NT + r))
                            if t >= 1:
                                pool.wait_ge(qr_ready, due(qr_ready, it, l * 2 * NT + r - 2))
                            q4 = qn[:, i, :].rearrange("p (h d) -> p h d", h=H2)
                            b4 = qb[:, i, :].rearrange("p (h d) -> p h d", h=H2)
                            for lo, hi in ((0, HD2 // 2), (HD2 // 2, 0)):
                                last = g.tensor_tensor(b4[:, :, lo:lo + HD2 // 2], q4[:, :, hi:hi + HD2 // 2],
                                                       wide(rotl[:, l, t % 2, 2 * i + 1, lo:lo + HD2 // 2], [P, H2, HD2 // 2], 1), ALU.mult)
                            last.then_inc(qb_ready, 1)
                        if r + 2 < 2 * NT:
                            i = r % 2
                            pool.wait_ge(ss_ready, due(ss_ready, it, l * 2 * NT + r + 2))
                            g.tensor_tensor(rr[:, i, :], ss[:, i, :], half[:], ALU.pow).then_inc(rr_ready, 1)
                    scales(2 + l)
                scales(4)
                pool.wait_ge(kern_in, due(kern_in, it, 0))
                for u, (bb, h) in enumerate(CONV):
                    taps = kern[:, bb, h * 9:(h + 1) * 9].rearrange("p (a c) -> p c a", a=3)
                    dst = band[:, u % SR]
                    if u >= SR:
                        pool.wait_ge(full_of(("c3", u - SR)), full_at(("c3", u - SR), it))
                    if u:
                        pool.wait_ge(band_ready, due(band_ready, it, u - 1))
                    for c, diagonal in enumerate((dst, diag_k[:, 0], diag_k[:, 1])):
                        last = g.tensor_tensor(diagonal, wide(diag[:, c, :], [P, 3, GW], 1), wide(taps[:, c, :], [P, 3, GW], 2), ALU.mult)
                    last.then_inc(band_part, 1)
                    pool.wait_ge(band_part, own(band_part, it))
                    g.tensor_tensor(dst, dst, diag_k[:, 0], ALU.add).then_inc(band_part, 1)
                    pool.wait_ge(band_part, own(band_part, it))
                    g.tensor_tensor(dst, dst, diag_k[:, 1], ALU.add).then_inc(band_ready, 1)
                scales(5)
                pool.wait_ge(full_of(("r4", NT - 1)), full_at(("r4", NT - 1), it))
                g.tensor_tensor(pool_fence[:], half[0:1, 0:1], half[0:1, 0:1], ALU.mult)
                g.memset(V1[0:C, :], 0.0).then_inc(v1_zero, 1)

        @block.sync
        def _(sp):
            for dst, src in first_loads:
                sp.dma_start(dst[:], src).then_inc(first_in, 16)

            def load_context(step):
                for j in range(HB // NB):
                    sp.dma_start(hctx[:, :, j], a["ctxT"].rearrange("(s j) d n -> s j d n", j=HB // NB)[bass.ds(step, 1), j].rearrange("o (k p) n -> p (o k) n", p=P)).then_inc(hist_in, 16)

            load_context(0)
            for dst, src in loads:
                sp.dma_start(dst[:], src).then_inc(weights_in, 16)
            with sp.Fori(0, B // HB - 1) as it:
                sp.wait_ge(hist_h, due(hist_h, it, 0))
                load_context(it + 1)
            it = 0
            sp.wait_ge(kp_ready, due(kp_ready, it, 0))
            sp.dma_start(kern_d, kp[:].rearrange("b h n -> b (h n)")).then_inc(kern_out, 16)
            sp.wait_ge(kern_out, 16)
            sp.dma_start(spare[:], a["L1_xattn_ctx_b2"]).then_inc(x_out, 16)

            def load(step):
                sp.dma_start(xin[:], a["x"][bass.ds(step, 1)].rearrange("o (t p) n -> p (o t) n", p=P)).then_inc(x_in, 16)
                sp.dma_start(ctxT[:], a["ctxT"][bass.ds(step, 1)].rearrange("o (k p) n -> p (o k) n", p=P)).then_inc(ctx_in, 16)
                sp.dma_start(kern[:], kern_d.rearrange("(s b) n -> s (b n)", b=NB)[bass.ds(step, 1)].rearrange(
                    "o n -> (o n)").partition_broadcast(P).rearrange("p (b n) -> p b n", b=NB)).then_inc(kern_in, 16)

            def store(it):
                sp.wait_ge(xo_ready, due(xo_ready, it, NT - 1))
                sp.dma_start(out[bass.ds(it, 1)].rearrange("o (t p) n -> p (o t) n", p=P), y[:]).then_inc(x_out, 16)

            load(0)
            if ITERS > 1:
                with sp.Fori(0, ITERS - 1) as it:
                    sp.wait_ge(band_ready, due(band_ready, it, len(CONV) - 1))
                    load(it + 1)
                    store(it)
            store(ITERS - 1)
            sp.wait_ge(x_out, 16 * (ITERS + 1))


def _constants():
    f = np.float32
    p = np.arange(P)
    ident = np.eye(P, dtype=f)
    shift = np.zeros((P, 2, P), f)
    shift[p[:-1], 0, p[:-1] + 1] = 1
    shift[P - 1, 1, 0] = 1
    diag = np.zeros((P, 3, GW), f)
    for c in range(3):
        diag[p, c, p + 2 - c] = 1
    causal = np.zeros((P, 2, P), f)
    causal[:, 0, :] = np.where(p[:, None] > p[None, :], FAR, 0)
    causal[:, 1, :] = np.where(p[:, None] < p[None, :], FAR, 0)
    parity = np.stack([(p // HD) % 2 == 0, (p // HD) % 2 == 1], 1).astype(f)
    head_rows = (p[:, None] // HD == np.arange(HK)[None, :]).astype(f)
    upper = np.stack([p < HD2, p >= HD2], 1).astype(f)
    half_idx = np.arange(0, HD2, 2, dtype=f)
    inv = (1.0 / 10000.0 ** (half_idx / HD2)).astype(f)
    t = np.arange(T, dtype=f)
    fr = t[:, None] * inv[None, :]
    fr = np.concatenate([fr, fr], -1)
    base = ((half_idx + 0.4 * HD2) / (1.4 * HD2)).astype(f)
    sc = base[None, :] ** ((t - T // 2) / f(64))[:, None]
    sc = np.concatenate([sc, sc], -1).astype(f)
    sign = np.where(np.arange(HD2) < HD2 // 2, -1, 1).astype(f)
    cos, sin = np.cos(fr), np.sin(fr) * sign
    rot = np.stack([cos * sc * 8, sin * sc * 8, cos / sc, sin / sc], 1).astype(f)
    rot = rot.reshape(2, P, 4, HD2).transpose(1, 0, 2, 3).copy()
    return {"ident": ident, "shift": shift, "diag": diag, "causal": causal, "parity": parity, "head_rows": head_rows, "upper": upper, "rot": rot}


def kernel(**inputs):
    import concourse.bacc as _bacc
    from concourse.bass_utils import run_bass_kernel_spmd as _run

    arrays = _constants()
    plain = {k: np.asarray(v) for k, v in inputs.items()}
    arrays["x"] = plain.pop("x").reshape(STEPS, NB * T, D)
    arrays["ctxT"] = plain.pop("ctx_1024").reshape(STEPS, NB * C, D).transpose(0, 2, 1)
    arrays["mask_1x1xSxS2_ik0"] = plain.pop("mask_1x1xSxS2_ik0").reshape(T, C)
    far = plain.pop("mask_SxS_bc0")
    arrays["far"], arrays["farT"] = (np.ascontiguousarray(m).view(np.int32) for m in (far, far.T))
    for name in ("L0_xattn_Wq", "L0_xattn_Wk", "L0_xattn_Wv", "L0_xattn_Wo", "L1_ffn_W_r", "L1_ffn_W_k", "L1_ffn_W_v"):
        arrays[name] = plain.pop(name).T
    w1, b1, w2, b2 = (plain.pop(f"L0_ffn_{n}") for n in ("w1", "b1", "w2", "b2"))
    w1p = np.zeros((DEPTH, D, (2 * HF + 1) * P), np.float32)
    b1p = np.zeros((DEPTH, (2 * HF + 1) * P), np.float32)
    for j in range(HF):
        w1p[:, :, 2 * j * P:(2 * j + 1) * P] = w1[:, :, HID + j * P:HID + (j + 1) * P]
        b1p[:, 2 * j * P:(2 * j + 1) * P] = b1[:, HID + j * P:HID + (j + 1) * P]
        w1p[:, :, (2 * j + 1) * P:(2 * j + 2) * P] = w1[:, :, j * P:(j + 1) * P]
        b1p[:, (2 * j + 1) * P:(2 * j + 2) * P] = b1[:, j * P:(j + 1) * P]
    lo = 2 * HF * P
    w1p[:, :, lo:lo + HR], w1p[:, :, lo + 64:lo + 64 + HR] = w1[:, :, HF * P:HID], w1[:, :, HID + HF * P:]
    b1p[:, lo:lo + HR], b1p[:, lo + 64:lo + 64 + HR] = b1[:, HF * P:HID], b1[:, HID + HF * P:]
    w2p = np.zeros((DEPTH, (HF + 1) * P, D), np.float32)
    w2p[:, :HID] = w2
    w2p[:, HID] = b2
    arrays |= {"w1p": w1p, "w2p": w2p}
    for name in ("L0_ffn_ln_g", "L0_ffn_ln_b", "L0_xattn_bq", "L0_xattn_bk", "L1_ffn_mu_r", "L1_ffn_mu_k", "L1_xattn_ctx_b1"):
        plain[name] = np.swapaxes(plain[name].reshape(*plain[name].shape[:-1], -1, P), -1, -2)
    arrays["b1p"] = np.swapaxes(b1p.reshape(DEPTH, -1, P), -1, -2)
    plain["L1_xattn_ctx_b2"] = plain["L1_xattn_ctx_b2"].reshape(1, 1)
    arrays |= plain
    arrays = {k: np.ascontiguousarray(v) for k, v in arrays.items()}

    nc = _bacc.Bacc("TRN2", target_bir_lowering=False, num_devices=1)
    aps = {n: nc.dram_tensor(f"in_{n}", v.shape, mybir.dt.from_np(v.dtype), kind="ExternalInput").ap() for n, v in arrays.items()}
    out = nc.dram_tensor("out_0", (STEPS, NB * T, D), F32, kind="ExternalOutput").ap()
    bass_cross_local_conv_mix_kernel(nc, aps, out)
    r = _run(nc, [{f"in_{k}": v for k, v in arrays.items()}], core_ids=[0])
    return r.results[0]["out_0"].reshape(B, T, D)
```

```python
from contextlib import ExitStack

import numpy as np

import concourse.bass as bass
from concourse import mybir

F32 = mybir.dt.float32
U8 = mybir.dt.uint8
I32 = mybir.dt.int32
ALU = mybir.AluOpType
ACT = mybir.ActivationFunctionType
AX_X = mybir.AxisListType.X

P = 128
B, T, D = 32, 256, 256
KD = D // P
C = 77
H, HD = 16, 16
H2, HD2 = 8, 64
INNER = H2 * HD2
DEPTH = 2
HID = 682
HF = HID // P
HR = HID - HF * P
HIST = 512
NB = 2
STEPS = B // NB
HB = 4
HS = 2
HN = HB * HS
NT = NB * T // P
HK = P // HD
PAR = 2
GW = P + 2
EPS = 1e-5
NEG = -1e9
FAR = -1e30
ER, PR = 4, 3
SR = 3
RING = 6

ITERS = STEPS
LAG1, LAG2 = 3, 2


def local_groups(t):
    if t % 2 == 0:
        return [(par, [par, par + 2, par + 4, par + 6], [t]) for par in range(2)]
    return [(par, [par + 4 * hf, par + 4 * hf + 2], [t - 1, t]) for hf in range(2) for par in range(2)]


LOCAL = [(t, g) for t in range(NT) for g in range(len(local_groups(t)))]
MID = len(LOCAL) // 2
CROSS = [(t, r) for t in range(NT) for r in range(4)]
MID1 = len(CROSS) // 2
CONV = [(bb, h) for bb in range(NB) for h in range(H)]


def bass_cross_local_conv_mix_kernel(nc, a, out):
    with ExitStack() as ctx:
        def sb(name, shape, dt=F32):
            return ctx.enter_context(nc.sbuf_tensor(name, shape, dt))

        def sem(name):
            return ctx.enter_context(nc.semaphore(name))

        def carve(whole, lo, shape):
            n = int(np.prod(shape[1:]))
            ap = whole[0:shape[0], lo:lo + n]
            names = "abcd"[:len(shape) - 1]
            sizes = dict(zip(names, shape[1:]))
            return ap if len(shape) == 2 else ap.rearrange(f"p ({' '.join(names)}) -> p {' '.join(names)}", **sizes)

        qk_cols = sb("qk_cols", [P, 2 * 4 * NT * P + P])
        e_cols = sb("e_cols", [P, (ER + PR) * 512])
        o_cols = sb("o_cols", [P, 2 * NT * INNER])
        h_cols = sb("h_cols", [P, (2 + HF + 1) * NT * P])

        bank = [ctx.enter_context(nc.psum_tensor(f"bank{b}", [P, 512], F32)) for b in range(8)]

        W = {}
        first_loads, loads = [], []

        def weight(name, shape, src, dt=F32, at=None, first=False):
            W[name] = sb("w_" + name, shape, dt) if at is None else carve(*at, shape)
            (first_loads if first else loads).append((W[name], src))
            return W[name]

        def kmaj(ap):
            return ap.rearrange("(k p) n -> p k n", p=P)

        def column(ap, n):
            return ap.rearrange("(k p) -> p k", p=P) if n * P == ap.shape[0] else ap

        ident = weight("ident", [P, P], a["ident"], first=True)
        shiftm = weight("shift", [P, 2, P], a["shift"])
        diag = weight("diag", [P, 3, GW], a["diag"])
        causal = weight("causal", [P, 2, P], a["causal"])
        parity = weight("parity", [P, PAR], a["parity"])
        weight("head_rows", [P, HK], a["head_rows"])
        weight("upper", [P, 2], a["upper"])
        rot = weight("rot", [P, 2, 4, HD2], a["rot"])
        for name in ("L0_xattn_Wq", "L0_xattn_Wk", "L0_xattn_Wv", "L0_xattn_Wo", "L1_xattn_Wq", "L1_xattn_Wk",
                     "L1_xattn_Wv", "L1_xattn_proj_W", "L1_ffn_W_r", "L1_ffn_W_k", "L1_ffn_W_v"):
            weight(name, [P, KD, D], kmaj(a[name]))
        for l in range(DEPTH):
            weight(f"qkv{l}", [P, KD, 3 * INNER], kmaj(a["L0_ffn_wqkv"][l]))
            weight(f"wo{l}", [P, INNER // P, D], kmaj(a["L0_ffn_wo"][l]))
            weight(f"w1{l}", [P, KD, 2 * HF * P + P], kmaj(a["w1p"][l]))
            w2 = weight(f"w2{l}", [P, HF + 1, D], kmaj(a["w2p"][l]))
            weight(f"g{l}", [P, KD], a["L0_ffn_ln_g"][l])
            weight(f"b{l}", [P, KD], a["L0_ffn_ln_b"][l])
            weight(f"b1{l}", [P, 2 * HF + 1], a["b1p"][l])
            for n in ("q", "k"):
                weight(f"{n}s{l}", [P, HD2], a[f"L0_ffn_{n}_scale"][l].partition_broadcast(P))
        for name in ("L0_xattn_bq", "L0_xattn_bk", "L1_ffn_mu_r", "L1_ffn_mu_k"):
            weight(name, [P, KD], a[name])
        for name in ("L0_xattn_bv", "L0_xattn_bo", "L1_xattn_proj_b"):
            weight(name, [P, D], a[name].partition_broadcast(P))
        mask_i = weight("mask_i", [P, 2, C], a["mask_1x1xSxS2_ik0"].rearrange("(k p) n -> p k n", p=P), I32)
        weight("far_u", [P, 2, T // 4], a["far"].rearrange("(k p) n -> p k n", p=P), I32)
        weight("farT_u", [P, 2, T // 4], a["farT"].rearrange("(k p) n -> p k n", p=P), I32)
        weight("histW", [P, KD, HIST], kmaj(a["L1_xattn_hist_W"]), at=(e_cols, 0), first=True)
        weight("histb", [P, HIST], a["L1_xattn_hist_b"].partition_broadcast(P), at=(e_cols, 1024), first=True)
        weight("histg", [P, HIST], a["L1_xattn_hist_ln_g"].partition_broadcast(P), at=(e_cols, 1536), first=True)
        weight("histB", [P, HIST], a["L1_xattn_hist_ln_b"].partition_broadcast(P), at=(e_cols, 2048), first=True)
        weight("ctxW1", [P, HIST // P, P], kmaj(a["L1_xattn_ctx_W1"]), at=(qk_cols, 0), first=True)
        weight("ctxb1", [P, 1], a["L1_xattn_ctx_b1"], first=True)
        weight("ctxW2", [P, 1], a["L1_xattn_ctx_W2"], first=True)
        weight("ctxb2", [1, 1], a["L1_xattn_ctx_b2"], first=True)
        weight("kgW1", [P, HIST // P, D], kmaj(a["L1_xattn_kg_W1"]), at=(qk_cols, 512))
        weight("kgW2", [P, KD, H * 9], kmaj(a["L1_xattn_kg_W2"]), at=(qk_cols, 1536))
        weight("kgb1", [B, D], a["L1_xattn_kg_b1"].partition_broadcast(B), at=(qk_cols, 1824))
        weight("kgg", [B, D], a["L1_xattn_kg_ln_g"].partition_broadcast(B), at=(qk_cols, 2080))
        weight("kgB", [B, D], a["L1_xattn_kg_ln_b"].partition_broadcast(B), at=(qk_cols, 2336))
        weight("kgb2", [B, H * 9], a["L1_xattn_kg_b2"].partition_broadcast(B), at=(qk_cols, 2592))

        negm = sb("negm", [P, 2, C])
        far = sb("far_m", [P, 2, T])
        keepT = sb("keepT", [P, 2, T])
        rotl = sb("rotl", [P, DEPTH, 2, 4, HD2])
        bq_scaled = sb("bq_scaled", [P, KD])
        omr = sb("omr", [P, 2, KD])
        half = sb("half", [P, H2])

        xin = sb("xin", [P, NT, D])
        xn0 = carve(o_cols, 2 * NT * INNER - NT * D, [P, NT, D])
        x = sb("x", [P, NT, D])
        y = sb("y", [P, NT, D])
        xo = y
        xn = sb("xn", [P, NT, D])
        ctxT = sb("ctxT", [P, KD, NB * C])
        F = sb("F", [P, KD, NB, T + 1])
        QT = carve(h_cols, 2900, [P, KD, NB * T])
        KT1 = carve(o_cols, 0, [P, KD, NB, HK, C])
        V1 = carve(qk_cols, 0, [P, NB * KD * HK * P + P])
        E = carve(e_cols, 0, [P, ER, 512])
        PT = carve(e_cols, ER * 512, [P, PR, 512])
        stats = sb("stats", [P, NT, 2, 6])
        mv = sb("mv", [P, NT, 2])
        rstd = sb("rstd", [P, NT])
        mx = sb("mx", [P, ER, 4])
        sums = sb("sums", [P, ER, 4])
        rsums = sb("rsums", [P, ER, 4])
        rz = sb("rz", [P, 2 * H])
        sq = carve(h_cols, 0, [P, 2, INNER])
        ss = sb("ss", [P, 2, H2])
        rr = sb("rr", [P, 2, H2])
        qn = carve(h_cols, 2 * INNER, [P, 2, INNER])
        qa = carve(o_cols, 0, [P, 4, INNER])
        qb = carve(h_cols, 4 * INNER, [P, 2, INNER])
        QT2 = carve(qk_cols, 0, [P, 4, NT * P])
        KT2 = [carve(qk_cols, 4 * NT * P, [P, 4, NT * P]), carve(o_cols, NT * INNER, [P, 4, NT * P])]
        V2 = sb("V2", [P, NT, H2, HD2 + 1])
        O2 = carve(o_cols, 0, [P, NT, INNER])
        OT = carve(o_cols, NT * INNER, [P, INNER // P, NT * P])
        G = carve(h_cols, 0, [P, 2, NT * P])
        HH = carve(h_cols, 2 * NT * P, [P, HF + 1, NT * P])
        KT3 = carve(qk_cols, 0, [P, KD, PAR, NB * T])
        V3 = carve(h_cols, 1812, [P, NT, H, HD + 1])
        S0 = carve(h_cols, 0, [P, SR, 2, T + 2])
        band = carve(qk_cols, 4 * NT * P, [P, SR, 3, GW])
        diag_k = carve(o_cols, 0, [P, SR, 2, 3 * GW])
        kern = sb("kern", [P, NB, H * 9])
        XR = carve(qk_cols, 4 * NT * P, [P, 2, KD, NB * T])
        KA = carve(o_cols, 0, [P, KD, NB * T])
        sg = carve(h_cols, 0, [P, 2, D])
        kern_d = nc.dram_tensor("kernels_of_all", [B, H * 9], F32).ap()

        eh = carve(o_cols, 0, [P, HS, HB, HIST])
        ehT = carve(h_cols, 0, [P, HS, HIST // P, HB, C])
        h1 = carve(h_cols, HIST // P * HN * C, [P, HS, HB * C])
        hctx = [carve(h_cols, (HIST // P + 1) * HN * C, [P, KD, HB // NB, NB * C]),
                carve(e_cols, 5 * HIST, [P, KD, HB // NB, NB * C])]
        hstats = sb("hstats", [P, HS, HB, 6])
        hmv = sb("hmv", [P, HS, HB, 2])
        hrstd = sb("hrstd", [P, HS, HB])
        aw = sb("aw", [1, HN, C])
        awc = sb("awc", [P, HN])
        am = sb("am", [1, HN, 3])
        cc = sb("cc", [P, HIST // P, B])
        one = sb("one", [1, 1])
        spare = sb("spare", [1, 1])
        spare_a = sb("spare_a", [1, 3 + 3 * DEPTH])
        spare_v = sb("spare_v", [1, NT])
        fence = sb("fence", [1, 1])
        pool_fence = sb("pool_fence", [1, 1])
        kg = carve(h_cols, 0, [B, D])
        kgT = carve(h_cols, D, [P, KD, B])
        kp = carve(h_cols, 2 * D, [B, H, 9])
        km = sb("km", [B, 2, H])

        per_step, given = {}, {}

        def signal(name, count=1, by=1):
            s = sem(name)
            per_step[s], given[s] = (count, by), 0
            return s

        def due(s, it, n):
            count, by = per_step[s]
            return (it * count + n + 1) * by

        def own(s, it):
            given[s] += 1
            return due(s, it, given[s] - 1)

        place, fills = {}, [0] * 8
        bank_full = [sem(f"bank_full{b}") for b in range(8)]

        def full_of(key):
            return bank_full[place[key][0]]

        def full_at(key, it):
            b, n = place[key]
            return it * fills[b] + n + 1

        def bank_of(key):
            return bank[place[key][0]]

        LN = 5
        NF = 9
        first_in, weights_in, consts_set, kern_out = sem("first_in"), sem("weights_in"), sem("consts_set"), sem("kern_out")
        x_in, ctx_in, kern_in = signal("x_in", 1, 16), signal("ctx_in", 1, 16), signal("kern_in", 1, 16)
        x_out = signal("x_out", 1, 16)
        xo_ready = signal("xo_ready", NT)
        hist_in = signal("hist_in", HN // NB, 16)
        hist_go = signal("hist_go")
        hist_h, hist_T, hist_1 = signal("hist_h", HS), signal("hist_T", HS), signal("hist_1", HS)
        hist_2, hist_w, hist_c = signal("hist_2", HS), signal("hist_w"), signal("hist_c")
        hist_dve = signal("hist_dve", 4 * HS + 5)
        hist_var, hist_rstd = signal("hist_var", HS), signal("hist_rstd", HS)
        ehs_ready, eh_ready, ehT_ready, h1_ready = signal("ehs_ready", HS), signal("eh_ready", HS), signal("ehT_ready", HS), signal("h1_ready", HS)
        aws_ready, awe_ready, aw_ready, awc_ready = signal("aws_ready"), signal("awe_ready"), signal("aw_ready"), signal("awc_ready")
        cc_ready = signal("cc_ready")
        kg_1, kg_T, kg_2, kg_dve = signal("kg_1"), signal("kg_T"), signal("kg_2"), signal("kg_dve")
        kg_var, kg_rstd = signal("kg_var"), signal("kg_rstd")
        kgs_ready, kg_ready, kgT_ready = signal("kgs_ready"), signal("kg_ready"), signal("kgT_ready")
        kps_ready, kpe_ready, kp_ready = signal("kps_ready"), signal("kpe_ready"), signal("kp_ready")
        ln_stats, ln_moments = signal("ln_stats", LN * NB), signal("ln_moments", LN * NB)
        var_ready, rstd_ready = signal("var_ready", LN * NB), signal("rstd_ready", LN * NB)
        x0_ready = signal("x0_ready", NT)
        x0_stats, x0_moments, x0_var, x0_rstd = signal("x0_stats"), signal("x0_moments"), signal("x0_var"), signal("x0_rstd")
        tok_ready = signal("tok_ready", (NF - 2) * NT)

        def tok_at(n, t):
            return (n - 2) * NT + t if n < 7 else 5 * NT + t // 2 * NT + (n - 7) * 2 + t % 2

        def feat_at(n, bb):
            return NB * n + bb if n < 7 else NB * 7 + NB * bb + n - 7

        feat_a, feat_v = signal("feat_a", NF * NB), signal("feat_v", NF * NB)
        NSM = len(CROSS) + DEPTH * len(LOCAL) + len(CONV)
        sm_masked = signal("sm_masked", NSM)
        rz_ready = signal("rz_ready", DEPTH * NT * 2 + NT)
        e1_ready, p1_ready, pt1_ready = signal("e1_ready", len(CROSS)), signal("p1_ready", len(CROSS)), signal("pt1_ready", len(CROSS) // 2)
        pt1_odd = signal("pt1_odd", len(CROSS) // 2)
        e2_ready, p2_ready, pt2_ready = signal("e2_ready", DEPTH * len(LOCAL)), signal("p2_ready", DEPTH * len(LOCAL)), signal("pt2_ready", DEPTH * len(LOCAL))
        e3_ready, p3_ready, pt3_ready = signal("e3_ready", len(CONV)), signal("p3_ready", len(CONV)), signal("pt3_ready", len(CONV))
        rs1_ready = signal("rs1_ready", len(CROSS))
        pn1_ready = signal("pn1_ready", len(CROSS))
        v1_zero = signal("v1_zero")
        q1_ready = signal("q1_ready", KD)
        kv1_ready = signal("kv1_ready", 1 + NB)
        xb_ready = signal("xb_ready", NT)
        x1_ready = signal("x1_ready", NT)
        sq_ready = signal("sq_ready", DEPTH * NT * 2)
        ss_sum, ss_ready = signal("ss_sum", DEPTH * NT * 2), signal("ss_ready", DEPTH * NT * 2)
        nrm_ready = signal("nrm_ready", DEPTH * NT * 2)
        rr_ready = signal("rr_ready", DEPTH * NT * 2)
        qn_ready, qa_ready = signal("qn_ready", DEPTH * NT * 2), signal("qa_ready", DEPTH * NT * 2)
        qb_ready = signal("qb_ready", DEPTH * NT * 2)
        qr_ready, kr_ready = signal("qr_ready", DEPTH * NT), signal("kr_ready", DEPTH * NT)
        qkT_ready, v2_ready = signal("qkT_ready", DEPTH * NT * 2), signal("v2_ready", DEPTH * NT)
        o2_ready, oT_ready = signal("o2_ready", DEPTH * NT), signal("oT_ready", DEPTH * NT)
        y_ready, w2_read = signal("y_ready", DEPTH * NT), signal("w2_read", DEPTH * NT)
        ones_row = signal("ones_row", DEPTH)
        g_ready, hh_ready = signal("g_ready", DEPTH * (HF + 1)), signal("hh_ready", DEPTH * (HF + 1))
        x2_ready = signal("x2_ready", NB)
        qk3_ready, v3_ready, ones3_ready = signal("qk3_ready", 2 * KD), signal("v3_ready", NT), signal("ones3_ready")
        s0_ready = signal("s0_ready", len(CONV))
        third_ready = signal("third_ready", len(CONV))
        band_part, band_ready = signal("band_part", 2 * len(CONV)), signal("band_ready", len(CONV))
        x3_ready, x3_bias = signal("x3_ready", NB), signal("x3_bias")
        xr_part, xr_ready = signal("xr_part", 2 * NB), signal("xr_ready", 2 * NB)
        ka_part, ka_ready = signal("ka_part"), signal("ka_ready")
        ka1_part, ka1_ready = signal("ka1_part"), signal("ka1_ready")
        sg_ready, sg_part = signal("sg_ready", NT), signal("sg_part", NT)

        def tile_cols(t, shift=0):
            return slice((t % 2) * P + 1 - shift, (t % 2) * P + P + 1 - shift)

        def wide(ap, shape, axis):
            return ap.unsqueeze(axis).broadcast_to(shape)

        L = range(DEPTH)
        block = ctx.enter_context(nc.Block())

        @block.tensor
        def _(pe):
            pe.wait_ge(first_in, 16 * len(first_loads))
            pe.wait_ge(consts_set, 1)
            mm = nc.tensor.matmul
            tp = nc.tensor.transpose

            with pe.Fori(0, B // HN) as it:
                pe.wait_ge(hist_in, due(hist_in, it, HN // NB - 1))
                pe.wait_ge(hist_go, due(hist_go, it, 0))
                for j in range(HS):
                    for bb in range(HB):
                        for k in range(KD):
                            last = mm(bank[HB * j + bb][0:C, :], hctx[j][:, k, bb // NB, (bb % NB) * C:(bb % NB + 1) * C], W["histW"][:, k, :],
                                      start=k == 0, stop=k == KD - 1)
                    last.then_inc(hist_h, 1)
                for j in range(HS):
                    pe.wait_ge(eh_ready, due(eh_ready, it, j))
                    for bb in range(HB):
                        for c in range(HIST // P):
                            last = tp(bank[HB * j + bb][:, c * P:c * P + C], eh[0:C, j, bb, c * P:(c + 1) * P], ident[0:C, 0:C])
                    last.then_inc(hist_T, 1)
                for j in range(HS):
                    pe.wait_ge(ehT_ready, due(ehT_ready, it, j))
                    for c in range(HIST // P):
                        last = mm(bank[HB * j][:, 0:HB * C], W["ctxW1"][:, c, :], ehT[:, j, c, :, :].rearrange("p b n -> p (b n)"),
                                  start=c == 0, stop=c == HIST // P - 1)
                    last.then_inc(hist_1, 1)
                for j in range(HS):
                    pe.wait_ge(h1_ready, due(h1_ready, it, j))
                    mm(bank[HB * j + 1][0:1, 0:HB * C], W["ctxW2"][:, 0:1], h1[:, j, :], start=True, stop=True).then_inc(hist_2, 1)
                pe.wait_ge(aw_ready, due(aw_ready, it, 0))
                for bb in range(HN):
                    last = mm(bank[2][0:C, bb:bb + 1], aw[0:1, bb, :], one[0:1, 0:1], start=True, stop=True)
                last.then_inc(hist_w, 1)
                pe.wait_ge(awc_ready, due(awc_ready, it, 0))
                for c in range(HIST // P):
                    for bb in range(HN):
                        last = mm(bank[3][:, c * HN + bb:c * HN + bb + 1], eh[0:C, bb // HB, bb % HB, c * P:(c + 1) * P],
                                  awc[0:C, bb:bb + 1], start=True, stop=True)
                last.then_inc(hist_c, 1)
            pe.wait_ge(weights_in, 16 * len(loads))
            pe.wait_ge(consts_set, 2)
            it = 0
            pe.wait_ge(cc_ready, due(cc_ready, it, 0))
            for c in range(HIST // P):
                last = mm(bank[0][0:B, 0:D], cc[:, c, :], W["kgW1"][:, c, :], start=c == 0, stop=c == HIST // P - 1)
            last.then_inc(kg_1, 1)
            pe.wait_ge(kg_ready, due(kg_ready, it, 0))
            for k in range(KD):
                last = tp(bank[1][:, k * B:(k + 1) * B], kg[:, k * P:(k + 1) * P], ident[0:B, 0:B])
            last.then_inc(kg_T, 1)
            pe.wait_ge(kgT_ready, due(kgT_ready, it, 0))
            for k in range(KD):
                last = mm(bank[2][0:B, 0:H * 9], kgT[:, k, :], W["kgW2"][:, k, :], start=k == 0, stop=k == KD - 1)
            last.then_inc(kg_2, 1)
            pe.wait_ge(kp_ready, due(kp_ready, it, 0))

            with pe.Fori(0, ITERS) as it:
                turn, readers = [0, 0], {}

                def take(key, read, ring=0):
                    b = turn[0] % RING if ring == 0 else RING + turn[1] % (8 - RING)
                    turn[ring] += 1
                    if b in readers:
                        pe.wait_ge(readers[b][0], due(readers[b][0], it, readers[b][1]))
                    readers[b] = read
                    place[key] = (b, fills[b])
                    fills[b] += 1
                    return bank[b]

                def seq(m, bb):
                    return F[:, m, bb, 1:T + 1]

                def to_features(n, src, bb):
                    for m in range(KD):
                        b = take(("fT", n, m, bb), ((feat_a, feat_v)[m], feat_at(n, bb)))
                        for t in (2 * bb, 2 * bb + 1):
                            if m == 0 and n == 0:
                                pe.wait_ge(x0_ready, due(x0_ready, it, t))
                            elif m == 0:
                                pe.wait_ge(tok_ready, due(tok_ready, it, tok_at(n, t)))
                            last = tp(b[:, (t % 2) * P:(t % 2 + 1) * P], src[:, t, m * P:(m + 1) * P], ident[:])
                        last.then_inc(full_of(("fT", n, m, bb)), 1)

                def features_in(n, bb):
                    pe.wait_ge(feat_a, due(feat_a, it, feat_at(n, bb)))
                    pe.wait_ge(feat_v, due(feat_v, it, feat_at(n, bb)))

                def to_tokens(key, reader, w, n=D, shift=False, src=None, col=0):
                    t = key[-1]
                    b = take(key, reader)
                    for k in range(KD):
                        if src is None:
                            lhs = F[:, k, t // 2, tile_cols(t, 1 if shift and k == 1 else 0)]
                        else:
                            lhs = src(k)[:, t * P:(t + 1) * P]
                        last = mm(b[:, 0:n], lhs, w[:, k, col:col + n], start=k == 0, stop=k == KD - 1)
                    last.then_inc(full_of(key), 1)

                def to_columns(key, reader, w, m, rhs, part=None, ring=0):
                    if part in (None, 0):
                        b = take(key, reader, ring)
                    else:
                        b = bank_of(key)
                    for bb in range(NB) if part is None else (part,):
                        for k in range(KD):
                            last = mm(b[:, bb * T:(bb + 1) * T], w[:, k, m * P:(m + 1) * P], rhs(k, bb), start=k == 0, stop=k == KD - 1)
                    if part != 0:
                        last.then_inc(full_of(key), 1)

                pe.wait_ge(ctx_in, due(ctx_in, it, 0))
                b = take(("k1",), (kv1_ready, 0))
                for m in range(KD):
                    for k in range(KD):
                        last = mm(b[:, m * 256:m * 256 + NB * C], W["L0_xattn_Wk"][:, k, m * P:(m + 1) * P], ctxT[:, k, :],
                                  start=k == 0, stop=k == KD - 1)
                last.then_inc(full_of(("k1",)), 1)
                for bb in range(NB):
                    b = take(("v1", bb), (kv1_ready, 1 + bb))
                    for k in range(KD):
                        last = mm(b[0:C, 0:D], ctxT[:, k, bb * C:(bb + 1) * C], W["L0_xattn_Wv"][:, k, :],
                                  start=k == 0, stop=k == KD - 1)
                    last.then_inc(full_of(("v1", bb)), 1)
                for bb in range(NB):
                    to_features(0, xn0, bb)
                for bb in range(NB):
                    features_in(0, bb)
                    for m in range(KD):
                        to_columns(("q1", m), (q1_ready, m), W["L0_xattn_Wq"], m, seq, part=bb)
                pe.wait_ge(q1_ready, due(q1_ready, it, KD - 1))
                pe.wait_ge(kv1_ready, due(kv1_ready, it, NB))
                for u in range(-LAG1, len(CROSS) + 1):
                    if u == MID1 + 3:
                        features_in(1, 0)
                        for t in range(2):
                            to_tokens(("o1", t), (x1_ready, t), W["L0_xattn_Wo"])
                    if u + LAG1 < len(CROSS):
                        t, r = CROSS[u + LAG1]
                        b = take(("s1", u + LAG1), (e1_ready, u + LAG1))
                        m, lo = 4 * r // HK, 4 * r % HK
                        mm(b[:, 0:4 * C], QT[:, m, t * P:(t + 1) * P], KT1[:, m, t // 2, lo:lo + 4, :].rearrange("p a n -> p (a n)"),
                           start=True, stop=True).then_inc(full_of(("s1", u + LAG1)), 1)
                    if 0 <= u < len(CROSS):
                        b = take(("t1", u), ((pt1_ready, pt1_odd)[u % 2], u // 2))
                        pe.wait_ge(pn1_ready, due(pn1_ready, it, u))
                        for i in range(4):
                            last = tp(b[0:C, i * P:(i + 1) * P], E[:, u % ER, i * C:(i + 1) * C], ident[:])
                        last.then_inc(full_of(("t1", u)), 1)
                    if u >= 1:
                        t, r = CROSS[u - 1]
                        m = 4 * r // HK
                        if r == 0 and t % 2 == 0:
                            z = [take(("fT", 1, k, t // 2), ((feat_a, feat_v)[k], NB + t // 2), ring=1) for k in range(KD)]
                        if u % 2:
                            pe.wait_ge(pt1_ready, due(pt1_ready, it, (u - 1) // 2))
                        else:
                            pe.wait_ge(pt1_odd, due(pt1_odd, it, (u - 1) // 2))
                        for i in range(4):
                            h = 4 * r + i
                            col = ((t // 2) * H + h) * P
                            last = mm(z[m][:, (t % 2) * P:(t % 2 + 1) * P], V1[0:C, col:col + P], PT[0:C, (u - 1) % PR, i * P:(i + 1) * P],
                                      start=h % HK == 0, stop=h % HK == HK - 1)
                        if t % 2 == 1 and h % HK == HK - 1:
                            last.then_inc(full_of(("fT", 1, m, t // 2)), 1)
                to_features(2, y, 0)
                features_in(1, 1)
                for t in range(2, NT):
                    to_tokens(("o1", t), (x1_ready, t), W["L0_xattn_Wo"])

                for l in L:
                    if l > 0:
                        to_features(2 + 2 * l, y, 0)
                    features_in(2 + 2 * l, 0)

                    def turn_qk(t):
                        for i, k in enumerate(("qT", "kT")):
                            n = l * 2 * NT + 2 * t + i
                            if i == 0:
                                pe.wait_ge(qr_ready, due(qr_ready, it, l * NT + t))
                            else:
                                pe.wait_ge(kr_ready, due(kr_ready, it, l * NT + t))
                            b = take((k, l, t), (qkT_ready, n), ring=int(t < 2))
                            for hp in range(4):
                                last = tp(b[:, hp * P:(hp + 1) * P], qa[:, n % 4, hp * P:(hp + 1) * P], ident[:])
                            last.then_inc(full_of((k, l, t)), 1)

                    for t in range(NT):
                        if t == 1:
                            to_features(2 + 2 * l, y, 1)
                        if t == 2:
                            features_in(2 + 2 * l, 1)
                        for i, k in enumerate(("q2", "k2", "v2")):
                            reader = (v2_ready, l * NT + t) if i == 2 else (qn_ready, l * 2 * NT + 2 * t + i)
                            to_tokens((k, l, t), reader, W[f"qkv{l}"], n=INNER, shift=True, col=i * INNER)
                        if t >= 2:
                            turn_qk(t - 2)
                    pe.wait_ge(v2_ready, due(v2_ready, it, l * NT + NT - 1))
                    n = 3 + 2 * l

                    def turn_heads(bb):
                        for t in (2 * bb, 2 * bb + 1):
                            pe.wait_ge(o2_ready, due(o2_ready, it, l * NT + t))
                            b = take(("oT", l, t), (oT_ready, l * NT + t))
                            for k in range(INNER // P):
                                last = tp(b[:, k * P:(k + 1) * P], O2[:, t, k * P:(k + 1) * P], ident[:])
                            last.then_inc(full_of(("oT", l, t)), 1)

                    def project(bb):
                        for t in (2 * bb, 2 * bb + 1):
                            pe.wait_ge(oT_ready, due(oT_ready, it, l * NT + t))
                            b = take(("wo", l, t), (y_ready, l * NT + t))
                            for k in range(INNER // P):
                                last = mm(b[:, 0:D], OT[:, k, t * P:(t + 1) * P], W[f"wo{l}"][:, k, :],
                                          start=k == 0, stop=k == INNER // P - 1)
                            last.then_inc(full_of(("wo", l, t)), 1)

                    def shift(bb):
                        b = take(("sh", l, bb), (tok_ready, tok_at(n, 2 * bb + 1)))
                        t = 2 * bb
                        pe.wait_ge(y_ready, due(y_ready, it, l * NT + t + 1))
                        mm(b[:, 0:P], shiftm[:, 0, :], y[:, t, P:D], start=True, stop=True)
                        mm(b[:, P:2 * P], shiftm[:, 0, :], y[:, t + 1, P:D], start=True, stop=False)
                        mm(b[:, P:2 * P], shiftm[:, 1, :], y[:, t, P:D], start=False, stop=True).then_inc(full_of(("sh", l, bb)), 1)

                    def columns(j, bb):
                        for i, k in enumerate(("g", "a")):
                            to_columns((k, l, j), (hh_ready, l * (HF + 1) + j), W[f"w1{l}"], 2 * j + i, seq, part=bb, ring=j)

                    for u in range(-LAG2, len(LOCAL) + 1):
                        if u == MID + 4:
                            project(0)
                        if u == MID + 6:
                            shift(0)
                        if u + LAG2 < len(LOCAL):
                            t, g = LOCAL[u + LAG2]
                            if g == 0:
                                pe.wait_ge(qkT_ready, due(qkT_ready, it, l * 2 * NT + 2 * t + 1))
                            b = take(("s2", l, u + LAG2), (e2_ready, l * len(LOCAL) + u + LAG2))
                            par, heads, tiles = local_groups(t)[g]
                            w = P * len(tiles)
                            for i, h in enumerate(heads):
                                last = mm(b[:, i * w:(i + 1) * w], QT2[:, h // 2, t * P:(t + 1) * P],
                                          KT2[par][:, h // 2, tiles[0] * P:tiles[0] * P + w], start=True, stop=True)
                            last.then_inc(full_of(("s2", l, u + LAG2)), 1)
                        if 0 <= u < len(LOCAL):
                            b = take(("t2", l, u), (pt2_ready, l * len(LOCAL) + u))
                            pe.wait_ge(p2_ready, due(p2_ready, it, l * len(LOCAL) + u))
                            for i in range(4):
                                last = tp(b[:, i * P:(i + 1) * P], E[:, u % ER, i * P:(i + 1) * P], ident[:])
                            last.then_inc(full_of(("t2", l, u)), 1)
                        if u in (0, 2):
                            turn_qk(NT - 2 + u // 2)
                        if u >= 1:
                            t, g = LOCAL[u - 1]
                            if g == 0:
                                zs = [take(("z2", l, t, hf), (o2_ready, l * NT + t), ring=1) for hf in range(2)]
                            pe.wait_ge(pt2_ready, due(pt2_ready, it, l * len(LOCAL) + u - 1))
                            par, heads, tiles = local_groups(t)[g]
                            blk = 0
                            for h in heads:
                                for j, kt in enumerate(tiles):
                                    last = mm(zs[h // 4][:, (h % 4) * (HD2 + 1):(h % 4 + 1) * (HD2 + 1)],
                                              PT[:, (u - 1) % PR, blk * P:(blk + 1) * P], V2[:, kt, h, :],
                                              start=j == 0, stop=j == len(tiles) - 1)
                                    blk += 1
                                if h in (3, 7):
                                    last.then_inc(full_of(("z2", l, t, h // 4)), 1)
                        if u == MID + 2:
                            turn_heads(0)
                    turn_heads(1)
                    to_features(n, xn, 0)
                    project(1)
                    features_in(n, 0)
                    shift(1)
                    columns(0, 0)
                    columns(1, 0)
                    to_features(n, xn, 1)
                    features_in(n, 1)
                    columns(0, 1)
                    columns(1, 1)
                    for j in range(2, HF):
                        for i, k in enumerate(("g", "a")):
                            to_columns((k, l, j), (hh_ready, l * (HF + 1) + j), W[f"w1{l}"], 2 * j + i, seq)
                    to_columns(("r", l), (hh_ready, l * (HF + 1) + HF), W[f"w1{l}"], 2 * HF, seq)
                    for t in range(NT):
                        b = take(("w2", l, t), (w2_read, l * NT + t))
                        for k in range(HF + 1):
                            if t == 0:
                                pe.wait_ge(hh_ready, due(hh_ready, it, l * (HF + 1) + k))
                            r = P if k < HF else HR + 1
                            last = mm(b[:, 0:D], HH[0:r, k, t * P:(t + 1) * P], W[f"w2{l}"][0:r, k, :],
                                      start=k == 0, stop=k == HF)
                        last.then_inc(full_of(("w2", l, t)), 1)

                for bb in range(NB):
                    to_features(6, xn, bb)
                    features_in(6, bb)
                    for m in range(KD):
                        to_columns(("q3", m), (qk3_ready, m), W["L1_xattn_Wq"], m, seq, part=bb)
                    for m in range(KD):
                        to_columns(("k3", m), (qk3_ready, KD + m), W["L1_xattn_Wk"], m, seq, part=bb)
                for t in range(NT):
                    to_tokens(("v3", t), (v3_ready, t), W["L1_xattn_Wv"])
                pe.wait_ge(qk3_ready, due(qk3_ready, it, 2 * KD - 1))
                pe.wait_ge(v3_ready, due(v3_ready, it, NT - 1))
                pe.wait_ge(ones3_ready, due(ones3_ready, it, 0))
                for u in range(-2, len(CONV) + 1):
                    if u + 2 < len(CONV):
                        bb, h = CONV[u + 2]
                        b = take(("s3", u + 2), (s0_ready, u + 2))
                        r = (h // 2) % 4
                        rows = slice(32 * r, 32 * r + 32)
                        for jt in range(2):
                            last = mm(b[:, jt * T:(jt + 1) * T],
                                      KT3[rows, h // 8, h % 2, bb * T + jt * P:bb * T + (jt + 1) * P],
                                      QT[rows, h // 8, bb * T:(bb + 1) * T], start=True, stop=True)
                        last.then_inc(full_of(("s3", u + 2)), 1)
                    if 0 <= u + 1 < len(CONV):
                        b = take(("c3", u + 1), (e3_ready, u + 1))
                        pe.wait_ge(band_ready, due(band_ready, it, u + 1))
                        pe.wait_ge(s0_ready, due(s0_ready, it, u + 1))
                        for i2 in range(2):
                            n = 0
                            for jt in range(2):
                                for tap in range(3):
                                    lo = jt * (P - 1)
                                    last = mm(b[:, i2 * T + lo:i2 * T + lo + P + 1],
                                              S0[:, (u + 1) % SR, jt, i2 * P + tap:i2 * P + tap + P],
                                              band[:, (u + 1) % SR, tap, 1 - jt:1 - jt + P + 1],
                                              start=n == 0, stop=n == 5, skip_group_check=True)
                                    n += 1
                        last.then_inc(full_of(("c3", u + 1)), 1)
                    if 0 <= u < len(CONV):
                        b = take(("t3", u), (pt3_ready, u))
                        pe.wait_ge(p3_ready, due(p3_ready, it, u))
                        for jt in range(2):
                            for i2 in range(2):
                                last = tp(b[:, (jt * 2 + i2) * P:(jt * 2 + i2 + 1) * P],
                                          E[:, u % ER, i2 * T + jt * P:i2 * T + (jt + 1) * P], ident[:])
                        last.then_inc(full_of(("t3", u)), 1)
                    if u >= 1:
                        bb, h = CONV[u - 1]
                        if h == 0:
                            zs = [take(("z3", bb, i2), (tok_ready, tok_at(7, 2 * bb + i2)), ring=1) for i2 in range(2)]
                        pe.wait_ge(pt3_ready, due(pt3_ready, it, u - 1))
                        for i2 in range(2):
                            for jt in range(2):
                                last = mm(zs[i2][:, h * (HD + 1):(h + 1) * (HD + 1)],
                                          PT[:, (u - 1) % PR, (jt * 2 + i2) * P:(jt * 2 + i2 + 1) * P],
                                          V3[:, 2 * bb + jt, h, :], start=jt == 0, stop=jt == 1)
                            if h == H - 1:
                                last.then_inc(full_of(("z3", bb, i2)), 1)
                    if u == H + 2:
                        to_features(7, xn, 0)
                    if u == H + 4:
                        features_in(7, 0)
                        for t in range(2):
                            to_tokens(("p3", t), (x3_ready, 0), W["L1_xattn_proj_W"])
                    if u == H + 11:
                        to_features(8, xn, 0)
                to_features(7, xn, 1)
                features_in(7, 1)
                for t in range(2, NT):
                    to_tokens(("p3", t), (x3_ready, 1), W["L1_xattn_proj_W"])

                for bb in range(NB):
                    if bb == 1:
                        to_features(8, xn, 1)
                    pe.wait_ge(xr_ready, due(xr_ready, it, 2 * bb))
                    for m in range(KD):
                        to_columns(("kk", m), ((ka_ready, ka1_ready)[m], 0), W["L1_ffn_W_k"], m, lambda k, bb: XR[:, 0, k, bb * T:(bb + 1) * T], part=bb, ring=1)
                    pe.wait_ge(xr_ready, due(xr_ready, it, 2 * bb + 1))
                    for t in (2 * bb, 2 * bb + 1):
                        to_tokens(("r4", t), (sg_ready, t), W["L1_ffn_W_r"], src=lambda k: XR[:, 1, k, :])
                pe.wait_ge(ka_ready, due(ka_ready, it, 0))
                pe.wait_ge(ka1_ready, due(ka1_ready, it, 0))
                for t in range(NT):
                    to_tokens(("v4", t), (sg_part, t), W["L1_ffn_W_v"], src=lambda k: KA[:, k, :])
                pe.wait_ge(sg_ready, due(sg_ready, it, NT - 1))
                pe.wait_ge(sg_part, due(sg_part, it, NT - 1))

        @block.scalar
        def _(act):
            act.wait_ge(first_in, 16 * len(first_loads))
            f, copy = nc.scalar.activation, nc.scalar.copy
            with act.Fori(0, B // HN) as it:
                for j in range(HS):
                    act.wait_ge(ehs_ready, due(ehs_ready, it, j))
                    f(eh[0:C, j], eh[0:C, j], ACT.Gelu).then_inc(eh_ready, 1)
                for j in range(HS):
                    act.wait_ge(hist_1, due(hist_1, it, j))
                    f(h1[:, j, :], bank[HB * j][:, 0:HB * C], ACT.Gelu, bias=W["ctxb1"][:, 0:1]).then_inc(h1_ready, 1)
                act.wait_ge(aws_ready, due(aws_ready, it, 0))
                f(aw[:], aw[:], ACT.Exp).then_inc(awe_ready, 1)
            it = 0
            act.wait_ge(weights_in, 16 * len(loads))
            act.wait_ge(consts_set, 2)
            act.wait_ge(kgs_ready, due(kgs_ready, it, 0))
            f(kg[:], kg[:], ACT.Gelu).then_inc(kg_ready, 1)
            act.wait_ge(kps_ready, due(kps_ready, it, 0))
            f(kp[:], kp[:], ACT.Exp).then_inc(kpe_ready, 1)

            with act.Fori(0, ITERS) as it:

                uses = iter(range(3 + 3 * DEPTH))

                def ahead(func):
                    c = next(uses)
                    f(spare_a[:, c:c + 1], one[0:1, 0:1], func)

                def features(n, bb, l=None):
                    act.wait_ge(full_of(("fT", n, 0, bb)), full_at(("fT", n, 0, bb), it))
                    src = bank_of(("fT", n, 0, bb))[:, 0:T]
                    if l is None:
                        ins = copy(F[:, 0, bb, 1:T + 1], src)
                    else:
                        ins = f(F[:, 0, bb, 1:T + 1], src, ACT.Identity, bias=W[f"b{l}"][:, 0:1], scale=W[f"g{l}"][:, 0:1])
                    ins.then_inc(feat_a, 1)

                def exponentials(u, n, groups, width, scores, probs, total=None):
                    act.wait_ge(scores, due(scores, it, n))
                    for g in range(groups):
                        e = E[:, u % ER, g * width:(g + 1) * width]
                        if total is None:
                            last = f(e, e, ACT.Exp, bias=mx[:, u % ER, g:g + 1])
                        else:
                            last = f(e, e, ACT.Exp, bias=mx[:, u % ER, g:g + 1], accum_out=total[:, u % ER, g:g + 1])
                    last.then_inc(probs, 1)

                def turned(u, key, rows, probs_turned):
                    act.wait_ge(full_of(key), full_at(key, it))
                    copy(PT[0:rows, u % PR, :], bank_of(key)[0:rows, :]).then_inc(probs_turned, 1)

                ahead(ACT.Exp)
                features(0, 0)
                features(0, 1)
                for m in range(KD):
                    act.wait_ge(full_of(("q1", m)), full_at(("q1", m), it))
                    f(QT[:, m, :], bank_of(("q1", m))[:, :], ACT.Identity, bias=bq_scaled[:, m:m + 1], scale=HD ** -0.5).then_inc(q1_ready, 1)
                for u in range(len(CROSS) + 2):
                    if u < len(CROSS):
                        exponentials(u, u, 4, C, e1_ready, p1_ready, sums)
                    if u >= 2 and u % 2 == 0:
                        turned(u - 2, ("t1", u - 2), C, pt1_ready)
                    if u == MID1 + 1:
                        features(1, 0)
                features(1, 1)
                for l in L:
                    features(2 + 2 * l, 0)
                    ahead(ACT.Sqrt)

                    def turn_qk(t):
                        act.wait_ge(full_of(("qT", l, t)), full_at(("qT", l, t), it))
                        copy(QT2[:, :, t * P:(t + 1) * P], bank_of(("qT", l, t))[:, :].rearrange("p (h t) -> p h t", h=4)).then_inc(qkT_ready, 1)
                        act.wait_ge(full_of(("kT", l, t)), full_at(("kT", l, t), it))
                        b = bank_of(("kT", l, t))
                        for par in range(2):
                            last = f(KT2[par][:, :, t * P:(t + 1) * P], b[:, :].rearrange("p (h t) -> p h t", h=4), ACT.Copy, scale=W["upper"][:, par:par + 1])
                        last.then_inc(qkT_ready, 1)

                    for t in range(NT):
                        for i, k in enumerate(("q2", "k2")):
                            act.wait_ge(full_of((k, l, t)), full_at((k, l, t), it))
                            b = bank_of((k, l, t))
                            if t >= 1:
                                act.wait_ge(ss_sum, due(ss_sum, it, l * 2 * NT + 2 * (t - 1) + i))
                            f(sq[:, i, :], b[:, :], ACT.Square).then_inc(sq_ready, 1)
                        act.wait_ge(full_of(("v2", l, t)), full_at(("v2", l, t), it))
                        b = bank_of(("v2", l, t))
                        copy(V2[:, t, :, 0:HD2], b[:, :].rearrange("p (h d) -> p h d", h=H2)).then_inc(v2_ready, 1)
                        for i in range(2):
                            n = l * 2 * NT + 2 * t + i
                            act.wait_ge(ss_ready, due(ss_ready, it, n))
                            if t >= 1:
                                act.wait_ge(qn_ready, due(qn_ready, it, n - 2))
                            f(rr[:, i, :], ss[:, i, :], ACT.Sqrt).then_inc(nrm_ready, 1)
                        if t == 0:
                            features(2 + 2 * l, 1)
                        if t >= 2:
                            turn_qk(t - 2)
                    ahead(ACT.Exp)

                    def heads_turned(bb):
                        for t in (2 * bb, 2 * bb + 1):
                            act.wait_ge(full_of(("oT", l, t)), full_at(("oT", l, t), it))
                            b = bank_of(("oT", l, t))
                            copy(OT[:, :, t * P:(t + 1) * P], b[:, :].rearrange("p (k t) -> p k t", k=INNER // P)).then_inc(oT_ready, 1)

                    for u in range(len(LOCAL) + 1):
                        if u < len(LOCAL):
                            heads = len(local_groups(LOCAL[u][0])[0][1])
                            exponentials(u, l * len(LOCAL) + u, heads, 512 // heads, e2_ready, p2_ready)
                        if u >= 1:
                            turned(u - 1, ("t2", l, u - 1), P, pt2_ready)
                        if u in (1, 3):
                            turn_qk(NT - 2 + u // 2)
                        if u == MID + 3:
                            heads_turned(0)
                    heads_turned(1)
                    ahead(ACT.Gelu)
                    features(3 + 2 * l, 0, l)
                    features(3 + 2 * l, 1, l)
                    for j in range(HF):
                        act.wait_ge(full_of(("g", l, j)), full_at(("g", l, j), it))
                        b = bank_of(("g", l, j))
                        if j >= 2:
                            act.wait_ge(hh_ready, due(hh_ready, it, l * (HF + 1) + j - 2))
                        f(G[:, j % 2, :], b[:, :], ACT.Gelu, bias=W[f"b1{l}"][:, 2 * j:2 * j + 1]).then_inc(g_ready, 1)
                    act.wait_ge(full_of(("r", l)), full_at(("r", l), it))
                    b = bank_of(("r", l))
                    act.wait_ge(hh_ready, due(hh_ready, it, l * (HF + 1) + HF - 2))
                    f(G[0:HR, HF % 2, :], b[64:64 + HR, :], ACT.Gelu, bias=W[f"b1{l}"][64:64 + HR, 2 * HF:2 * HF + 1]).then_inc(g_ready, 1)
                features(6, 0)
                features(6, 1)
                ahead(ACT.Exp)
                for t in range(NT):
                    act.wait_ge(full_of(("v3", t)), full_at(("v3", t), it))
                    b = bank_of(("v3", t))
                    copy(V3[:, t, :, 0:HD], b[:, 0:D].rearrange("p (h d) -> p h d", h=H)).then_inc(v3_ready, 1)

                def third_diagonal(u):
                    bb, h = CONV[u]
                    if u >= SR:
                        act.wait_ge(full_of(("c3", u - SR)), full_at(("c3", u - SR), it))
                    for tap in range(3):
                        k = h * 9 + tap * 3 + 2
                        last = f(diag_k[:, u % SR, 1, tap * GW:(tap + 1) * GW], diag[:, 2, :], ACT.Copy, scale=kern[:, bb, k:k + 1])
                    last.then_inc(third_ready, 1)

                act.wait_ge(kern_in, due(kern_in, it, 0))
                for u in range(SR):
                    third_diagonal(u)
                for u in range(len(CONV) + 1):
                    if u < len(CONV):
                        exponentials(u, u, 2, T, e3_ready, p3_ready)
                    if u >= 1:
                        turned(u - 1, ("t3", u - 1), P, pt3_ready)
                    if u + SR < len(CONV):
                        third_diagonal(u + SR)
                    if u == H + 3:
                        features(7, 0)
                    if u == H + 12:
                        features(8, 0)

                def mixed(bb):
                    act.wait_ge(feat_a, due(feat_a, it, feat_at(8, bb)))
                    act.wait_ge(feat_v, due(feat_v, it, feat_at(8, bb)))
                    for i in range(2):
                        for k in range(KD):
                            last = f(XR[:, i, k, bb * T:(bb + 1) * T], F[:, k, bb, 0:T], ACT.Copy, scale=omr[:, i, k:k + 1])
                        last.then_inc(xr_part, 1)

                def gates(bb):
                    for t in (2 * bb, 2 * bb + 1):
                        act.wait_ge(full_of(("r4", t)), full_at(("r4", t), it))
                        b = bank_of(("r4", t))
                        if t >= 2:
                            act.wait_ge(xo_ready, due(xo_ready, it, t - 2))
                        f(sg[:, t % 2, :], b[:, 0:D], ACT.Sigmoid).then_inc(sg_ready, 1)

                mixed(0)
                ahead(ACT.Sigmoid)
                features(7, 1)
                gates(0)
                features(8, 1)
                mixed(1)
                act.wait_ge(full_of(("kk", 1)), full_at(("kk", 1), it))
                f(KA[:, 1, :], bank_of(("kk", 1))[:, :], ACT.Relu).then_inc(ka1_part, 1)
                act.wait_ge(ka1_part, due(ka1_part, it, 0))
                f(KA[:, 1, :], KA[:, 1, :], ACT.Square).then_inc(ka1_ready, 1)
                gates(1)

        @block.vector
        def _(dve):
            dve.wait_ge(first_in, 16 * len(first_loads))
            v = nc.vector
            tt, ts, stt = v.tensor_tensor, v.tensor_scalar, v.scalar_tensor_tensor
            with dve.Fori(0, B // HN) as it:
                v.tensor_copy(spare_v[:, 0:1], ident[0:1, 0:1]).then_inc(hist_go, 1)
                for j in range(HS):
                    dve.wait_ge(hist_h, due(hist_h, it, j))
                    for bb in range(HB):
                        last = tt(eh[0:C, j, bb, :], bank[HB * j + bb][0:C, :], W["histb"][0:C], ALU.add)
                    last.then_inc(hist_dve, 1)
                    dve.wait_ge(hist_dve, own(hist_dve, it))
                    for bb in range(HB):
                        last = v.bn_stats(hstats[0:C, j, bb, :], eh[0:C, j, bb, :])
                    last.then_inc(hist_dve, 1)
                    dve.wait_ge(hist_dve, own(hist_dve, it))
                    v.memset(fence[:], 0.0)
                    for bb in range(HB):
                        last = v.bn_aggr(hmv[0:C, j, bb, :], hstats[0:C, j, bb, :])
                    last.then_inc(hist_dve, 1)
                    dve.wait_ge(hist_dve, own(hist_dve, it))
                    ts(hrstd[0:C, j, :], hmv[0:C, j, :, 1], EPS, None, ALU.add).then_inc(hist_var, 1)
                    for bb in range(HB):
                        last = stt(eh[0:C, j, bb, :], eh[0:C, j, bb, :], hmv[0:C, j, bb, 0:1], W["histg"][0:C], ALU.subtract, ALU.mult)
                    last.then_inc(hist_dve, 1)
                    dve.wait_ge(hist_rstd, due(hist_rstd, it, j))
                    dve.wait_ge(hist_dve, own(hist_dve, it))
                    for bb in range(HB):
                        last = stt(eh[0:C, j, bb, :], eh[0:C, j, bb, :], hrstd[0:C, j, bb:bb + 1], W["histB"][0:C], ALU.mult, ALU.add)
                    last.then_inc(ehs_ready, 1)
                for j in range(HS):
                    dve.wait_ge(hist_T, due(hist_T, it, j))
                    for bb in range(HB):
                        last = v.tensor_copy(ehT[:, j, :, bb, :], bank[HB * j + bb][:, :].rearrange("p (c n) -> p c n", c=HIST // P)[:, :, 0:C])
                    last.then_inc(ehT_ready, 1)
                for j in range(HS):
                    dve.wait_ge(hist_2, due(hist_2, it, j))
                    last = ts(aw[0:1, HB * j:HB * (j + 1)].rearrange("p b n -> p (b n)"), bank[HB * j + 1][0:1, 0:HB * C], W["ctxb2"][0:1, 0:1], None, ALU.add)
                last.then_inc(hist_dve, 1)
                dve.wait_ge(hist_dve, own(hist_dve, it))
                v.tensor_reduce(am[0:1, :, 0], aw[0:1], AX_X, ALU.max).then_inc(hist_dve, 1)
                dve.wait_ge(hist_dve, own(hist_dve, it))
                tt(aw[0:1], aw[0:1], am[0:1, :, 0:1].broadcast_to([1, HN, C]), ALU.subtract).then_inc(aws_ready, 1)
                dve.wait_ge(awe_ready, due(awe_ready, it, 0))
                v.tensor_reduce(am[0:1, :, 1], aw[0:1], AX_X, ALU.add).then_inc(hist_dve, 1)
                dve.wait_ge(hist_dve, own(hist_dve, it))
                v.reciprocal(am[0:1, :, 2], am[0:1, :, 1]).then_inc(hist_dve, 1)
                dve.wait_ge(hist_dve, own(hist_dve, it))
                tt(aw[0:1], aw[0:1], am[0:1, :, 2:3].broadcast_to([1, HN, C]), ALU.mult).then_inc(aw_ready, 1)
                dve.wait_ge(hist_w, due(hist_w, it, 0))
                v.tensor_copy(awc[0:C, :], bank[2][0:C, 0:HN]).then_inc(awc_ready, 1)
                dve.wait_ge(hist_c, due(hist_c, it, 0))
                v.tensor_copy(cc[:, :, bass.ds(it * HN, HN)],
                              bank[3][:, 0:HIST // P * HN].rearrange("p (c b) -> p c b", b=HN)).then_inc(hist_dve, 1)
                dve.wait_ge(hist_dve, own(hist_dve, it))

            dve.wait_ge(weights_in, 16 * len(loads))
            ts(negm[:], W["mask_i"][:], 0.0, NEG, ALU.is_equal, ALU.mult)
            ts(far[:], W["far_u"][:].bitcast(U8), FAR, None, ALU.mult)
            ts(keepT[:], W["farT_u"][:].bitcast(U8), -1.0, 1.0, ALU.mult, ALU.add)
            for l in range(DEPTH):
                for hf in range(2):
                    for i, n in enumerate(("q", "k")):
                        sc = W[f"{n}s{l}"]
                        tt(rotl[:, l, hf, 2 * i, :], rot[:, hf, 2 * i, :], sc[:], ALU.mult)
                        for lo, hi in ((0, HD2 // 2), (HD2 // 2, 0)):
                            tt(rotl[:, l, hf, 2 * i + 1, lo:lo + HD2 // 2], rot[:, hf, 2 * i + 1, lo:lo + HD2 // 2],
                               sc[:, hi:hi + HD2 // 2], ALU.mult)
            ts(bq_scaled[:], W["L0_xattn_bq"][:], HD ** -0.5, None, ALU.mult)
            for i, n in enumerate(("k", "r")):
                last = ts(omr[:, i, :], W[f"L1_ffn_mu_{n}"][:], -1.0, 1.0, ALU.mult, ALU.add)
            last.then_inc(consts_set, 1)
            dve.wait_ge(consts_set, 2)
            it = 0
            v.tensor_copy(spare_v[:, 0:1], ident[0:1, 0:1]).then_inc(cc_ready, 1)
            dve.wait_ge(kg_1, due(kg_1, it, 0))
            tt(kg[:], bank[0][0:B, 0:D], W["kgb1"][:], ALU.add).then_inc(kg_dve, 1)
            dve.wait_ge(kg_dve, own(kg_dve, it))
            v.bn_stats(stats[0:B, 0, 0, :], kg[:]).then_inc(kg_dve, 1)
            dve.wait_ge(kg_dve, own(kg_dve, it))
            v.bn_aggr(mv[0:B, 0, :], stats[0:B, 0, 0, :]).then_inc(kg_dve, 1)
            dve.wait_ge(kg_dve, own(kg_dve, it))
            ts(rstd[0:B, 0:1], mv[0:B, 0, 1:2], EPS, None, ALU.add).then_inc(kg_var, 1)
            dve.wait_ge(kg_rstd, due(kg_rstd, it, 0))
            ts(kg[:], kg[:], mv[0:B, 0, 0:1], rstd[0:B, 0:1], ALU.subtract, ALU.mult).then_inc(kg_dve, 1)
            dve.wait_ge(kg_dve, own(kg_dve, it))
            tt(kg[:], kg[:], W["kgg"][:], ALU.mult).then_inc(kg_dve, 1)
            dve.wait_ge(kg_dve, own(kg_dve, it))
            tt(kg[:], kg[:], W["kgB"][:], ALU.add).then_inc(kgs_ready, 1)
            dve.wait_ge(kg_T, due(kg_T, it, 0))
            v.tensor_copy(kgT[:], bank[1][:, 0:KD * B].rearrange("p (k b) -> p k b", k=KD)).then_inc(kgT_ready, 1)
            dve.wait_ge(kg_2, due(kg_2, it, 0))
            tt(kp[:].rearrange("b h n -> b (h n)"), bank[2][0:B, 0:H * 9], W["kgb2"][:], ALU.add).then_inc(kg_dve, 1)
            dve.wait_ge(kg_dve, own(kg_dve, it))
            v.tensor_reduce(km[:, 0, :], kp[:], AX_X, ALU.max).then_inc(kg_dve, 1)
            dve.wait_ge(kg_dve, own(kg_dve, it))
            tt(kp[:], kp[:], wide(km[:, 0, :], [B, H, 9], 2), ALU.subtract).then_inc(kps_ready, 1)
            dve.wait_ge(kpe_ready, due(kpe_ready, it, 0))
            v.tensor_reduce(km[:, 0, :], kp[:], AX_X, ALU.add).then_inc(kg_dve, 1)
            dve.wait_ge(kg_dve, own(kg_dve, it))
            v.reciprocal(km[:, 1, :], km[:, 0, :]).then_inc(kg_dve, 1)
            dve.wait_ge(kg_dve, own(kg_dve, it))
            tt(kp[:], kp[:], wide(km[:, 1, :], [B, H, 9], 2), ALU.mult).then_inc(kp_ready, 1)

            def first_moments(step):
                dve.wait_ge(x_in, due(x_in, step, 0))
                for t in range(NT):
                    for i in range(2):
                        last = v.bn_stats(stats[:, t, i, :], xin[:, t, i * P:(i + 1) * P])
                last.then_inc(x0_stats, 1)
                dve.wait_ge(x0_stats, due(x0_stats, step, 0))
                v.memset(fence[:], 0.0)
                for t in range(NT):
                    last = v.bn_aggr(mv[:, t, :], stats[:, t].rearrange("p a b -> p (a b)"))
                last.then_inc(x0_moments, 1)
                dve.wait_ge(x0_moments, due(x0_moments, step, 0))
                ts(rstd[:], mv[:, :, 1], EPS, None, ALU.add).then_inc(x0_var, 1)

            def first_normalised(step):
                dve.wait_ge(x0_rstd, due(x0_rstd, step, 0))
                for t in range(NT):
                    ts(xn0[:, t, :], xin[:, t, :], mv[:, t, 0:1], rstd[:, t:t + 1], ALU.subtract, ALU.mult).then_inc(x0_ready, 1)

            first_moments(0)
            first_normalised(0)
            with dve.Fori(0, ITERS) as it:

                def moments(n, bb, halves):
                    for t in (2 * bb, 2 * bb + 1):
                        for i, part in enumerate(halves(t)):
                            last = v.bn_stats(stats[:, t, i, :], part)
                    last.then_inc(ln_stats, 1)
                    dve.wait_ge(ln_stats, own(ln_stats, it))
                    v.memset(fence[:], 0.0)
                    for t in (2 * bb, 2 * bb + 1):
                        last = v.bn_aggr(mv[:, t, :], stats[:, t].rearrange("p a b -> p (a b)"))
                    last.then_inc(ln_moments, 1)
                    dve.wait_ge(ln_moments, own(ln_moments, it))
                    ts(rstd[:, 2 * bb:2 * bb + 2], mv[:, 2 * bb:2 * bb + 2, 1], EPS, None, ALU.add).then_inc(var_ready, 1)

                def normalised(n, bb, halves, dst):
                    dve.wait_ge(rstd_ready, due(rstd_ready, it, NB * (n - 1) + bb))
                    for t in (2 * bb, 2 * bb + 1):
                        for i, part in enumerate(halves(t)):
                            w = D // len(halves(t))
                            last = ts(dst[:, t, i * w:(i + 1) * w], part, mv[:, t, 0:1], rstd[:, t:t + 1], ALU.subtract, ALU.mult)
                        last.then_inc(tok_ready, 1)

                def norm_to_features(n, fn, prepare, halves, dst, whole=None, l=None):
                    prepare(0)
                    moments(n, 0, halves)
                    normalised(n, 0, whole or halves, dst)
                    features(fn, 0, l)
                    prepare(1)
                    moments(n, 1, halves)
                    normalised(n, 1, whole or halves, dst)
                    features(fn, 1, l)

                def halves_of(src):
                    return lambda t: (src[:, t, 0:P], src[:, t, P:D])

                def whole_of(src):
                    return lambda t: (src[:, t, :],)

                def features(n, bb, l=None):
                    dve.wait_ge(full_of(("fT", n, 1, bb)), full_at(("fT", n, 1, bb), it))
                    src = bank_of(("fT", n, 1, bb))[:, 0:T]
                    if l is None:
                        ins = v.tensor_copy(F[:, 1, bb, 1:T + 1], src)
                    else:
                        ins = ts(F[:, 1, bb, 1:T + 1], src, W[f"g{l}"][:, 1:2], W[f"b{l}"][:, 1:2], ALU.mult, ALU.add)
                    ins.then_inc(feat_v, 1)

                def head_outputs(dst, src, heads, width, lo=0):
                    v.reciprocal(rz[:, lo:lo + heads], src[:, :, width]).then_inc(rz_ready, 1)
                    dve.wait_ge(rz_ready, own(rz_ready, it))
                    return tt(dst, src[:, :, 0:width], wide(rz[:, lo:lo + heads], [P, heads, width], 2), ALU.mult)

                def softmax_input(u, b, groups, width, mask, ready):
                    e = E[:, u % ER, 0:groups * width].rearrange("p (g n) -> p g n", g=groups)
                    m = mx[:, u % ER, 0:groups]
                    tt(e, b[:, 0:groups * width].rearrange("p (g n) -> p g n", g=groups), mask, ALU.add).then_inc(sm_masked, 1)
                    dve.wait_ge(sm_masked, own(sm_masked, it))
                    v.tensor_reduce(m, e, AX_X, ALU.max, negate=True).then_inc(ready, 1)

                dve.wait_ge(full_of(("k1",)), full_at(("k1",), it))
                b = bank_of(("k1",))
                for m in range(KD):
                    for bb in range(NB):
                        last = stt(KT1[:, m, bb], wide(b[:, m * 256 + bb * C:m * 256 + (bb + 1) * C], [P, HK, C], 1), W["L0_xattn_bk"][:, m:m + 1],
                                   wide(W["head_rows"][:], [P, HK, C], 2), ALU.add, ALU.mult)
                last.then_inc(kv1_ready, 1)
                features(0, 0)
                features(0, 1)
                dve.wait_ge(v1_zero, due(v1_zero, it, 0))
                for bb in range(NB):
                    dve.wait_ge(full_of(("v1", bb)), full_at(("v1", bb), it))
                    b = bank_of(("v1", bb))
                    for m in range(KD):
                        lo = (bb * KD + m) * HK * P
                        own_cols = V1[0:C, lo:lo + HK * (P + HD)].rearrange("p (h d) -> p h d", h=HK)[:, :, 0:HD]
                        last = tt(own_cols, b[0:C, m * P:(m + 1) * P].rearrange("p (h d) -> p h d", h=HK),
                                  W["L0_xattn_bv"][0:C, m * P:(m + 1) * P].rearrange("p (h d) -> p h d", h=HK), ALU.add)
                    last.then_inc(kv1_ready, 1)
                def add_cross(bb):
                    for t in (2 * bb, 2 * bb + 1):
                        dve.wait_ge(xb_ready, due(xb_ready, it, t))
                        dve.wait_ge(full_of(("o1", t)), full_at(("o1", t), it))
                        b = bank_of(("o1", t))
                        tt(x[:, t, :], x[:, t, :], b[:, 0:D], ALU.add).then_inc(x1_ready, 1)
                    dve.wait_ge(x1_ready, due(x1_ready, it, 2 * bb + 1))
                    if bb == 0:
                        dve.wait_ge(x_out, due(x_out, it, 0))

                for u in range(len(CROSS) + 2):
                    if u < len(CROSS):
                        dve.wait_ge(full_of(("s1", u)), full_at(("s1", u), it))
                        b = bank_of(("s1", u))
                        softmax_input(u, b, 4, C, wide(negm[:, CROSS[u][0] % 2, :], [P, 4, C], 1), e1_ready)
                    if 1 <= u <= len(CROSS):
                        dve.wait_ge(p1_ready, due(p1_ready, it, u - 1))
                        v.reciprocal(rsums[:, (u - 1) % ER, :], sums[:, (u - 1) % ER, :]).then_inc(rs1_ready, 1)
                    if u >= 3 and u % 2 == 1:
                        w = u - 2
                        dve.wait_ge(full_of(("t1", w)), full_at(("t1", w), it))
                        v.tensor_copy(PT[0:C, w % PR, :], bank_of(("t1", w))[0:C, :]).then_inc(pt1_odd, 1)
                    if u == MID1 + 2:
                        features(1, 0)
                    if u == MID1 + 6:
                        add_cross(0)
                        moments(1, 0, halves_of(x))
                    if u == MID1 + 8:
                        normalised(1, 0, whole_of(x), y)
                features(1, 1)
                features(2, 0)
                add_cross(1)
                moments(1, 1, halves_of(x))
                normalised(1, 1, whole_of(x), y)
                for l in L:
                    def local_softmax(u):
                        t, g = LOCAL[u]
                        dve.wait_ge(full_of(("s2", l, u)), full_at(("s2", l, u), it))
                        b = bank_of(("s2", l, u))
                        if t % 2 == 0:
                            softmax_input(u, b, 4, P, wide(W["causal"][:, 1, :], [P, 4, P], 1), e2_ready)
                        else:
                            softmax_input(u, b, 2, 2 * P, wide(W["causal"][:].rearrange("p a n -> p (a n)"), [P, 2, 2 * P], 1), e2_ready)

                    base = l * 2 * NT
                    for r in range(-2, 2 * NT):
                        if r + 2 < 2 * NT:
                            t, i = divmod(r + 2, 2)
                            dve.wait_ge(sq_ready, due(sq_ready, it, base + r + 2))
                            v.tensor_reduce(ss[:, i, :], sq[:, i, :].rearrange("p (h d) -> p h d", h=H2), AX_X, ALU.add).then_inc(ss_sum, 1)
                            dve.wait_ge(ss_sum, own(ss_sum, it))
                            ts(ss[:, i, :], ss[:, i, :], 1e-24, None, ALU.max).then_inc(ss_ready, 1)
                        if 0 <= r + 1 < 2 * NT:
                            t, i = divmod(r + 1, 2)
                            b = bank_of((("q2", "k2")[i], l, t))
                            dve.wait_ge(full_of((("q2", "k2")[i], l, t)), full_at((("q2", "k2")[i], l, t), it))
                            dve.wait_ge(nrm_ready, due(nrm_ready, it, base + r + 1))
                            v.reciprocal(rr[:, i, :], rr[:, i, :]).then_inc(rr_ready, 1)
                            dve.wait_ge(rr_ready, own(rr_ready, it))
                            q4 = qn[:, i, :].rearrange("p (h d) -> p h d", h=H2)
                            if r + 1 >= 2:
                                dve.wait_ge(qb_ready, due(qb_ready, it, base + r - 1))
                            tt(q4, b[:, :].rearrange("p (h d) -> p h d", h=H2), wide(rr[:, i, :], [P, H2, HD2], 2), ALU.mult).then_inc(qn_ready, 1)
                            dve.wait_ge(qn_ready, own(qn_ready, it))
                            if t >= 2:
                                dve.wait_ge(full_of((("qT", "kT")[i], l, t - 2)), full_at((("qT", "kT")[i], l, t - 2), it))
                            q3 = qa[:, (r + 1) % 4, :].rearrange("p (h d) -> p h d", h=H2)
                            tt(q3, q4, wide(rotl[:, l, t % 2, 2 * i, :], [P, H2, HD2], 1), ALU.mult).then_inc(qa_ready, 1)
                        if r >= 0 and r % 2 == 0:
                            dve.wait_ge(qb_ready, due(qb_ready, it, base + r))
                            dve.wait_ge(qa_ready, due(qa_ready, it, base + r))
                            tt(qa[:, r % 4, :], qa[:, r % 4, :], qb[:, r % 2, :], ALU.add).then_inc(qr_ready, 1)
                        if r == -1:
                            features(2 + 2 * l, 1)
                        if r >= 2 * NT - 3:
                            local_softmax(r - (2 * NT - 3))

                    n = 3 + 2 * l

                    def add_local(bb):
                        for t in (2 * bb, 2 * bb + 1):
                            dve.wait_ge(full_of(("wo", l, t)), full_at(("wo", l, t), it))
                            b = bank_of(("wo", l, t))
                            tt(y[:, t, :], y[:, t, :], b[:, 0:D], ALU.add).then_inc(y_ready, 1)
                        dve.wait_ge(y_ready, due(y_ready, it, l * NT + 2 * bb + 1))

                    def shifted(t):
                        return y[:, t, 0:P], bank_of(("sh", l, t // 2))[:, (t % 2) * P:(t % 2 + 1) * P]

                    for u in range(3, len(LOCAL) + 2):
                        if u < len(LOCAL):
                            local_softmax(u)
                        if u >= 2 and LOCAL[u - 2][1] == len(local_groups(LOCAL[u - 2][0])) - 1:
                            t = LOCAL[u - 2][0]
                            for hf in range(2):
                                dve.wait_ge(full_of(("z2", l, t, hf)), full_at(("z2", l, t, hf), it))
                                b = bank_of(("z2", l, t, hf))
                                z = b[:, 0:4 * (HD2 + 1)].rearrange("p (h d) -> p h d", h=4)
                                last = head_outputs(O2[:, t, hf * 256:(hf + 1) * 256].rearrange("p (h d) -> p h d", h=4), z, 4, HD2, 4 * hf)
                            last.then_inc(o2_ready, 1)
                        if u == MID + 5:
                            add_local(0)
                        if u == MID + 6:
                            dve.wait_ge(full_of(("sh", l, 0)), full_at(("sh", l, 0), it))
                            moments(2 + l, 0, shifted)
                        if u == MID + 7:
                            normalised(2 + l, 0, shifted, xn)

                    features(n, 0, l)
                    add_local(1)
                    dve.wait_ge(full_of(("sh", l, 1)), full_at(("sh", l, 1), it))
                    moments(2 + l, 1, shifted)
                    normalised(2 + l, 1, shifted, xn)
                    features(n, 1, l)
                    v.memset(HH[32:64, HF, :], 1.0).then_inc(ones_row, 1)
                    dve.wait_ge(ones_row, own(ones_row, it))
                    for j in range(HF + 1):
                        dve.wait_ge(full_of(("a", l, j) if j < HF else ("r", l)), full_at(("a", l, j) if j < HF else ("r", l), it))
                        b = bank_of(("a", l, j) if j < HF else ("r", l))
                        r = P if j < HF else HR
                        dve.wait_ge(g_ready, due(g_ready, it, l * (HF + 1) + j))
                        stt(HH[0:r, j, :], b[0:r, :], W[f"b1{l}"][0:r, 2 * j + (j < HF):2 * j + (j < HF) + 1], G[0:r, j % 2, :],
                                  ALU.add, ALU.mult).then_inc(hh_ready, 1)

                    def add_ffn(bb):
                        for t in (2 * bb, 2 * bb + 1):
                            dve.wait_ge(full_of(("w2", l, t)), full_at(("w2", l, t), it))
                            b = bank_of(("w2", l, t))
                            tt(y[:, t, :], y[:, t, :], b[:, 0:D], ALU.add).then_inc(w2_read, 1)
                        dve.wait_ge(w2_read, due(w2_read, it, l * NT + 2 * bb + 1))

                    if l < DEPTH - 1:
                        for bb in range(NB):
                            add_ffn(bb)
                            for t in (2 * bb, 2 * bb + 1):
                                v.tensor_copy(spare_v[:, t:t + 1], y[0:1, t, 0:1]).then_inc(tok_ready, 1)
                        features(4 + 2 * l, 0)

                def add_transformer(bb):
                    add_ffn(bb)
                    tt(x[:, 2 * bb:2 * bb + 2, :], x[:, 2 * bb:2 * bb + 2, :], y[:, 2 * bb:2 * bb + 2, :], ALU.add).then_inc(x2_ready, 1)
                    dve.wait_ge(x2_ready, own(x2_ready, it))

                norm_to_features(4, 6, add_transformer, halves_of(x), xn, whole_of(x))
                for m in range(KD):
                    dve.wait_ge(full_of(("q3", m)), full_at(("q3", m), it))
                    b = bank_of(("q3", m))
                    ts(QT[:, m, :], b[:, :], HD ** -0.5, None, ALU.mult).then_inc(qk3_ready, 1)
                for m in range(KD):
                    dve.wait_ge(full_of(("k3", m)), full_at(("k3", m), it))
                    b = bank_of(("k3", m))
                    for par in range(PAR):
                        last = ts(KT3[:, m, par, :], b[:, :], parity[:, par:par + 1], None, ALU.mult)
                    last.then_inc(qk3_ready, 1)
                for edge in (0, T + 1):
                    v.memset(S0[:, :, :, edge:edge + 1], 0.0)
                v.memset(V3[:, :, :, HD:HD + 1], 1.0).then_inc(ones3_ready, 1)
                def add_conv(bb):
                    for t in (2 * bb, 2 * bb + 1):
                        dve.wait_ge(full_of(("p3", t)), full_at(("p3", t), it))
                        b = bank_of(("p3", t))
                        last = tt(x[:, t, :], x[:, t, :], b[:, 0:D], ALU.add)
                    last.then_inc(x3_ready, 1)
                    dve.wait_ge(x3_ready, own(x3_ready, it))

                for u in range(-2, len(CONV)):
                    if u + 2 < len(CONV):
                        bb, h = CONV[u + 2]
                        dve.wait_ge(full_of(("s3", u + 2)), full_at(("s3", u + 2), it))
                        b = bank_of(("s3", u + 2))
                        tt(S0[:, (u + 2) % SR, :, 1:T + 1], b[:, :].rearrange("p (j i) -> p j i", j=2), keepT[:], ALU.mult).then_inc(s0_ready, 1)
                    if 0 <= u + 1 < len(CONV):
                        dve.wait_ge(full_of(("c3", u + 1)), full_at(("c3", u + 1), it))
                        b = bank_of(("c3", u + 1))
                        softmax_input(u + 1, b, 2, T, far[:], e3_ready)
                    if u == 1:
                        tt(x[:], x[:], wide(W["L1_xattn_proj_b"][:], [P, NT, D], 1), ALU.add).then_inc(x3_bias, 1)
                        dve.wait_ge(x3_bias, own(x3_bias, it))
                    if u == H // 2:
                        first_moments(it + 1)
                    if u == H - 1:
                        first_normalised(it + 1)
                    if u == H + 3:
                        features(7, 0)
                    if u == H + 5:
                        add_conv(0)
                        moments(5, 0, halves_of(x))
                    if u == H + 9:
                        normalised(5, 0, whole_of(x), xn)
                    if u == H + 12:
                        features(8, 0)
                    if u >= 1 and (u - 1) % H == H - 1:
                        bb = (u - 1) // H
                        for i2 in range(2):
                            dve.wait_ge(full_of(("z3", bb, i2)), full_at(("z3", bb, i2), it))
                            b = bank_of(("z3", bb, i2))
                            z = b[:, 0:H * (HD + 1)].rearrange("p (h d) -> p h d", h=H)
                            head_outputs(xn[:, 2 * bb + i2, :].rearrange("p (h d) -> p h d", h=H), z, H, HD, H * i2).then_inc(tok_ready, 1)
                bb = NB - 1
                for i2 in range(2):
                    dve.wait_ge(full_of(("z3", bb, i2)), full_at(("z3", bb, i2), it))
                    b = bank_of(("z3", bb, i2))
                    z = b[:, 0:H * (HD + 1)].rearrange("p (h d) -> p h d", h=H)
                    head_outputs(xn[:, 2 * bb + i2, :].rearrange("p (h d) -> p h d", h=H), z, H, HD, H * i2).then_inc(tok_ready, 1)
                def mixed(bb):
                    for i, n in enumerate(("k", "r")):
                        dve.wait_ge(xr_part, due(xr_part, it, 2 * bb + i))
                        for k in range(KD):
                            dst = XR[:, i, k, bb * T:(bb + 1) * T]
                            last = stt(dst, F[:, k, bb, 1:T + 1], W[f"L1_ffn_mu_{n}"][:, k:k + 1], dst, ALU.mult, ALU.add)
                        last.then_inc(xr_ready, 1)

                features(7, 1)
                mixed(0)
                add_conv(1)
                moments(5, 1, halves_of(x))
                normalised(5, 1, whole_of(x), xn)
                features(8, 1)
                mixed(1)
                dve.wait_ge(full_of(("kk", 0)), full_at(("kk", 0), it))
                ts(KA[:, 0, :], bank_of(("kk", 0))[:, :], 0.0, None, ALU.max).then_inc(ka_part, 1)
                dve.wait_ge(ka_part, own(ka_part, it))
                tt(KA[:, 0, :], KA[:, 0, :], KA[:, 0, :], ALU.mult).then_inc(ka_ready, 1)
                for t in range(NT):
                    dve.wait_ge(sg_ready, due(sg_ready, it, t))
                    g = sg[:, t % 2, :]
                    dve.wait_ge(full_of(("v4", t)), full_at(("v4", t), it))
                    b = bank_of(("v4", t))
                    tt(g, g, b[:, 0:D], ALU.mult).then_inc(sg_part, 1)
                    dve.wait_ge(sg_part, own(sg_part, it))
                    tt(xo[:, t, :], x[:, t, :], g, ALU.add).then_inc(xo_ready, 1)

        @block.gpsimd
        def _(pool):
            g = nc.gpsimd
            g.memset(half[:], -0.5)
            g.memset(F[:], 0.0)
            g.memset(V2[:], 1.0)
            g.memset(one[:], 1.0).then_inc(consts_set, 1)
            with pool.Fori(0, B // HN) as it:
                for j in range(HS):
                    pool.wait_ge(hist_var, due(hist_var, it, j))
                    g.tensor_tensor(hrstd[0:C, j, :], hrstd[0:C, j, :], half[0:C, 0:HB], ALU.pow).then_inc(hist_rstd, 1)
            it = 0
            pool.wait_ge(kg_var, due(kg_var, it, 0))
            g.tensor_tensor(rstd[0:B, 0:1], rstd[0:B, 0:1], half[0:B, 0:1], ALU.pow).then_inc(kg_rstd, 1)
            pool.wait_ge(weights_in, 16 * len(loads))
            pool.wait_ge(consts_set, 2)
            pool.wait_ge(kp_ready, due(kp_ready, 0, 0))
            g.memset(V1[0:C, :], 0.0).then_inc(v1_zero, 1)
            pool.wait_ge(x0_var, due(x0_var, 0, 0))
            g.tensor_tensor(rstd[:], rstd[:], half[:, 0:NT], ALU.pow).then_inc(x0_rstd, 1)
            with pool.Fori(0, ITERS) as it:

                def scale(n, bb):
                    pool.wait_ge(var_ready, due(var_ready, it, NB * (n - 1) + bb))
                    r = rstd[:, 2 * bb:2 * bb + 2]
                    g.tensor_tensor(r, r, half[:, 0:2], ALU.pow).then_inc(rstd_ready, 1)

                pool.wait_ge(x_in, due(x_in, it, 0))
                pool.wait_ge(kv1_ready, due(kv1_ready, it, 0))
                for t in range(NT):
                    g.tensor_tensor(x[:, t, :], xin[:, t, :], W["L0_xattn_bo"][:], ALU.add).then_inc(xb_ready, 1)
                for u in range(len(CROSS)):
                    pool.wait_ge(rs1_ready, due(rs1_ready, it, u))
                    e = E[:, u % ER, 0:4 * C].rearrange("p (g n) -> p g n", g=4)
                    g.tensor_tensor(e, e, wide(rsums[:, u % ER, :], [P, 4, C], 2), ALU.mult).then_inc(pn1_ready, 1)
                    if u == MID1 + 5:
                        scale(1, 0)
                scale(1, 1)
                for l in L:
                    for r in range(2 * NT):
                        t, i = divmod(r, 2)
                        pool.wait_ge(qn_ready, due(qn_ready, it, l * 2 * NT + r))
                        if t >= 1 and i == 0:
                            pool.wait_ge(qr_ready, due(qr_ready, it, l * NT + t - 1))
                        elif t >= 1:
                            pool.wait_ge(kr_ready, due(kr_ready, it, l * NT + t - 1))
                        q4 = qn[:, i, :].rearrange("p (h d) -> p h d", h=H2)
                        b4 = qb[:, i, :].rearrange("p (h d) -> p h d", h=H2)
                        for lo, hi in ((0, HD2 // 2), (HD2 // 2, 0)):
                            last = g.tensor_tensor(b4[:, :, lo:lo + HD2 // 2], q4[:, :, hi:hi + HD2 // 2],
                                                   wide(rotl[:, l, t % 2, 2 * i + 1, lo:lo + HD2 // 2], [P, H2, HD2 // 2], 1), ALU.mult)
                        last.then_inc(qb_ready, 1)
                        if i == 1:
                            pool.wait_ge(qb_ready, due(qb_ready, it, l * 2 * NT + r))
                            pool.wait_ge(qa_ready, due(qa_ready, it, l * 2 * NT + r))
                            g.tensor_tensor(qa[:, r % 4, :], qa[:, r % 4, :], qb[:, i, :], ALU.add).then_inc(kr_ready, 1)
                    for bb in range(NB):
                        scale(2 + l, bb)
                for bb in range(NB):
                    scale(4, bb)
                pool.wait_ge(kern_in, due(kern_in, it, 0))
                for u, (bb, h) in enumerate(CONV):
                    taps = kern[:, bb, h * 9:(h + 1) * 9].rearrange("p (a c) -> p c a", a=3)
                    if u >= SR:
                        pool.wait_ge(full_of(("c3", u - SR)), full_at(("c3", u - SR), it))
                    dst = band[:, u % SR]
                    second, third = (diag_k[:, u % SR, c].rearrange("p (a n) -> p a n", a=3) for c in range(2))
                    for c, diagonal in enumerate((dst, second)):
                        last = g.tensor_tensor(diagonal, wide(diag[:, c, :], [P, 3, GW], 1), wide(taps[:, c, :], [P, 3, GW], 2), ALU.mult)
                    last.then_inc(band_part, 1)
                    pool.wait_ge(band_part, own(band_part, it))
                    g.tensor_tensor(dst, dst, second, ALU.add).then_inc(band_part, 1)
                    pool.wait_ge(band_part, own(band_part, it))
                    pool.wait_ge(third_ready, due(third_ready, it, u))
                    g.tensor_tensor(dst, dst, third, ALU.add).then_inc(band_ready, 1)
                    if u == H + 8:
                        scale(5, 0)
                    if u == H // 2 + 3:
                        pool.wait_ge(x0_var, due(x0_var, it + 1, 0))
                        g.tensor_tensor(rstd[:], rstd[:], half[:, 0:NT], ALU.pow).then_inc(x0_rstd, 1)
                scale(5, 1)
                pool.wait_ge(full_of(("r4", NT - 1)), full_at(("r4", NT - 1), it))
                g.tensor_tensor(pool_fence[:], half[0:1, 0:1], half[0:1, 0:1], ALU.mult)
                g.memset(V1[0:C, :], 0.0).then_inc(v1_zero, 1)

        @block.sync
        def _(sp):
            for dst, src in first_loads:
                sp.dma_start(dst[:], src).then_inc(first_in, 16)

            def load_context(step):
                for j in range(HN // NB):
                    sp.dma_start(hctx[j * NB // HB][:, :, j % (HB // NB)], a["ctxT"].rearrange("(s j) d n -> s j d n", j=HN // NB)[bass.ds(step, 1), j].rearrange(
                        "o (k p) n -> p (o k) n", p=P)).then_inc(hist_in, 16)

            load_context(0)
            for dst, src in loads:
                sp.dma_start(dst[:], src).then_inc(weights_in, 16)
            with sp.Fori(0, B // HN - 1) as it:
                sp.wait_ge(hist_h, due(hist_h, it, HS - 1))
                load_context(it + 1)
            it = 0
            sp.wait_ge(kp_ready, due(kp_ready, it, 0))
            sp.dma_start(kern_d, kp[:].rearrange("b h n -> b (h n)")).then_inc(kern_out, 16)
            sp.wait_ge(kern_out, 16)
            sp.dma_start(spare[:], a["L1_xattn_ctx_b2"]).then_inc(x_out, 16)

            def load_x(step):
                sp.dma_start(xin[:], a["x"][bass.ds(step, 1)].rearrange("o (t p) n -> p (o t) n", p=P)).then_inc(x_in, 16)

            def load_rest(step):
                sp.dma_start(ctxT[:], a["ctxT"][bass.ds(step, 1)].rearrange("o (k p) n -> p (o k) n", p=P)).then_inc(ctx_in, 16)
                sp.dma_start(kern[:], kern_d.rearrange("(s b) n -> s (b n)", b=NB)[bass.ds(step, 1)].rearrange(
                    "o n -> (o n)").partition_broadcast(P).rearrange("p (b n) -> p b n", b=NB)).then_inc(kern_in, 16)

            def store(it):
                sp.wait_ge(xo_ready, due(xo_ready, it, NT - 1))
                sp.dma_start(out[bass.ds(it, 1)].rearrange("o (t p) n -> p (o t) n", p=P), y[:]).then_inc(x_out, 16)

            load_x(0)
            load_rest(0)
            if ITERS > 1:
                with sp.Fori(0, ITERS - 1) as it:
                    sp.wait_ge(x0_ready, due(x0_ready, it, NT - 1))
                    sp.wait_ge(xb_ready, due(xb_ready, it, NT - 1))
                    load_x(it + 1)
                    sp.wait_ge(band_ready, due(band_ready, it, len(CONV) - 1))
                    load_rest(it + 1)
                    store(it)
            sp.wait_ge(x0_ready, due(x0_ready, ITERS - 1, NT - 1))
            sp.wait_ge(xb_ready, due(xb_ready, ITERS - 1, NT - 1))
            load_x(ITERS - 1)
            store(ITERS - 1)
            sp.wait_ge(x_out, 16 * (ITERS + 1))


def _constants():
    f = np.float32
    p = np.arange(P)
    ident = np.eye(P, dtype=f)
    shift = np.zeros((P, 2, P), f)
    shift[p[:-1], 0, p[:-1] + 1] = 1
    shift[P - 1, 1, 0] = 1
    diag = np.zeros((P, 3, GW), f)
    for c in range(3):
        diag[p, c, p + 2 - c] = 1
    causal = np.zeros((P, 2, P), f)
    causal[:, 0, :] = np.where(p[:, None] > p[None, :], FAR, 0)
    causal[:, 1, :] = np.where(p[:, None] < p[None, :], FAR, 0)
    parity = np.stack([(p // HD) % 2 == 0, (p // HD) % 2 == 1], 1).astype(f)
    head_rows = (p[:, None] // HD == np.arange(HK)[None, :]).astype(f)
    upper = np.stack([p < HD2, p >= HD2], 1).astype(f)
    half_idx = np.arange(0, HD2, 2, dtype=f)
    inv = (1.0 / 10000.0 ** (half_idx / HD2)).astype(f)
    t = np.arange(T, dtype=f)
    fr = t[:, None] * inv[None, :]
    fr = np.concatenate([fr, fr], -1)
    base = ((half_idx + 0.4 * HD2) / (1.4 * HD2)).astype(f)
    sc = base[None, :] ** ((t - T // 2) / f(64))[:, None]
    sc = np.concatenate([sc, sc], -1).astype(f)
    sign = np.where(np.arange(HD2) < HD2 // 2, -1, 1).astype(f)
    cos, sin = np.cos(fr), np.sin(fr) * sign
    rot = np.stack([cos * sc * 8, sin * sc * 8, cos / sc, sin / sc], 1).astype(f)
    rot = rot.reshape(2, P, 4, HD2).transpose(1, 0, 2, 3).copy()
    return {"ident": ident, "shift": shift, "diag": diag, "causal": causal, "parity": parity, "head_rows": head_rows, "upper": upper, "rot": rot}


def kernel(**inputs):
    import concourse.bacc as _bacc
    from concourse.bass_utils import run_bass_kernel_spmd as _run

    arrays = _constants()
    plain = {k: np.asarray(v) for k, v in inputs.items()}
    arrays["x"] = plain.pop("x").reshape(STEPS, NB * T, D)
    arrays["ctxT"] = plain.pop("ctx_1024").reshape(STEPS, NB * C, D).transpose(0, 2, 1)
    arrays["mask_1x1xSxS2_ik0"] = plain.pop("mask_1x1xSxS2_ik0").reshape(T, C)
    far = plain.pop("mask_SxS_bc0")
    arrays["far"], arrays["farT"] = (np.ascontiguousarray(m).view(np.int32) for m in (far, far.T))
    for name in ("L0_xattn_Wq", "L0_xattn_Wk", "L0_xattn_Wv", "L0_xattn_Wo", "L1_ffn_W_r", "L1_ffn_W_k", "L1_ffn_W_v"):
        arrays[name] = plain.pop(name).T
    w1, b1, w2, b2 = (plain.pop(f"L0_ffn_{n}") for n in ("w1", "b1", "w2", "b2"))
    w1p = np.zeros((DEPTH, D, (2 * HF + 1) * P), np.float32)
    b1p = np.zeros((DEPTH, (2 * HF + 1) * P), np.float32)
    for j in range(HF):
        w1p[:, :, 2 * j * P:(2 * j + 1) * P] = w1[:, :, HID + j * P:HID + (j + 1) * P]
        b1p[:, 2 * j * P:(2 * j + 1) * P] = b1[:, HID + j * P:HID + (j + 1) * P]
        w1p[:, :, (2 * j + 1) * P:(2 * j + 2) * P] = w1[:, :, j * P:(j + 1) * P]
        b1p[:, (2 * j + 1) * P:(2 * j + 2) * P] = b1[:, j * P:(j + 1) * P]
    lo = 2 * HF * P
    w1p[:, :, lo:lo + HR], w1p[:, :, lo + 64:lo + 64 + HR] = w1[:, :, HF * P:HID], w1[:, :, HID + HF * P:]
    b1p[:, lo:lo + HR], b1p[:, lo + 64:lo + 64 + HR] = b1[:, HF * P:HID], b1[:, HID + HF * P:]
    w2p = np.zeros((DEPTH, (HF + 1) * P, D), np.float32)
    w2p[:, :HID] = w2
    w2p[:, HID] = b2
    arrays |= {"w1p": w1p, "w2p": w2p}
    for name in ("L0_ffn_ln_g", "L0_ffn_ln_b", "L0_xattn_bq", "L0_xattn_bk", "L1_ffn_mu_r", "L1_ffn_mu_k", "L1_xattn_ctx_b1"):
        plain[name] = np.swapaxes(plain[name].reshape(*plain[name].shape[:-1], -1, P), -1, -2)
    arrays["b1p"] = np.swapaxes(b1p.reshape(DEPTH, -1, P), -1, -2)
    plain["L1_xattn_ctx_b2"] = plain["L1_xattn_ctx_b2"].reshape(1, 1)
    arrays |= plain
    arrays = {k: np.ascontiguousarray(v) for k, v in arrays.items()}

    nc = _bacc.Bacc("TRN2", target_bir_lowering=False, num_devices=1)
    aps = {n: nc.dram_tensor(f"in_{n}", v.shape, mybir.dt.from_np(v.dtype), kind="ExternalInput").ap() for n, v in arrays.items()}
    out = nc.dram_tensor("out_0", (STEPS, NB * T, D), F32, kind="ExternalOutput").ap()
    bass_cross_local_conv_mix_kernel(nc, aps, out)
    r = _run(nc, [{f"in_{k}": v for k, v in arrays.items()}], core_ids=[0])
    return r.results[0]["out_0"].reshape(B, T, D)
```
